# Optimizing a Trainium2 kernel written in Bass

```python
import numpy as np
import jax
import jax.numpy as jnp

def _softmax(x, axis=-1):
    return jax.nn.softmax(x, axis=axis)

def _gelu(x):
    return jax.nn.gelu(x, approximate=True)

def _silu(x):
    return jax.nn.silu(x)

def _sigmoid(x):
    return jax.nn.sigmoid(x)

def _layernorm(x, axis=-1, eps=1e-05):
    m = jnp.mean(x, axis=axis, keepdims=True)
    v = jnp.var(x, axis=axis, keepdims=True)
    return (x - m) / jnp.sqrt(v + eps)

def _scatter_add(tgt, idx, src, axis=0):
    return tgt.at[idx].add(src)

def _segment_sum(src, seg, n):
    return jax.ops.segment_sum(src, seg, n)
kernel_name = 'mk_gnn_resnorm_d4_gnn_r64_8f796e'

def setup_inputs(seed: int=0):
    np.random.seed(seed)
    _w = jnp.asarray

    def _rec_inputs():
        import jax
        import jax.numpy as jnp
        _gk = jax.random.key(seed)
        x = -0.0005121 + 1.001 * jax.random.normal(jax.random.fold_in(_gk, 1), (100000, 32), jnp.float32)
        src = jax.random.randint(jax.random.fold_in(_gk, 2), (25000,), 0, 100000, jnp.int32)
        dst = jax.random.randint(jax.random.fold_in(_gk, 3), (25000,), 0, 100000, jnp.int32)
        _o = jnp.argsort(dst, stable=True)
        src = src[_o]
        dst = dst[_o]
        edge_attr_3 = 0.000549083 + 1.00031 * jax.random.normal(jax.random.fold_in(_gk, 12), (25000, 3), jnp.float32)
        edge_attr_5 = -0.000325185 + 1.00005 * jax.random.normal(jax.random.fold_in(_gk, 13), (25000, 5), jnp.float32)
        edge_type_86 = jax.random.randint(jax.random.fold_in(_gk, 15), (25000,), 0, 86, jnp.int32)
        edge_weight = jax.random.uniform(jax.random.fold_in(_gk, 16), (25000,), jnp.float32, 0.0, 1)
        edge_weight1 = 0.000452788 + 0.999756 * jax.random.normal(jax.random.fold_in(_gk, 17), (25000, 1), jnp.float32)
        return (x, src, dst, edge_attr_3, edge_attr_5, edge_type_86, edge_weight, edge_weight1)
    x, src, dst, edge_attr_3, edge_attr_5, edge_type_86, edge_weight, edge_weight1 = _rec_inputs()

    def _L0_gnn_setup():
        import jax, jax.numpy as jnp
        import numpy as np
        N_NODES = 100000
        N_EDGES = 25000
        C_IN = 32
        C_OUT = 32
        BN_EPS = 1e-05
        IMPROVED = False

        def _gcn_conv(x, src, dst, ew, W, b):
            n = x.shape[0]
            fill = jnp.float32(2.0 if IMPROVED else 1.0)
            loop = jnp.arange(n, dtype=src.dtype)
            s = jnp.concatenate([src, loop])
            d = jnp.concatenate([dst, loop])
            w = jnp.concatenate([ew, jnp.full((n,), fill, dtype=ew.dtype)])
            deg = jax.ops.segment_sum(w, d, num_segments=n)
            dinv = jnp.where(deg > 0, jax.lax.rsqrt(deg), 0.0)
            norm = dinv[s] * w * dinv[d]
            xw = x @ W
            msg = xw[s] * norm[:, None]
            out = jax.ops.segment_sum(msg, d, num_segments=n)
            return out + b

        def _batchnorm(x, gamma, beta):
            mean = jnp.mean(x, axis=0)
            var = jnp.mean(jnp.square(x - mean), axis=0)
            return (x - mean) * jax.lax.rsqrt(var + BN_EPS) * gamma + beta
        key = jax.random.key(seed)
        ks = jax.random.split(key, 6)
        x = jax.random.normal(ks[0], (N_NODES, C_IN), dtype=jnp.float32)
        src = jax.random.randint(ks[1], (N_EDGES,), 0, N_NODES, dtype=jnp.int32)
        dst = jax.random.randint(ks[2], (N_EDGES,), 0, N_NODES, dtype=jnp.int32)
        edge_weight = jax.random.uniform(ks[3], (N_EDGES,), dtype=jnp.float32)
        W = jax.random.normal(ks[4], (C_IN, C_OUT), dtype=jnp.float32) * (1.0 / np.sqrt(C_IN))
        b = jnp.zeros((C_OUT,), dtype=jnp.float32)
        gamma = jnp.ones((C_OUT,), dtype=jnp.float32)
        beta = jnp.zeros((C_OUT,), dtype=jnp.float32)
        return {'x': x, 'src': src, 'dst': dst, 'edge_weight': edge_weight, 'W': W, 'b': b, 'gamma': gamma, 'beta': beta}
    _L0_gnn_all = _L0_gnn_setup()
    _L0_gnn_in = {k: v for k, v in _L0_gnn_all.items() if k in ('W', 'b', 'gamma', 'beta')}
    del _L0_gnn_all

    def _L1_gnn_setup():
        import jax, jax.numpy as jnp
        import numpy as np
        N_NODES = 50000
        N_EDGES = 12500
        INP_DIM = 32
        OUT_DIM = 32
        ATTN_DIM = 32
        NUM_RELS = 86
        NUM_BASES = 16
        GAMMA = 0.0
        key = jax.random.key(seed)
        ks = jax.random.split(key, 12)
        return {'h': jax.random.normal(ks[0], (N_NODES, INP_DIM), jnp.float32), 'weight': jax.random.normal(ks[1], (NUM_BASES, INP_DIM, OUT_DIM), jnp.float32), 'w_comp': jax.random.normal(ks[2], (NUM_RELS, NUM_BASES), jnp.float32), 'self_loop_weight': jax.random.normal(ks[3], (INP_DIM, OUT_DIM), jnp.float32), 'A1_w': jax.random.normal(ks[4], (ATTN_DIM, INP_DIM), jnp.float32), 'A1_b': jax.random.normal(ks[5], (ATTN_DIM,), jnp.float32), 'A2_w': jax.random.normal(ks[6], (ATTN_DIM, INP_DIM), jnp.float32), 'A2_b': jax.random.normal(ks[7], (ATTN_DIM,), jnp.float32), 'rel_emb': jax.random.normal(ks[8], (NUM_RELS, ATTN_DIM), jnp.float32), 'src': jax.random.randint(ks[9], (N_EDGES,), 0, N_NODES, jnp.int32), 'dst': jax.random.randint(ks[10], (N_EDGES,), 0, N_NODES, jnp.int32), 'etype': jax.random.randint(ks[11], (N_EDGES,), 0, NUM_RELS, jnp.int32)}
    _L1_gnn_all = _L1_gnn_setup()
    _L1_gnn_in = {k: v for k, v in _L1_gnn_all.items() if k in ('weight', 'w_comp', 'self_loop_weight', 'A1_w', 'A1_b', 'A2_w', 'A2_b', 'rel_emb')}
    del _L1_gnn_all

    def _L2_gnn_setup():
        import jax, jax.numpy as jnp
        import numpy as np
        NUM_LAYERS = 3
        ALPHA = 0.9
        N_NODES = 100000
        N_CLASSES = 32
        N_EDGES = 50000

        def _gcn_norm(edge_index, edge_weight, num_nodes):
            row, col = (edge_index[0], edge_index[1])
            deg = jax.ops.segment_sum(edge_weight, col, num_segments=num_nodes)
            deg_inv_sqrt = jnp.where(deg > 0, jax.lax.rsqrt(jnp.maximum(deg, 1e-38)), 0.0)
            return deg_inv_sqrt[row] * edge_weight * deg_inv_sqrt[col]
        key = jax.random.key(seed)
        k1, k2, k3 = jax.random.split(key, 3)
        y = jax.random.uniform(k1, (N_NODES, N_CLASSES), dtype=jnp.float32)
        edge_index = jax.random.randint(k2, (2, N_EDGES), 0, N_NODES, dtype=jnp.int64)
        edge_weight = jax.random.uniform(k3, (N_EDGES,), dtype=jnp.float32)
        return {'y': y, 'edge_index': edge_index, 'edge_weight': edge_weight}
    _L2_gnn_all = _L2_gnn_setup()
    _L2_gnn_in = {k: v for k, v in _L2_gnn_all.items() if k in ()}
    del _L2_gnn_all

    def _L3_gnn_setup():
        import jax, jax.numpy as jnp
        import numpy as np
        import math
        M = 8
        COMBOS = [(0, 0, 0), (0, 1, 1), (1, 0, 1), (1, 1, 0), (1, 1, 1), (2, 1, 1)]

        def _cg_coeff(j1, m1, j2, m2, j3, m3):
            if m3 != m1 + m2:
                return 0.0
            f = math.factorial
            vmin = max(0, j2 - j3 - m1, j1 + m2 - j3)
            vmax = min(j1 + j2 - j3, j1 - m1, j2 + m2)
            pref = (2 * j3 + 1) * f(j3 + j1 - j2) * f(j3 - j1 + j2) * f(j1 + j2 - j3) / f(j1 + j2 + j3 + 1)
            pref *= f(j3 + m3) * f(j3 - m3) * f(j1 - m1) * f(j1 + m1) * f(j2 - m2) * f(j2 + m2)
            s = 0.0
            for v in range(vmin, vmax + 1):
                s += (-1) ** v / (f(v) * f(j1 + j2 - j3 - v) * f(j1 - m1 - v) * f(j2 + m2 - v) * f(j3 - j2 + m1 + v) * f(j3 - j1 - m2 + v))
            return math.sqrt(pref) * s

        def _su2_cg(l1, l2, l3):
            C = np.zeros((2 * l1 + 1, 2 * l2 + 1, 2 * l3 + 1), dtype=np.complex128)
            for m1 in range(-l1, l1 + 1):
                for m2 in range(-l2, l2 + 1):
                    m3 = m1 + m2
                    if -l3 <= m3 <= l3:
                        C[m1 + l1, m2 + l2, m3 + l3] = _cg_coeff(l1, m1, l2, m2, l3, m3)
            return C

        def _qmat(l):
            q = np.zeros((2 * l + 1, 2 * l + 1), dtype=np.complex128)
            for m in range(-l, 0):
                q[l + m, l + abs(m)] = 1 / np.sqrt(2)
                q[l + m, l - abs(m)] = -1j / np.sqrt(2)
            q[l, l] = 1.0
            for m in range(1, l + 1):
                q[l + m, l + abs(m)] = (-1) ** m / np.sqrt(2)
                q[l + m, l - abs(m)] = 1j * (-1) ** m / np.sqrt(2)
            return (-1j) ** l * q

        def _so3_cg(l1, l2, l3):
            C = np.einsum('ij,kl,mn,ikn->jlm', _qmat(l1), _qmat(l2), np.conj(_qmat(l3)).T, _su2_cg(l1, l2, l3))
            assert np.abs(C.imag).max() < 1e-06
            C = C.real
            return C / np.linalg.norm(C)
        CG = {c: jnp.asarray(_so3_cg(*c), dtype=jnp.float32) for c in COMBOS}
        N, E = (100000, 25000)
        ks = jax.random.split(jax.random.key(seed), 6)
        return {'node_irreps': jax.random.normal(ks[0], (N, 4 * M), jnp.float32), 'edge_index': jax.random.randint(ks[1], (2, E), 0, N, dtype=jnp.int32), 'sh0': jax.random.normal(ks[2], (E, 1), jnp.float32), 'sh1': jax.random.normal(ks[3], (E, 3), jnp.float32), 'sh2': jax.random.normal(ks[4], (E, 5), jnp.float32), 'W': jax.random.normal(ks[5], (len(COMBOS), M, M), jnp.float32)}
    _L3_gnn_all = _L3_gnn_setup()
    _L3_gnn_in = {k: v for k, v in _L3_gnn_all.items() if k in ('W',)}
    del _L3_gnn_all
    return {'x': x, 'src': src, 'dst': dst, 'edge_attr_3': edge_attr_3, 'edge_attr_5': edge_attr_5, 'edge_type_86': edge_type_86, 'edge_weight': edge_weight, 'edge_weight1': edge_weight1, 'L0_gnn_W': _L0_gnn_in['W'], 'L0_gnn_b': _L0_gnn_in['b'], 'L0_gnn_gamma': _L0_gnn_in['gamma'], 'L0_gnn_beta': _L0_gnn_in['beta'], 'L1_gnn_weight': _L1_gnn_in['weight'], 'L1_gnn_w_comp': _L1_gnn_in['w_comp'], 'L1_gnn_self_loop_weight': _L1_gnn_in['self_loop_weight'], 'L1_gnn_A1_w': _L1_gnn_in['A1_w'], 'L1_gnn_A1_b': _L1_gnn_in['A1_b'], 'L1_gnn_A2_w': _L1_gnn_in['A2_w'], 'L1_gnn_A2_b': _L1_gnn_in['A2_b'], 'L1_gnn_rel_emb': _L1_gnn_in['rel_emb'], 'L3_gnn_W': _L3_gnn_in['W']}

def reference(x, src, dst, edge_attr_3, edge_attr_5, edge_type_86, edge_weight, edge_weight1, L0_gnn_W, L0_gnn_b, L0_gnn_gamma, L0_gnn_beta, L1_gnn_weight, L1_gnn_w_comp, L1_gnn_self_loop_weight, L1_gnn_A1_w, L1_gnn_A1_b, L1_gnn_A2_w, L1_gnn_A2_b, L1_gnn_rel_emb, L3_gnn_W):
    import jax
    import jax.numpy as jnp

    def _L0_gnn_ref(x, src, dst, edge_weight, W, b, gamma, beta):
        import jax, jax.numpy as jnp
        import numpy as np
        N_NODES = 100000
        N_EDGES = 25000
        C_IN = 32
        C_OUT = 32
        BN_EPS = 1e-05
        IMPROVED = False

        def _gcn_conv(x, src, dst, ew, W, b):
            n = x.shape[0]
            fill = jnp.float32(2.0 if IMPROVED else 1.0)
            loop = jnp.arange(n, dtype=src.dtype)
            s = jnp.concatenate([src, loop])
            d = jnp.concatenate([dst, loop])
            w = jnp.concatenate([ew, jnp.full((n,), fill, dtype=ew.dtype)])
            deg = jax.ops.segment_sum(w, d, num_segments=n)
            dinv = jnp.where(deg > 0, jax.lax.rsqrt(deg), 0.0)
            norm = dinv[s] * w * dinv[d]
            xw = x @ W
            msg = xw[s] * norm[:, None]
            out = jax.ops.segment_sum(msg, d, num_segments=n)
            return out + b

        def _batchnorm(x, gamma, beta):
            mean = jnp.mean(x, axis=0)
            var = jnp.mean(jnp.square(x - mean), axis=0)
            return (x - mean) * jax.lax.rsqrt(var + BN_EPS) * gamma + beta
        h = _gcn_conv(x, src, dst, edge_weight, W, b)
        h = _batchnorm(h, gamma, beta)
        return jax.nn.relu(h)

    def _L1_gnn_ref(h, weight, w_comp, self_loop_weight, A1_w, A1_b, A2_w, A2_b, rel_emb, src, dst, etype):
        import jax, jax.numpy as jnp
        import numpy as np
        N_NODES = 50000
        N_EDGES = 12500
        INP_DIM = 32
        OUT_DIM = 32
        ATTN_DIM = 32
        NUM_RELS = 86
        NUM_BASES = 16
        GAMMA = 0.0
        E = src.shape[0]
        N = h.shape[0]
        x = h[src]
        y = h[dst]
        c = w_comp[etype]
        xb = jnp.einsum('ei,bio->ebo', x, weight)
        msg = jnp.einsum('eb,ebo->eo', c, xb)
        x_hat = x @ A1_w.T + A1_b
        y_hat = y @ A2_w.T + A2_b + rel_emb[etype]
        scale = jnp.sqrt(jnp.asarray(INP_DIM, h.dtype))
        a = jnp.tanh(jax.nn.relu(jnp.sum(x_hat * y_hat, axis=-1) / scale))
        a = jnp.where(a > GAMMA, a, jnp.zeros_like(a))
        nei = jax.ops.segment_sum(a[:, None] * msg, dst, num_segments=N)
        last_e = jax.ops.segment_max(jnp.arange(E, dtype=jnp.int32), dst, num_segments=N)
        last_e = jnp.clip(last_e, 0, E - 1)
        curr = h[src[last_e]] @ self_loop_weight
        in_deg = jax.ops.segment_sum(jnp.ones((E,), h.dtype), dst, num_segments=N)
        h_new = jnp.where((in_deg > 0)[:, None], nei + curr, jnp.zeros_like(nei))
        return jax.nn.relu(h_new)

    def _L2_gnn_ref(y, edge_index, edge_weight):
        import jax, jax.numpy as jnp
        import numpy as np
        NUM_LAYERS = 3
        ALPHA = 0.9
        N_NODES = 100000
        N_CLASSES = 32
        N_EDGES = 50000

        def _gcn_norm(edge_index, edge_weight, num_nodes):
            row, col = (edge_index[0], edge_index[1])
            deg = jax.ops.segment_sum(edge_weight, col, num_segments=num_nodes)
            deg_inv_sqrt = jnp.where(deg > 0, jax.lax.rsqrt(jnp.maximum(deg, 1e-38)), 0.0)
            return deg_inv_sqrt[row] * edge_weight * deg_inv_sqrt[col]
        num_nodes = y.shape[0]
        row, col = (edge_index[0], edge_index[1])
        norm = _gcn_norm(edge_index, edge_weight, num_nodes)
        res = (1.0 - ALPHA) * y
        out = y
        for _ in range(NUM_LAYERS):
            msg = norm[:, None] * out[row]
            agg = jax.ops.segment_sum(msg, col, num_segments=num_nodes)
            out = jnp.clip(agg * ALPHA + res, 0.0, 1.0)
        return out

    def _L3_gnn_ref(node_irreps, edge_index, sh0, sh1, sh2, W):
        import jax, jax.numpy as jnp
        import numpy as np
        import math
        M = 8
        COMBOS = [(0, 0, 0), (0, 1, 1), (1, 0, 1), (1, 1, 0), (1, 1, 1), (2, 1, 1)]

        def _cg_coeff(j1, m1, j2, m2, j3, m3):
            if m3 != m1 + m2:
                return 0.0
            f = math.factorial
            vmin = max(0, j2 - j3 - m1, j1 + m2 - j3)
            vmax = min(j1 + j2 - j3, j1 - m1, j2 + m2)
            pref = (2 * j3 + 1) * f(j3 + j1 - j2) * f(j3 - j1 + j2) * f(j1 + j2 - j3) / f(j1 + j2 + j3 + 1)
            pref *= f(j3 + m3) * f(j3 - m3) * f(j1 - m1) * f(j1 + m1) * f(j2 - m2) * f(j2 + m2)
            s = 0.0
            for v in range(vmin, vmax + 1):
                s += (-1) ** v / (f(v) * f(j1 + j2 - j3 - v) * f(j1 - m1 - v) * f(j2 + m2 - v) * f(j3 - j2 + m1 + v) * f(j3 - j1 - m2 + v))
            return math.sqrt(pref) * s

        def _su2_cg(l1, l2, l3):
            C = np.zeros((2 * l1 + 1, 2 * l2 + 1, 2 * l3 + 1), dtype=np.complex128)
            for m1 in range(-l1, l1 + 1):
                for m2 in range(-l2, l2 + 1):
                    m3 = m1 + m2
                    if -l3 <= m3 <= l3:
                        C[m1 + l1, m2 + l2, m3 + l3] = _cg_coeff(l1, m1, l2, m2, l3, m3)
            return C

        def _qmat(l):
            q = np.zeros((2 * l + 1, 2 * l + 1), dtype=np.complex128)
            for m in range(-l, 0):
                q[l + m, l + abs(m)] = 1 / np.sqrt(2)
                q[l + m, l - abs(m)] = -1j / np.sqrt(2)
            q[l, l] = 1.0
            for m in range(1, l + 1):
                q[l + m, l + abs(m)] = (-1) ** m / np.sqrt(2)
                q[l + m, l - abs(m)] = 1j * (-1) ** m / np.sqrt(2)
            return (-1j) ** l * q

        def _so3_cg(l1, l2, l3):
            C = np.einsum('ij,kl,mn,ikn->jlm', _qmat(l1), _qmat(l2), np.conj(_qmat(l3)).T, _su2_cg(l1, l2, l3))
            assert np.abs(C.imag).max() < 1e-06
            C = C.real
            return C / np.linalg.norm(C)
        CG = {c: jnp.asarray(_so3_cg(*c), dtype=jnp.float32) for c in COMBOS}
        N, E = (node_irreps.shape[0], edge_index.shape[1])
        src = node_irreps[edge_index[0]]
        feats = {0: src[:, :M][:, :, None], 1: src[:, M:].reshape(E, M, 3)}
        sh = {0: sh0, 1: sh1, 2: sh2}
        msg = {0: jnp.zeros((E, M, 1), node_irreps.dtype), 1: jnp.zeros((E, M, 3), node_irreps.dtype)}
        for idx, (le, ln, lo) in enumerate(COMBOS):
            base = jnp.einsum('ijk,ei,emj->emk', CG[le, ln, lo], sh[le], feats[ln])
            msg[lo] = msg[lo] + jnp.einsum('io,eik->eok', W[idx], base)
        tgt = edge_index[1]
        agg0 = jax.ops.segment_sum(msg[0].reshape(E, M), tgt, num_segments=N)
        agg1 = jax.ops.segment_sum(msg[1].reshape(E, 3 * M), tgt, num_segments=N)
        return jnp.concatenate([agg0, agg1], axis=1)
    edge_index = jnp.stack([src, dst])
    x = _layernorm(x + _L0_gnn_ref(x, src, dst, edge_weight, L0_gnn_W, L0_gnn_b, L0_gnn_gamma, L0_gnn_beta), axis=-1)
    x = _layernorm(x + _L1_gnn_ref(x, L1_gnn_weight, L1_gnn_w_comp, L1_gnn_self_loop_weight, L1_gnn_A1_w, L1_gnn_A1_b, L1_gnn_A2_w, L1_gnn_A2_b, L1_gnn_rel_emb, src, dst, edge_type_86), axis=-1)
    x = _layernorm(x + _L2_gnn_ref(x, edge_index, edge_weight), axis=-1)
    x = _layernorm(x + _L3_gnn_ref(x, edge_index, edge_weight1, edge_attr_3, edge_attr_5, L3_gnn_W), axis=-1)
    return x

_drawn_inputs = setup_inputs


def setup_inputs(seed=0):
    import zlib

    import numpy as np

    out = dict(_drawn_inputs(seed))
    spreads = {'L0_gnn_b': (0.0, 0.1), 'L0_gnn_gamma': (1.0, 0.2), 'L0_gnn_beta': (0.0, 0.1)}
    factors = {}
    for name, (base, spread) in spreads.items():
        noise = np.random.default_rng([zlib.crc32(name.encode()), seed]).standard_normal(out[name].shape)
        drawn = base * np.exp(spread * noise) if base else spread * noise
        out[name] = jnp.asarray(drawn.astype(out[name].dtype))
    for name, factor in factors.items():
        out[name] = (out[name] * factor).astype(out[name].dtype)
    return out
```

```python
from contextlib import ExitStack

import concourse.bass as bass
from concourse import mybir

N, E, D = 100000, 25000, 32
BLOCKS, TILES = 4, 7
BLOCK = TILES * 32
CHUNK = BLOCKS * BLOCK
CHUNKS = -(-E // CHUNK)
RING = 4
ROUNDS = CHUNKS // RING
ROWS = CHUNKS * BLOCKS
FULL = E // BLOCK
TAIL = E - FULL * BLOCK
FAR = 2 * N
NOWHERE = 1 << 22
AUG = 36
BASES, RELS = 16, 86
SH = 9
PLANES = 6 + SH
STATK = 25
STATS = N // (128 * STATK)
LEFT = (N - STATS * 128 * STATK) // STATK
DK = 32
DSTEPS = 4 * ROUNDS
DSTRIDE = (N - 128 * DK) // (DSTEPS - 1)
assert (N - 128 * DK) % (DSTEPS - 1) == 0 and CHUNKS == RING * ROUNDS and LEFT * STATK == N - STATS * 128 * STATK
EPS = 1e-5
ALPHA = 0.9
TINY = 1.2e-38
GATHER = 16 * TILES
CUR, Q1, Q2, CO, QW = 0, 32, 64, 96, 112


def at(n):
    return slice(n, n + 1) if isinstance(n, int) else bass.ds(n, 1)


def whole(t):
    return t[tuple([slice(None)] * len(t.shape))]


def build(nc, x, src, dst, attr3, attr5, etype, ew, ew1, bgb_in, w_gcn, w2, w4, wq, relc, wcat, cg, wt,
          ident, own_in, own_blocks, relno_in, aug, plane, mask, tab_b, tab_r, tab_o1, tab_o2, tab_o3, out):
    fp32, bf16, i32 = mybir.dt.float32, mybir.dt.bfloat16, mybir.dt.int32
    ALU, ACT, AX = mybir.AluOpType, mybir.ActivationFunctionType, mybir.AxisListType
    ctx = ExitStack()
    with ctx:
        def sb(name, shape, dt=fp32):
            return ctx.enter_context(nc.sbuf_tensor(name, shape, dt))

        def sem(name):
            return ctx.enter_context(nc.semaphore(name))

        Z = sb("Z", [128, CHUNKS, TILES, 2 * D])
        P = sb("P", [128, CHUNKS, TILES, D])
        slot = sb("slot", [128, RING, TILES, 2 * D])
        idx = sb("idx", [128, RING, TILES], i32)
        oslot = sb("oslot", [128, RING, TILES, D])
        oidx = sb("oidx", [128, RING, TILES], i32)
        cont = sb("cont", [128, CHUNKS, BLOCK], bf16)
        pref = sb("pref", [128, CHUNKS, BLOCK], bf16)
        through = sb("through", [32, ROWS], bf16)
        scal = sb("scal", [128, PLANES, TILES, 32])
        srcs, dsts, degree, ends, weight, home = (scal[:, k] for k in range(6))
        dinv = sb("dinv", [128, TILES, 32])
        dis = sb("dis", [128, TILES, 32])
        endinv = sb("endinv", [128, TILES, 32])
        minus = sb("minus", [128, TILES, 32])
        norm2 = sb("norm2", [128, TILES, 32])
        ta = sb("ta", [128, 2, TILES, 32])
        tb = sb("tb", [128, 2, TILES, 32])
        tm = sb("tm", [128, 2, TILES, 32])
        own = sb("own", [128, TILES, 32])
        i_src = sb("i_src", [128, TILES, 32], i32)
        i_dst = sb("i_dst", [128, TILES, 32], i32)
        i_aug = sb("i_aug", [128, TILES, 32], i32)
        i_out = sb("i_out", [128, TILES, 32], i32)
        i_ptr = sb("i_ptr", [128, TILES, 32], i32)
        i_home = sb("i_home", [128, TILES, 32], i32)
        idx2 = sb("idx2", [128, RING, TILES], i32)
        trow = sb("trow", [128, CHUNKS, TILES, 4])
        tslot = sb("tslot", [128, RING, TILES, 4])
        planes = Z[:, :, :, :].rearrange("p c t f -> p (c t f)")
        natural = planes[:, 0:PLANES * BLOCK].rearrange("p (k e) -> p k e", e=BLOCK)
        bp = planes[0:ROWS, PLANES * BLOCK:2 * PLANES * BLOCK].rearrange("p (k e) -> p k e", e=BLOCK)
        wide = sb("wide", [128, 6 * DK * D])
        dx, dy, dc, dq, do_, dxt = (wide[:, k * DK * D:(k + 1) * DK * D] for k in range(6))
        cgs = wide[0:D, 0:6 * D * SH].rearrange("p (k f n) -> p k f n", k=6, f=D)
        bs2 = wide[0:D, 6 * D * SH:7 * D * SH].rearrange("p (f n) -> p f n", n=SH)
        by_rows = wide[0:ROWS, 7 * D * SH:]
        raw3, raw5 = by_rows[:, 0:3 * BLOCK], by_rows[:, 3 * BLOCK:8 * BLOCK]
        bcont, bpref, bsum, bzero = (by_rows[:, k * BLOCK:(k + 1) * BLOCK] for k in range(8, 12))
        bdst, bprev, bnext, bsrc = (by_rows[:, k * BLOCK:(k + 1) * BLOCK].bitcast(i32) for k in range(12, 16))
        bmask = by_rows[:, 16 * BLOCK:17 * BLOCK].bitcast(bf16).rearrange("p (k e) -> p k e", k=2)
        bown = by_rows[:, 17 * BLOCK:18 * BLOCK]
        bgo, bback, blast = (raw3[:, k * BLOCK:(k + 1) * BLOCK] for k in range(3))
        gl = wide[:, 0:2 * TILES * D].rearrange("p (q t f) -> p q t f", q=2, t=TILES)
        gr = wide[:, 512:512 + 2 * TILES * (D + 1)].rearrange("p (q t f) -> p q t f", q=2, t=TILES)
        oh = wide[0:RELS, 0:CHUNK]
        prod = wide[:, 1024:1024 + 2 * D * BASES].rearrange("p (q n) -> p q n", q=2)
        wide2 = sb("wide2", [128, 4 * CHUNK])
        stx = wide2[:, 0:2 * STATK * D].rearrange("p (q k f) -> p q k f", q=2, f=D)
        sta = wide2[:, 2 * STATK * D:2 * STATK * (D + AUG)].rearrange("p (q k f) -> p q k f", q=2, f=AUG)
        fx = wide2[0:65, 0:2 * CHUNK].rearrange("p (q e) -> p q e", q=2)
        pz = wide2[:, 2 * CHUNK:2 * CHUNK + TILES * 2 * D].rearrange("p (t f) -> p t f", f=2 * D)
        cur = wide2[:, 2 * CHUNK + TILES * 2 * D:3 * CHUNK].rearrange("p (q t f) -> p q t f", q=2, f=D)
        types = wide2[0:RELS, 3 * CHUNK:4 * CHUNK].bitcast(i32)
        brow = sb("brow", [1, 6, ROWS + 1])
        bcarry = sb("bcarry", [ROWS, 2])
        msg, msg2, agg = (sb(n, [128, TILES, D]) for n in ("msg", "msg2", "agg"))
        fm, fs, fo = (sb(n, [128, BLOCK]) for n in ("fm", "fs", "fo"))
        blk = sb("blk", [32, BLOCKS])
        run = sb("run", [32, BLOCKS + 1])
        carry = sb("carry", [128, 1])
        y, yc, yq = (sb(n, [128, 2 * TILES, D]) for n in ("y", "yc", "yq"))
        ysum, yvar, ystd, yr = (sb(n, [128, 2 * TILES]) for n in ("ysum", "yvar", "ystd", "yr"))
        sw = sb("sw", [128, TILES])
        ob = sb("ob", [128, 2, TILES, D])
        ca = sb("ca", [128, TILES, BASES])
        att = sb("att", [128, 3, TILES])
        eps = sb("eps", [128, 2])
        dsum, dvar, dstd, dr = (sb(n, [128, DK]) for n in ("dsum", "dvar", "dstd", "dr"))
        idn = sb("idn", [128, 128])
        zer = sb("zer", [128, D + 1])
        ones = sb("ones", [128, 128])
        gram = sb("gram", [32, D + 1])
        wg, vv = sb("wg", [32, D]), sb("vv", [32, D])
        srep = sb("srep", [32, 128])
        bgb = sb("bgb", [128, 3, D])
        st = sb("st", [128, 8, D])
        w2s = sb("w2s", [65, 2 * D])
        w4s = sb("w4s", [128, 128])
        t16 = sb("t16", [1, 16, D])
        wqs = sb("wqs", [65, QW])
        relcs = sb("relcs", [RELS, D + BASES])
        wcs = sb("wcs", [32, D * BASES])
        relno = sb("relno", [RELS, 1])
        wts = sb("wts", [32, 6, D])
        bs = sb("bs", [32, D, SH])
        bank = [ctx.enter_context(nc.psum_tensor(f"bank{i}", [128, 512], fp32)) for i in range(8)]
        G = bank[7][0:32, 0:D + 1]

        (cleared, blocks_in, consts_in, planes_set, planes_out, planes_in, masks_in, ends_scanned, ends_turned,
         ends_summed, carry_out, roots_in, roots_out, indices_set, own_used, stx_free, sta_set, sta_free) = (sem(n) for n in (
             "cleared blocks_in consts_in planes_set planes_out planes_in masks_in ends_scanned ends_turned "
             "ends_summed carry_out roots_in roots_out indices_set own_used stx_free sta_set sta_free").split())
        stx_in = [sem(f"stx_in{q}") for q in range(2)]
        aug_out = [sem(f"aug_out{q}") for q in range(2)]
        (gram_done, gram_read, mean_done, vv_set, square_done, spread_in, spread_out, bn_set, table3_set) = (sem(n) for n in (
            "gram_done gram_read mean_done vv_set square_done spread_in spread_out bn_set table3_set").split())
        def each(what, passes):
            return {n: sem(f"{what}_{n}") for n in passes.split()}

        staged = each("staged", "D T A R O1 O2 O3 H")
        used = each("used", "A O1 O2 O3")
        stored = each("stored", "B R O1 O2 O3")
        turned = each("turned", "B R H")
        fx_set = each("fx_set", "B R H")
        var_set = each("var_set", "B R O3 H")
        std_set = each("std_set", "B R O3 H")
        gathered = {n: [sem(f"gathered_{n}{j}") for j in range(RING)] for n in "D T A R O1 O2 O3 H".split()}
        scattered = [sem(f"scattered{j}") for j in range(RING)]
        tabled = {n: [sem(f"tabled_{n}{j}") for j in range(2)] for n in "B R O1 O2 O3".split()}
        (copied_a, gram_set, gram_used, pz_set, bn_out, bn_used, types_in, types_read, q_set, q_used, cur_set, dot_set, tanh_set,
         xb_set_r, xb_used_r, xb_set_h, xb_used_h, rows_set) = (sem(n) for n in (
             "copied_a gram_set gram_used pz_set bn_out bn_used types_in types_read q_set q_used cur_set dot_set tanh_set "
             "xb_set_r xb_used_r xb_set_h xb_used_h rows_set").split())
        pool_passed, pe_passed = sem("pool_passed"), sem("pe_passed")
        (d_in, d_turned, d_xt, d_prod, d_y, d_c1, d_q1, d_v1, d_s1, d_x2, d_relu, d_c2, d_q2, d_v2, d_s2, d_set, d_out) = (
            sem(f"dense_{n}") for n in "in turned xt prod y c1 q1 v1 s1 x2 relu c2 q2 v2 s2 set out".split())
        block = ctx.enter_context(nc.Block())

        def rounds(eng, body):
            body(0)
            with eng.Fori(1, ROUNDS - 1) as r:
                body(r)
            body(ROUNDS - 1)

        def hold(eng, semaphore, value, passed=None):
            if isinstance(value, int):
                if value > 0:
                    eng.wait_ge(semaphore, value)
            else:
                eng.wait_ge(semaphore, value)
                if passed is not None:
                    eng.sem_inc(passed, 1)

        def last(c):
            return isinstance(c, int) and c >= CHUNKS

        def col(t, c):
            return t[:, :, at(c)].rearrange("p t c -> p (t c)")

        def chunk(t, c, a=0, z=None):
            return t[:, at(c), :, a:z].rearrange("p c t f -> p (c t) f")

        def over(v, n=D):
            return v.unsqueeze(2).broadcast_to([v.shape[0], v.shape[1], n])

        @block.sync
        def _(sp):
            for t, a in ((idn, ident), (own, own_in), (bown, own_blocks), (relno, relno_in), (wg, w_gcn), (w2s, w2), (w4s, w4), (wqs, wq),
                         (relcs, relc), (wcs, wcat), (cgs, cg), (wts, wt), (bgb, bgb_in.unsqueeze(0).broadcast_to([128, 3, D]))):
                sp.dma_start(whole(t), a).then_inc(consts_in, 16)
            sp.wait_ge(cleared, 1)
            sp.dma_start(bprev[0:1, 1:BLOCK], dst[0:BLOCK - 1].unsqueeze(0)).then_inc(blocks_in, 16)
            for t, a, lo, off, w in ((bdst, dst, 0, 0, 1), (bprev, dst, 1, -1, 1), (bnext, dst, 0, 1, 1), (bsrc, src, 0, 0, 1),
                                     (bp[:, 4], ew, 0, 0, 1), (bp[:, 6], ew1, 0, 0, 1), (raw3, attr3, 0, 0, 3), (raw5, attr5, 0, 0, 5)):
                k = BLOCK * w
                sp.dma_start(t[lo:FULL, :], a[lo * k + off:FULL * k + off].rearrange("(p k) -> p k", k=k)).then_inc(blocks_in, 16)
                sp.dma_start(t[FULL:FULL + 1, 0:TAIL * w - off], a[FULL * k + off:E * w].unsqueeze(0)).then_inc(blocks_in, 16)
            sp.wait_ge(planes_set, 1)
            sp.dma_start(plane.rearrange("k (p e) -> p k e", e=BLOCK), bp).then_inc(planes_out, 16)
            sp.dma_start(mask.rearrange("k (p e) -> p k e", e=BLOCK), bmask[:, :, :]).then_inc(planes_out, 16)
            sp.wait_ge(planes_out, 32)
            by_block = plane.rearrange("k (c b e) -> b c k e", b=BLOCKS, e=BLOCK)
            masks = mask.rearrange("k (c b e) -> k b c e", b=BLOCKS, e=BLOCK)
            for q in range(BLOCKS):
                sp.dma_start(natural[32 * q:32 * q + CHUNKS], by_block[q]).then_inc(planes_in, 16)
            for k, t in enumerate((cont, pref)):
                for q in range(BLOCKS):
                    sp.dma_start(t[32 * q:32 * q + 32], masks[k, q].unsqueeze(0).broadcast_to([32, CHUNKS, BLOCK])).then_inc(masks_in, 16)
            ends_row = mask.rearrange("k (p e) -> k e p", e=BLOCK)[1, BLOCK - 1]
            with nc.allow_non_contiguous_dma("one column of the blocks"):
                sp.dma_start(through[:, :], ends_row.unsqueeze(0).broadcast_to([32, ROWS])).then_inc(masks_in, 16)

            def load_stat(q, n0, parts):
                rows = x[n0:n0 + parts * STATK] if isinstance(n0, int) else x[bass.ds(n0, parts * STATK)]
                sp.dma_start(stx[0:parts, q], rows.rearrange("(p k) f -> p k f", k=STATK)).then_inc(stx_in[q], 16)

            def store_stat(q, n0, parts):
                rows = aug[n0:n0 + parts * STATK] if isinstance(n0, int) else aug[bass.ds(n0, parts * STATK)]
                sp.dma_start(rows.rearrange("(p k) f -> p k f", k=STATK), sta[0:parts, q]).then_inc(aug_out[q], 16)

            step = 128 * STATK
            load_stat(0, 0, 128)
            load_stat(1, step, 128)
            with sp.Fori(0, (STATS - 3) // 2) as r:
                for q in range(2):
                    k = 2 * r + q
                    hold(sp, sta_set, k + 1)
                    store_stat(q, k * step, 128)
                    load_stat(q, (k + 2) * step, 128)
            for k in range(STATS - 3, STATS + 1):
                sp.wait_ge(sta_set, k + 1)
                store_stat(k % 2, k * step, 128 if k < STATS else LEFT)
                if k + 2 <= STATS:
                    load_stat(k % 2, (k + 2) * step, 128 if k + 2 < STATS else LEFT)

            def store_table(name, table, c, j, rows):
                hold(sp, stored[name], c + 1)
                view = table.rearrange("(c p t) f -> c p t f", p=128, t=TILES)[at(c)]
                sp.dma_start(view.rearrange("c p t f -> (c p) t f"), rows).then_inc(tabled[name][j % 2], 16)

            def dense_rows(t, k):
                n = 128 * DK
                v = t[k * DSTRIDE:k * DSTRIDE + n] if isinstance(k, int) else t[bass.ds(k * DSTRIDE, n)]
                return v.rearrange("(p k) f -> p (k f)", k=DK)

            def dense_store(k):
                hold(sp, d_set, k + 1)
                sp.dma_start(dense_rows(out, k), do_).then_inc(d_out, 16)

            def dense_load(k):
                hold(sp, d_y, k)
                sp.dma_start(dx, dense_rows(x, k)).then_inc(d_in, 16)

            def b_round(r):
                for j in range(RING):
                    c = RING * r + j
                    store_table("B", tab_b, c, j, chunk(Z, c, D))
            rounds(sp, b_round)

            def load_types(c):
                n = min(CHUNK, E - c * CHUNK) if isinstance(c, int) else CHUNK
                row = etype[c * CHUNK:c * CHUNK + n] if isinstance(c, int) else etype[bass.ds(c * CHUNK, n)]
                hold(sp, types_read, c)
                sp.dma_start(types[:, 0:n], row.unsqueeze(0).broadcast_to([RELS, n])).then_inc(types_in, 16)

            def r_round(r):
                for j in range(RING):
                    c = RING * r + j
                    if not last(c + 1):
                        load_types(c + 1)
                    store_table("R", tab_r, c, j, chunk(Z, c, D))
            load_types(0)
            rounds(sp, r_round)

            dense_load(0)
            for name, table, first in (("O1", tab_o1, 0), ("O2", tab_o2, 2 * ROUNDS)):
                def o_round(r, name=name, table=table, first=first):
                    for j in range(RING):
                        store_table(name, table, RING * r + j, j, ob[:, j % 2])
                        if j % 2:
                            k = first + 2 * r + j // 2
                            dense_store(k)
                            if not (isinstance(k, int) and k == DSTEPS - 1):
                                dense_load(k + 1)
                rounds(sp, o_round)

            def o3_round(r):
                for j in range(RING):
                    c = RING * r + j
                    store_table("O3", tab_o3, c, j, chunk(Z, c, D))
            rounds(sp, o3_round)
            sp.wait_ge(d_out, 16 * DSTEPS)

        @block.gpsimd
        def _(pool):
            def gather(name, table, rows, c, j, width=D):
                hold(pool, staged[name], c + 1, pool_passed)
                for t in range(TILES):
                    nc.gpsimd.indirect_dma_start(
                        slot[:, j, t, 0:width], None, table, bass.IndirectOffsetOnAxis(ap=idx[:, j, t:t + 1], axis=0),
                        bounds_check=rows - 1, oob_is_err=False).then_inc(gathered[name][j], 16)
                if name == "R":
                    for t in range(TILES):
                        nc.gpsimd.indirect_dma_start(
                            slot[:, j, t, D:2 * D], None, table, bass.IndirectOffsetOnAxis(ap=idx2[:, j, t:t + 1], axis=0),
                            bounds_check=rows - 1, oob_is_err=False).then_inc(gathered[name][j], 16)

            def gathers(name, table, rows, width=D):
                def body(r):
                    for j in range(RING):
                        gather(name, table, rows, RING * r + j, j, width)
                rounds(pool, body)

            gathers("D", x, N)
            for q in range(2):
                pool.wait_ge(aug_out[q], 16 * ((STATS + 2 - q) // 2))
            quads = aug.rearrange("n (a f) -> (n a) f", f=4)

            def t_round(r):
                for j in range(RING):
                    hold(pool, staged["T"], RING * r + j + 1, pool_passed)
                    for t in range(TILES):
                        nc.gpsimd.indirect_dma_start(
                            quads, bass.IndirectOffsetOnAxis(ap=idx[:, j, t:t + 1], axis=0), tslot[:, j, t, :], None,
                            bounds_check=N * AUG // 4 - 1, oob_is_err=False).then_inc(gathered["T"][j], 16)
            rounds(pool, t_round)
            for j in range(RING):
                pool.wait_ge(gathered["T"][j], GATHER * ROUNDS)
            gathers("A", aug, N, AUG)
            for name, prev, table in (("R", "B", tab_b), ("O1", "R", tab_r), ("O2", "O1", tab_o1), ("O3", "O2", tab_o2)):
                for q in range(2):
                    pool.wait_ge(tabled[prev][q], 16 * CHUNKS // 2)
                gathers(name, table, ROWS * BLOCK)
            for q in range(2):
                pool.wait_ge(tabled["O3"][q], 16 * CHUNKS // 2)
            pool.wait_ge(d_out, 16 * DSTEPS)

            def scatter(c, j):
                hold(pool, rows_set, c + 1, pool_passed)
                for t in range(TILES):
                    nc.gpsimd.indirect_dma_start(
                        out, bass.IndirectOffsetOnAxis(ap=oidx[:, j, t:t + 1], axis=0), oslot[:, j, t, :], None,
                        bounds_check=N - 1, oob_is_err=False).then_inc(scattered[j], 16)

            def h_round(r):
                for j in range(RING):
                    c = RING * r + j
                    gather("H", tab_o3, ROWS * BLOCK, c, j)
                    if not (isinstance(c, int) and c < 2):
                        scatter(c - 2, (j - 2) % RING)
            rounds(pool, h_round)
            for c in (CHUNKS - 2, CHUNKS - 1):
                scatter(c, c % RING)
            for j in range(RING):
                pool.wait_ge(scattered[j], GATHER * ROUNDS)

        @block.scalar
        def _(act):
            def copy(o, i):
                return nc.scalar.activation(o, i, ACT.Copy)

            act.wait_ge(cleared, 1)
            act.wait_ge(roots_in, 1)
            nc.scalar.activation(tb[:, :, :, :], ta[:, :, :, :], ACT.Sqrt).then_inc(roots_out, 1)

            def stat(k, r, q, parts):
                hold(act, stx_in[q], 16 * (r + 1))
                hold(act, sta_free, k - 1)
                hold(act, aug_out[q], 16 * r)
                copy(sta[0:parts, q, :, 0:D], stx[0:parts, q]).then_inc(sta_set, 1)
            for k in range(2):
                stat(k, 0, k, 128)
            with act.Fori(1, STATS // 2) as r:
                for q in range(2):
                    stat(2 * r + q, r, q, 128)
            for k in range(STATS - 1, STATS + 1):
                stat(k, k // 2, k % 2, 128 if k < STATS else LEFT)

            def stage(name, c, j, rows, index):
                if rows is not None:
                    copy(slot[:, j, :, 0:D], chunk(rows, c, 0, D))
                copy(idx[:, j, :], col(index, c)).then_inc(staged[name], 1)

            for j in range(RING):
                act.wait_ge(gathered["T"][j], GATHER * ROUNDS)
            for c in range(RING - 1):
                stage("A", c, c, None, i_src)

            def a_round(r):
                for j in range(RING):
                    c = RING * r + j
                    hold(act, gathered["A"][j], GATHER * (r + 1))
                    copy(chunk(Z, c, 0, D), slot[:, j, :, 0:D]).then_inc(copied_a, 1)
                    if not last(c + RING - 1):
                        hold(act, used["A"], c)
                        stage("A", c + RING - 1, (j - 1) % RING, None, i_src)
            rounds(act, a_round)

            act.wait_ge(spread_in, 1)
            nc.scalar.activation(st[:, 4], st[:, 3], ACT.Sqrt, bias=eps[:, 0:1]).then_inc(spread_out, 1)

            def root(name, c, n=2 * TILES):
                hold(act, var_set[name], c + 1)
                nc.scalar.activation(ystd[:, 0:n], yvar[:, 0:n], ACT.Sqrt, bias=eps[:, 0:1], scale=1.0 / D).then_inc(std_set[name], 1)

            def evacuate(name, c, j, k):
                hold(act, turned[name], c + 1)
                copy(fx[0:k, j % 2, 0:512], bank[0][0:k, :])
                copy(fx[0:k, j % 2, 512:CHUNK], bank[1][0:k, 0:CHUNK - 512]).then_inc(fx_set[name], 1)

            act.wait_ge(bn_set, 1)

            def fetch_b(c, j):
                hold(act, turned["B"], c)
                copy(pz[:, :, 0:D], chunk(Z, c, 0, D))
                copy(pz[:, :, D:], chunk(P, c, 0, D)).then_inc(pz_set, 1)
                hold(act, bn_out, c - 1)
                evacuate("B", c, j, 2 * D)
            fetch_b(0, 0)

            def b_round(r):
                for j in range(RING):
                    c = RING * r + j
                    if not last(c + 1):
                        fetch_b(c + 1, j + 1)
                    root("B", c)
            rounds(act, b_round)

            act.wait_ge(stored["B"], CHUNKS)

            def stage_r(c, j):
                copy(idx2[:, j, :], col(i_home, c))
                stage("R", c, j, Z, i_ptr)
            for c in range(RING):
                stage_r(c, c)

            def q_view(b, n, lo, width):
                return b[:, 0:n * QW].rearrange("p (t w) -> p t w", w=QW)[:, :, lo:lo + width]

            def fetch_r(c, j):
                hold(act, xb_set_r, TILES * (c - 1))
                evacuate("R", c, j, 2 * D)
                hold(act, q_set, c + 1)
                hold(act, stored["R"], c - 1)
                copy(cur[:, j % 2, 0:4], q_view(bank[2], 4, CUR, D))
                copy(cur[:, j % 2, 4:TILES], q_view(bank[3], 3, CUR, D)).then_inc(cur_set, 1)
                hold(act, dot_set, c + 1)
                nc.scalar.activation(att[:, 1], att[:, 0], ACT.Tanh).then_inc(tanh_set, 1)
            fetch_r(0, 0)

            def r_round(r):
                for j in range(RING):
                    c = RING * r + j
                    if not last(c + 1):
                        fetch_r(c + 1, j + 1)
                    if not last(c + RING):
                        hold(act, turned["R"], c + 1)
                        stage_r(c + RING, j)
                    root("R", c)
            rounds(act, r_round)

            def dense(k):
                hold(act, d_turned, k + 1)
                hold(act, d_prod, k)
                copy(dxt[:, 0:512], bank[0][:, :])
                copy(dxt[:, 512:1024], bank[1][:, :]).then_inc(d_xt, 1)
                hold(act, d_c1, k + 1)
                nc.scalar.activation(dq, dc, ACT.Square).then_inc(d_q1, 1)
                hold(act, d_v1, k + 1)
                nc.scalar.activation(dstd[:, :], dvar[:, :], ACT.Sqrt, bias=eps[:, 1:2], scale=(1.0 + EPS) / D).then_inc(d_s1, 1)
                hold(act, d_x2, k + 1)
                nc.scalar.activation(dq, dy, ACT.Relu, scale=1.0 - ALPHA).then_inc(d_relu, 1)
                hold(act, d_c2, k + 1)
                nc.scalar.activation(dy, dq, ACT.Square).then_inc(d_q2, 1)
                hold(act, d_v2, k + 1)
                nc.scalar.activation(dstd[:, :], dvar[:, :], ACT.Sqrt, bias=eps[:, 1:2], scale=(1.0 + EPS) / D).then_inc(d_s2, 1)

            for name, prev, rows in (("O1", "R", Z), ("O2", "O1", P), ("O3", "O2", P)):
                act.wait_ge(stored[prev], CHUNKS)
                for c in range(RING):
                    stage(name, c, c, rows, i_ptr)

                def o_round(r, name=name, rows=rows):
                    for j in range(RING):
                        c = RING * r + j
                        if not last(c + RING):
                            hold(act, used[name], c + 1)
                            stage(name, c + RING, j, rows, i_ptr)
                        if name == "O3":
                            root(name, c)
                        elif j % 2:
                            dense((0 if name == "O1" else 2 * ROUNDS) + 2 * r + j // 2)
                rounds(act, o_round)

            act.wait_ge(stored["O3"], CHUNKS)
            for c in range(RING):
                stage("H", c, c, Z, i_ptr)

            def fetch_h(c, j):
                hold(act, xb_set_h, TILES * (c - 1))
                evacuate("H", c, j, D)
            fetch_h(0, 0)

            def h_round(r):
                for j in range(RING):
                    c = RING * r + j
                    if not last(c + 1):
                        fetch_h(c + 1, j + 1)
                    if not last(c + RING):
                        hold(act, turned["H"], c + 1)
                        stage("H", c + RING, j, Z, i_ptr)
                    root("H", c, TILES)
            rounds(act, h_round)

        @block.vector
        def _(dve):
            v = nc.vector

            def settle():
                v.drain()

            for t, value in ((bdst, FAR), (bprev, FAR), (bnext, FAR), (bsrc, 0)):
                v.memset(t[:, :], value)
            for t, value in ((planes[:, 0:2 * PLANES * BLOCK], 0.0), (by_rows[:, 0:12 * BLOCK], 0.0), (brow, 0.0), (zer, 0.0), (ones, 1.0), (eps[:, 0:1], EPS),
                             (eps[:, 1:2], EPS * EPS), (slot, 0.0), (trow, 0.0), (sta, 0.0)):
                v.memset(whole(t), value)
            settle()
            v.memset(bprev[0:1, 0:1], -1)
            v.memset(sta[:, :, :, D:D + 1], 1.0)
            v.memset(sta[:, :, :, D + 2:D + 3], float(NOWHERE))
            settle()
            v.memset(run[:, 0:1], 0.0).then_inc(cleared, 1)

            dve.wait_ge(blocks_in, 16 * 17)
            v.tensor_tensor(bcont, bdst[:, :], bprev[:, :], ALU.is_equal)
            v.tensor_tensor(bp[:, 3], bdst[:, :], bnext[:, :], ALU.not_equal)
            v.tensor_copy(bp[:, 0], bsrc[:, :])
            v.tensor_copy(bp[:, 1], bdst[:, :])
            v.tensor_copy(bp[:, 7:10], raw3.rearrange("p (e k) -> p k e", k=3))
            v.tensor_copy(bp[:, 10:15], raw5.rearrange("p (e k) -> p k e", k=5))
            settle()
            v.tensor_tensor_scan(bsum, bcont, bp[:, 4], 0.0, ALU.mult, ALU.add)
            v.tensor_tensor_scan(bpref, bcont, bzero, 1.0, ALU.mult, ALU.add)
            settle()
            dve.wait_ge(consts_in, 16 * 13)
            v.tensor_tensor(bback, bp[:, 3], bown, ALU.mult)
            v.tensor_scalar(bgo, bp[:, 3], -1.0, 1.0, ALU.mult, ALU.add)
            settle()
            v.tensor_tensor_scan(bp[:, 5, ::-1], bgo[:, ::-1], bback[:, ::-1], 0.0, ALU.mult, ALU.add)
            v.tensor_tensor_scan(blast[:, ::-1], bgo[:, ::-1], bzero, 1.0, ALU.mult, ALU.add)
            settle()
            v.tensor_copy(bmask[:, 0], bcont)
            v.tensor_copy(bmask[:, 1], bpref).then_inc(ends_scanned, 1)
            dve.wait_ge(ends_turned, 1)
            v.tensor_copy(brow[0:1, 0, 0:ROWS], bank[6][0:1, 0:ROWS])
            v.tensor_copy(brow[0:1, 1, 0:ROWS], bank[6][0:1, 128:128 + ROWS])
            v.tensor_copy(brow[0:1, 3, 0:ROWS], bank[6][0:1, 256:256 + ROWS])
            v.tensor_copy(brow[0:1, 4, 0:ROWS], bank[6][0:1, 384:384 + ROWS])
            settle()
            v.tensor_tensor_scan(brow[0:1, 5, 0:ROWS][:, ::-1], brow[0:1, 4, 0:ROWS][:, ::-1], brow[0:1, 3, 0:ROWS][:, ::-1], 0.0,
                                 ALU.mult, ALU.add)
            v.tensor_tensor_scan(brow[0:1, 2, 1:ROWS + 1], brow[0:1, 1, 0:ROWS], brow[0:1, 0, 0:ROWS], 0.0,
                                 ALU.mult, ALU.add).then_inc(ends_summed, 1)
            dve.wait_ge(carry_out, 1)
            v.tensor_copy(bcarry[:, :], bank[6][0:ROWS, 256:258])
            settle()
            v.scalar_tensor_tensor(bp[:, 5], blast, bcarry[:, 1:2], bp[:, 5], ALU.mult, ALU.add)
            v.scalar_tensor_tensor(bp[:, 2], bpref, bcarry[:, 0:1], bsum, ALU.mult, ALU.add).then_inc(planes_set, 1)

            dve.wait_ge(planes_in, 16 * BLOCKS)
            v.transpose(scal[:, :, :, :].rearrange("p k t c -> p (k t c)"), planes[:, 0:PLANES * BLOCK])
            settle()
            v.tensor_scalar(tm[:, 0], degree, 1.0, None, ALU.add)
            v.tensor_scalar(tm[:, 1], degree, 0.0, None, ALU.is_gt)
            v.tensor_scalar(ta[:, 1], degree, TINY, None, ALU.max)
            v.tensor_copy(i_home[:, :, :], home)
            v.tensor_copy(trow[:, :, :, 2].rearrange("p c t -> p t c"), own[:, :, 0:CHUNKS])
            v.tensor_copy(i_src[:, :, :], srcs)
            v.tensor_copy(i_dst[:, :, :], dsts)
            v.tensor_scalar(minus[:, :, :], ends, -1.0, None, ALU.mult)
            v.tensor_scalar(tb[:, 0], dsts, float(-NOWHERE), None, ALU.add)
            v.tensor_scalar(tb[:, 1], dsts, float(AUG // 4), float(D // 4 - NOWHERE), ALU.mult, ALU.add)
            settle()
            v.tensor_scalar(ta[:, 0], tm[:, 0], TINY, None, ALU.max)
            v.tensor_tensor(tb[:, 0], tb[:, 0], ends, ALU.mult)
            v.tensor_tensor(tb[:, 1], tb[:, 1], ends, ALU.mult)
            settle()
            v.tensor_scalar(tm[:, 0], tm[:, 0], 0.0, None, ALU.is_gt)
            v.tensor_scalar(i_out[:, :, :], tb[:, 0], float(NOWHERE), None, ALU.add)
            v.tensor_scalar(i_aug[:, :, :], tb[:, 1], float(NOWHERE), None, ALU.add).then_inc(roots_in, 1)
            dve.wait_ge(roots_out, 1)
            v.reciprocal(tb[:, :, :, :].rearrange("p k t c -> p (k t c)"), tb[:, :, :, :].rearrange("p k t c -> p (k t c)"))
            settle()
            v.tensor_tensor(dinv[:, :, :], tb[:, 0], tm[:, 0], ALU.mult)
            v.tensor_tensor(dis[:, :, :], tb[:, 1], tm[:, 1], ALU.mult)
            settle()
            v.tensor_tensor(endinv[:, :, :], dinv[:, :, :], ends, ALU.mult)
            v.tensor_copy(trow[:, :, :, 0].rearrange("p c t -> p t c"), dinv[:, :, 0:CHUNKS])
            v.tensor_copy(trow[:, :, :, 1].rearrange("p c t -> p t c"), dis[:, :, 0:CHUNKS])
            settle()

            def stage_d(c, j):
                v.tensor_copy(idx[:, j, :], col(i_dst, c)).then_inc(staged["D"], 1)
            for c in range(RING - 1):
                stage_d(c, c)

            def d_round(r):
                for j in range(RING):
                    c = RING * r + j
                    hold(dve, gathered["D"][j], GATHER * (r + 1))
                    v.tensor_copy(chunk(Z, c, D), slot[:, j, :, 0:D])
                    settle()
                    if not last(c + RING - 1):
                        stage_d(c + RING - 1, (j - 1) % RING)
            rounds(dve, d_round)

            def stage_t(c, j):
                v.tensor_copy(tslot[:, j], trow[:, at(c)].rearrange("p c t f -> p (c t) f"))
                v.tensor_copy(idx[:, j, :], col(i_aug, c)).then_inc(staged["T"], 1)
            for c in range(RING - 1):
                stage_t(c, c)

            def t_round(r):
                for j in range(RING):
                    c = RING * r + j
                    if not last(c + RING - 1):
                        if not (isinstance(c, int) and c == 0):
                            hold(dve, gathered["T"][(j - 1) % RING], GATHER * (r + (j > 0)))
                        stage_t(c + RING - 1, (j - 1) % RING)
            rounds(dve, t_round)

            for k in range(6):
                w_ = over(wts[:, k], SH)
                v.tensor_tensor((bs if k == 0 else bs2)[:, :, :], cgs[:, k], w_, ALU.mult)
                settle()
                if k:
                    v.tensor_tensor(bs[:, :, :], bs[:, :, :], bs2[:, :, :], ALU.add)
                    settle()

            def flat(t):
                return t[:, :, :].rearrange("p t f -> p (t f)")

            def sum_runs(c):
                v.transpose(fm[:, :], flat(msg))
                settle()
                v.tensor_tensor_scan(fs[:, :], cont[:, at(c)].rearrange("p c e -> p (c e)"), fm[:, :], 0.0, ALU.mult, ALU.add)
                settle()
                for q in range(BLOCKS):
                    v.tensor_copy(blk[:, q:q + 1], fs[32 * q:32 * q + 32, BLOCK - 1:BLOCK])
                settle()
                ends_ = through[:, c * BLOCKS:(c + 1) * BLOCKS] if isinstance(c, int) else through[:, bass.ds(c * BLOCKS, BLOCKS)]
                v.tensor_tensor_scan(run[:, 1:BLOCKS + 1], ends_, blk[:, :], run[:, 0:1], ALU.mult, ALU.add)
                settle()
                for q in range(BLOCKS):
                    v.tensor_copy(carry[32 * q:32 * q + 32, :], run[:, q:q + 1])
                settle()
                v.tensor_copy(run[:, 0:1], run[:, BLOCKS:BLOCKS + 1])
                v.scalar_tensor_tensor(fo[:, :], pref[:, at(c)].rearrange("p c e -> p (c e)"), carry[:, 0:1], fs[:, :], ALU.mult, ALU.add)
                settle()
                v.transpose(flat(agg), fo[:, :])
                settle()

            v.memset(gr, 1.0)
            settle()
            dve.wait_ge(masks_in, 16 * (2 * BLOCKS + 1))

            def a_round(r):
                for j in range(RING):
                    c = RING * r + j
                    hold(dve, gathered["A"][j], GATHER * (r + 1))
                    s = slot[:, j]
                    v.tensor_tensor(sw[:, :], col(weight, c), s[:, :, D], ALU.mult)
                    v.tensor_tensor(col(norm2, c), col(weight, c), s[:, :, D + 1], ALU.mult)
                    v.tensor_copy(col(i_ptr, c), s[:, :, D + 2])
                    v.tensor_tensor(msg2[:, :, :], chunk(Z, c, D), over(col(endinv, c)), ALU.mult)
                    settle()
                    v.tensor_tensor(msg[:, :, :], s[:, :, 0:D], over(sw[:, :]), ALU.mult)
                    settle()
                    v.tensor_tensor(msg[:, :, :], msg[:, :, :], msg2[:, :, :], ALU.add).then_inc(used["A"], 1)
                    settle()
                    sum_runs(c)
                    v.tensor_tensor(msg2[:, :, :], agg[:, :, :], over(col(dinv, c)), ALU.mult)
                    settle()
                    v.tensor_copy(chunk(P, c), msg2[:, :, :])
                    hold(dve, gram_used, c)
                    v.tensor_copy(gr[:, 0, :, 0:D], msg2[:, :, :])
                    v.tensor_copy(gr[:, 1, :, 0:D], chunk(Z, c, D))
                    v.tensor_tensor(gl[:, 0], msg2[:, :, :], over(col(ends, c)), ALU.mult)
                    v.tensor_tensor(gl[:, 1], chunk(Z, c, D), over(col(minus, c)), ALU.mult).then_inc(gram_set, 1)
                    settle()
            rounds(dve, a_round)

            dve.wait_ge(gram_done, 1)
            v.tensor_copy(gram[:, :], G)
            v.tensor_copy(srep[:, :], G[:, D:D + 1].broadcast_to([32, 128])).then_inc(gram_read, 1)
            dve.wait_ge(mean_done, 1)
            v.tensor_scalar(st[:, 0], bank[6][:, 0:D], 1.0 / N, None, ALU.mult)
            v.tensor_tensor(vv[:, :], bank[6][0:32, 64:64 + D], wg[:, :], ALU.mult).then_inc(vv_set, 1)
            dve.wait_ge(square_done, 1)
            v.tensor_scalar(st[:, 1], bank[6][:, 128:128 + D], 1.0 / N, None, ALU.mult)
            settle()
            v.tensor_tensor(st[:, 2], st[:, 0], st[:, 0], ALU.mult)
            v.tensor_tensor(st[:, 6], st[:, 0], bgb[:, 0], ALU.add)
            settle()
            v.tensor_tensor(st[:, 3], st[:, 1], st[:, 2], ALU.subtract)
            v.tensor_tensor(st[:, 6], bgb[:, 0], st[:, 6], ALU.subtract)
            settle()
            v.tensor_scalar(st[:, 3], st[:, 3], 0.0, None, ALU.max)
            settle()
            v.drain().then_inc(spread_in, 1)
            dve.wait_ge(spread_out, 1)
            v.reciprocal(st[:, 5], st[:, 4])
            settle()
            v.tensor_tensor(st[:, 5], st[:, 5], bgb[:, 1], ALU.mult)
            settle()
            v.tensor_tensor(st[:, 6], st[:, 6], st[:, 5], ALU.mult)
            settle()
            v.tensor_tensor(st[:, 7], st[:, 6], bgb[:, 2], ALU.add)

            def tiled(row, n):
                return row.unsqueeze(1).broadcast_to([row.shape[0], n, D])
            settle()
            v.tensor_tensor(w2s[0:64, :].rearrange("p (n f) -> p n f", f=D), w2s[0:64, :].rearrange("p (n f) -> p n f", f=D), tiled(st[0:64, 5], 2), ALU.mult)
            v.tensor_copy(w2s[64:65, :].rearrange("p (n f) -> p n f", f=D), tiled(st[64:65, 7], 2))
            v.tensor_tensor(w4s[:, :].rearrange("p (n f) -> p n f", f=D), w4s[:, :].rearrange("p (n f) -> p n f", f=D), tiled(st[:, 5], 4), ALU.mult)
            v.tensor_copy(t16[0:1], tiled(st[0:1, 7], 16))
            v.memset(fx[64:65], 1.0)
            settle()
            v.memset(run[:, 0:1], 0.0).then_inc(bn_set, 1)

            def layer_norm(name, c, o, n=2 * TILES):
                yn = y[:, 0:n]
                v.tensor_reduce(ysum[:, 0:n], yn, AX.X, ALU.add)
                settle()
                v.scalar_tensor_tensor(yc[:, 0:n], over(ysum[:, 0:n]), 1.0 / D, yn, ALU.mult, ALU.subtract)
                settle()
                v.tensor_tensor(yq[:, 0:n], yc[:, 0:n], yc[:, 0:n], ALU.mult)
                settle()
                v.tensor_reduce(yvar[:, 0:n], yq[:, 0:n], AX.X, ALU.add).then_inc(var_set[name], 1)
                hold(dve, std_set[name], c + 1)
                v.reciprocal(yr[:, 0:n], ystd[:, 0:n])
                settle()
                return v.scalar_tensor_tensor(o, yc[:, 0:n], -1.0, over(yr[:, 0:n]), ALU.mult, ALU.mult)

            def pairs(c):
                return Z[:, at(c)].rearrange("p c t (h f) -> p (c t h) f", f=D)

            yh = y[:, :, :].rearrange("p (t h) f -> p t h f", h=2)

            def b_round(r):
                for j in range(RING):
                    c = RING * r + j
                    hold(dve, bn_out, c + 1)
                    v.scalar_tensor_tensor(y[:, :, :], bank[2 + j % 2][:, 0:2 * TILES * D].rearrange("p (n f) -> p n f", f=D), 0.0, pairs(c),
                                           ALU.max, ALU.add).then_inc(bn_used, 1)
                    settle()
                    layer_norm("B", c, pairs(c)).then_inc(stored["B"], 1)
                    settle()
            rounds(dve, b_round)

            def basis(name, c, j, n, xb_set, xb_used):
                def times(t):
                    hold(dve, xb_set, TILES * c + t + 1)
                    v.tensor_tensor(prod[:, t % 2, 0:D * n].rearrange("p (f n) -> p f n", n=n),
                                    bank[4 + (j + t) % 2][:, 0:D * n].rearrange("p (f n) -> p f n", n=n),
                                    ca[:, t, 0:n].unsqueeze(1).broadcast_to([128, D, n]), ALU.mult).then_inc(xb_used, 1)
                times(0)
                for t in range(TILES):
                    settle()
                    if t + 1 < TILES:
                        times(t + 1)
                    v.tensor_reduce(msg[:, t, :], prod[:, t % 2, 0:D * n].rearrange("p (f n) -> p f n", n=n), AX.X, ALU.add)
                settle()

            def q_view(b, n, lo, width):
                return b[:, 0:n * QW].rearrange("p (t w) -> p t w", w=QW)[:, :, lo:lo + width]

            halves = ((bank[2], 0, 4), (bank[3], 4, TILES))

            def one_hot(c):
                hold(dve, types_in, 16 * (c + 1))
                hold(dve, q_set, c)
                v.tensor_scalar(oh.rearrange("k (t b r) -> k b t r", b=BLOCKS, r=32), types.rearrange("k (b t r) -> k b t r", b=BLOCKS, r=32),
                                relno[:, 0:1], None, ALU.is_equal).then_inc(types_read, 1)

            def dots(c):
                hold(dve, cur_set, c + 1)
                for b, lo, hi in halves:
                    v.tensor_copy(msg2[:, lo:hi], q_view(b, hi - lo, Q2, D))
                settle()
                for b, lo, hi in halves:
                    v.tensor_tensor(yq[:, lo:hi], q_view(b, hi - lo, Q1, D), msg2[:, lo:hi], ALU.mult)
                settle()
                v.tensor_reduce(att[:, 2], yq[:, 0:TILES], AX.X, ALU.add)
                settle()
                v.tensor_scalar(att[:, 0], att[:, 2], float(D ** -0.5), 0.0, ALU.mult, ALU.max).then_inc(dot_set, 1)

            one_hot(0)
            dots(0)
            v.memset(run[:, 0:1], 0.0)
            settle()

            def r_round(r):
                for j in range(RING):
                    c = RING * r + j
                    if not last(c + 1):
                        one_hot(c + 1)
                    hold(dve, tanh_set, c + 1)
                    for b, lo, hi in halves:
                        op = v.tensor_tensor(ca[:, lo:hi], q_view(b, hi - lo, CO, BASES), over(att[:, 1, lo:hi], BASES), ALU.mult)
                    op.then_inc(q_used, 1)
                    settle()
                    basis("R", c, j, BASES, xb_set_r, xb_used_r)
                    if not last(c + 1):
                        dots(c + 1)
                    sum_runs(c)
                    v.tensor_tensor(agg[:, :, :], agg[:, :, :], cur[:, j % 2], ALU.add)
                    v.tensor_copy(yh[:, :, 0], chunk(Z, c, 0, D))
                    settle()
                    v.scalar_tensor_tensor(yh[:, :, 1], agg[:, :, :], 0.0, chunk(Z, c, D), ALU.max, ALU.add)
                    settle()
                    layer_norm("R", c, pairs(c)).then_inc(stored["R"], 1)
                    settle()
            rounds(dve, r_round)

            def dense(k):
                hold(dve, d_prod, k + 1)
                v.scalar_tensor_tensor(dy[:, 0:512], bank[2][:, :], 0.0, dx[:, 0:512], ALU.max, ALU.add)
                v.scalar_tensor_tensor(dy[:, 512:1024], bank[3][:, :], 0.0, dx[:, 512:1024], ALU.max, ALU.add).then_inc(d_y, 1)
                settle()

                def groups(t):
                    return t.rearrange("p (k f) -> p k f", f=D)
                v.tensor_reduce(dsum[:, :], groups(dy), AX.X, ALU.add)
                settle()
                v.scalar_tensor_tensor(groups(dc), over(dsum[:, :]), 1.0 / D, groups(dy), ALU.mult, ALU.subtract).then_inc(d_c1, 1)
                hold(dve, d_q1, k + 1)
                v.tensor_reduce(dvar[:, :], groups(dq), AX.X, ALU.add).then_inc(d_v1, 1)
                hold(dve, d_s1, k + 1)
                v.reciprocal(dr[:, :], dstd[:, :])
                settle()
                v.scalar_tensor_tensor(groups(dy), groups(dc), -1.0, over(dr[:, :]), ALU.mult, ALU.mult).then_inc(d_x2, 1)
                hold(dve, d_relu, k + 1)
                v.scalar_tensor_tensor(dc, dq, 1.0, dy, ALU.min, ALU.add)
                settle()
                v.tensor_reduce(dsum[:, :], groups(dc), AX.X, ALU.add)
                settle()
                v.scalar_tensor_tensor(groups(dq), over(dsum[:, :]), 1.0 / D, groups(dc), ALU.mult, ALU.subtract).then_inc(d_c2, 1)
                hold(dve, d_q2, k + 1)
                v.tensor_reduce(dvar[:, :], groups(dy), AX.X, ALU.add).then_inc(d_v2, 1)
                hold(dve, d_s2, k + 1)
                v.reciprocal(dr[:, :], dstd[:, :])
                settle()
                hold(dve, d_out, 16 * k)
                v.scalar_tensor_tensor(groups(do_), groups(dq), -1.0, over(dr[:, :]), ALU.mult, ALU.mult).then_inc(d_set, 1)
                settle()

            for name in ("O1", "O2", "O3"):
                v.memset(run[:, 0:1], 0.0)
                settle()

                def o_round(r, name=name):
                    for j in range(RING):
                        c = RING * r + j
                        hold(dve, gathered[name][j], GATHER * (r + 1))
                        v.tensor_tensor(msg[:, :, :], slot[:, j, :, 0:D], over(col(norm2, c)), ALU.mult).then_inc(used[name], 1)
                        v.tensor_scalar(msg2[:, :, :], chunk(Z, c, D), 1.0 - ALPHA, None, ALU.mult)
                        if name == "O1":
                            v.tensor_scalar(yq[:, 0:TILES], chunk(Z, c, 0, D), 1.0 - ALPHA, 0.0, ALU.mult, ALU.max)
                            settle()
                            v.tensor_scalar(chunk(P, c), yq[:, 0:TILES], 1.0, None, ALU.min)
                        settle()
                        sum_runs(c)
                        v.tensor_tensor(agg[:, :, :], agg[:, :, :], over(col(dis, c)), ALU.mult)
                        settle()
                        v.scalar_tensor_tensor(msg[:, :, :], agg[:, :, :], ALPHA, msg2[:, :, :], ALU.mult, ALU.add)
                        settle()
                        if name == "O3":
                            v.tensor_scalar(msg[:, :, :], msg[:, :, :], 0.0, 1.0, ALU.max, ALU.min)
                            v.tensor_tensor(yh[:, :, 0], chunk(Z, c, 0, D), chunk(P, c), ALU.add)
                            settle()
                            v.tensor_tensor(yh[:, :, 1], chunk(Z, c, D), msg[:, :, :], ALU.add)
                            settle()
                            layer_norm(name, c, pairs(c)).then_inc(stored[name], 1)
                        else:
                            if not (isinstance(c, int) and c < 2):
                                hold(dve, tabled[name][j % 2], 16 * (2 * r + j // 2))
                            v.tensor_scalar(ob[:, j % 2], msg[:, :, :], 0.0, 1.0, ALU.max, ALU.min).then_inc(stored[name], 1)
                        settle()
                        if name != "O3" and j % 2:
                            dense((0 if name == "O1" else 2 * ROUNDS) + 2 * r + j // 2)
                rounds(dve, o_round)

            v.memset(run[:, 0:1], 0.0)

            def h_round(r):
                for j in range(RING):
                    c = RING * r + j
                    v.tensor_copy(ca[:, :, 0:SH], scal[:, 6:PLANES, :, at(c)].rearrange("p k t c -> p t (k c)"))
                    settle()
                    basis("H", c, j, SH, xb_set_h, xb_used_h)
                    sum_runs(c)
                    v.tensor_tensor(y[:, 0:TILES], agg[:, :, :], chunk(Z, c, D), ALU.add)
                    if not (isinstance(c, int) and c < RING):
                        hold(dve, scattered[j], GATHER * r)
                    v.tensor_copy(oidx[:, j, :], col(i_out, c))
                    settle()
                    layer_norm("H", c, oslot[:, j], TILES).then_inc(rows_set, 1)
                    settle()
            rounds(dve, h_round)

        @block.tensor
        def _(pe):
            t_ = nc.tensor
            pe.wait_ge(consts_in, 16 * 13)
            pe.wait_ge(cleared, 1)
            t_.matmul(G, zer[:, 0:32], zer[:, 0:D + 1], start=True, stop=False)
            pe.wait_ge(ends_scanned, 1)
            t_.transpose(bank[6][0:1, 0:ROWS], bsum[:, BLOCK - 1:BLOCK], idn[0:ROWS, 0:ROWS])
            t_.transpose(bank[6][0:1, 128:128 + ROWS], bpref[:, BLOCK - 1:BLOCK], idn[0:ROWS, 0:ROWS])
            t_.transpose(bank[6][0:1, 256:256 + ROWS], bp[:, 5, 0:1], idn[0:ROWS, 0:ROWS])
            t_.transpose(bank[6][0:1, 384:384 + ROWS], blast[:, 0:1], idn[0:ROWS, 0:ROWS]).then_inc(ends_turned, 1)
            pe.wait_ge(ends_summed, 1)
            t_.matmul(bank[6][0:ROWS, 256:257], brow[0:1, 2, 0:ROWS], ones[0:1, 0:1], start=True, stop=True)
            t_.matmul(bank[6][0:ROWS, 257:258], brow[0:1, 5, 1:ROWS + 1], ones[0:1, 0:1], start=True, stop=True).then_inc(carry_out, 1)

            def stat(k, q, parts):
                hold(pe, sta_set, k + 1)
                for i in range(STATK):
                    op = t_.matmul(G, sta[0:parts, q, i, 0:D], sta[0:parts, q, i, 0:D + 1], start=False, stop=False)
                op.then_inc(sta_free, 1)
            with pe.Fori(0, (STATS - 1) // 2) as r:
                for q in range(2):
                    stat(2 * r + q, q, 128)
            for k in range(STATS - 1, STATS + 1):
                stat(k, k % 2, 128 if k < STATS else LEFT)

            def a_round(r):
                for j in range(RING):
                    c = RING * r + j
                    hold(pe, gram_set, c + 1)
                    for q in range(2):
                        for t in range(TILES):
                            end = isinstance(c, int) and c == CHUNKS - 1 and q == 1 and t == TILES - 1
                            op = t_.matmul(G, gl[:, q, t, :], gr[:, q, t, :], start=False, stop=end)
                    op.then_inc(gram_used, 1)
            rounds(pe, a_round)
            t_.drain().then_inc(gram_done, 1)
            pe.wait_ge(gram_read, 1)
            t_.matmul(bank[6][:, 0:D], srep[:, :], wg[:, :], start=True, stop=True)
            t_.matmul(bank[6][0:32, 64:64 + D], gram[:, 0:D], wg[:, :], start=True, stop=True).then_inc(mean_done, 1)
            pe.wait_ge(vv_set, 1)
            t_.matmul(bank[6][:, 128:128 + D], ones[0:32, :], vv[:, :], start=True, stop=True).then_inc(square_done, 1)

            def turn(name, rows, k):
                for t in range(TILES):
                    b = bank[0] if t < 4 else bank[1]
                    op = t_.transpose(b[0:k, 128 * (t % 4):128 * (t % 4) + 128], rows[:, t, 0:k], idn[:, :])
                op.then_inc(turned[name], 1)

            pe.wait_ge(bn_set, 1)

            def b_round(r):
                for j in range(RING):
                    c = RING * r + j
                    hold(pe, pz_set, c + 1)
                    hold(pe, fx_set["B"], c, pe_passed)
                    turn("B", pz, 2 * D)
                    hold(pe, fx_set["B"], c + 1)
                    hold(pe, bn_used, c - 1)
                    for t in range(TILES):
                        op = t_.matmul(bank[2 + j % 2][:, 2 * D * t:2 * D * (t + 1)], fx[0:65, j % 2, 128 * t:128 * (t + 1)], w2s[:, :],
                                       start=True, stop=True)
                    op.then_inc(bn_out, 1)
            rounds(pe, b_round)

            def products(name, c, j, rhs, n, xb_set, xb_used):
                for t in range(TILES):
                    hold(pe, xb_used, TILES * c + t - 1)
                    t_.matmul(bank[4 + (j + t) % 2][:, 0:n], fx[0:D, j % 2, 128 * t:128 * (t + 1)], rhs, start=True, stop=True).then_inc(xb_set, 1)

            def turn_r(c, r, j):
                hold(pe, gathered["R"][j], 2 * GATHER * (r + 1), pe_passed)
                turn("R", slot[:, j], 2 * D)

            def attend(c, j):
                hold(pe, fx_set["R"], c + 1)
                hold(pe, q_used, c)
                hold(pe, types_read, c + 1)
                for t in range(TILES):
                    b = bank[2] if t < 4 else bank[3]
                    o = QW * (t % 4)
                    t_.matmul(b[:, o:o + QW], fx[0:65, j % 2, 128 * t:128 * (t + 1)], wqs[:, :], start=True, stop=False)
                    op = t_.matmul(b[:, o + Q2:o + QW], oh[:, 128 * t:128 * (t + 1)], relcs[:, :], start=False, stop=True)
                op.then_inc(q_set, 1)
            turn_r(0, 0, 0)
            attend(0, 0)

            def r_round(r):
                for j in range(RING):
                    c = RING * r + j
                    if not last(c + 1):
                        turn_r(c + 1, r + (j + 1) // RING, (j + 1) % RING)
                    products("R", c, j, wcs[:, :], D * BASES, xb_set_r, xb_used_r)
                    if not last(c + 1):
                        attend(c + 1, j + 1)
            rounds(pe, r_round)

            def dense(k):
                hold(pe, d_in, 16 * (k + 1))
                hold(pe, d_xt, k)
                for g in range(8):
                    op = t_.transpose(bank[g // 4][:, 128 * (g % 4):128 * (g % 4 + 1)], dx[:, 128 * g:128 * (g + 1)], idn[:, :])
                op.then_inc(d_turned, 1)
                hold(pe, d_xt, k + 1)
                hold(pe, d_y, k)
                for h in range(2):
                    t_.matmul(bank[2 + h][:, :], ones[0:1, :], t16[0:1].rearrange("p n f -> p (n f)"), start=True, stop=False)
                for g in range(8):
                    op = t_.matmul(bank[2 + g // 4][:, 128 * (g % 4):128 * (g % 4 + 1)], dxt[:, 128 * g:128 * (g + 1)], w4s[:, :],
                                   start=False, stop=g % 4 == 3)
                op.then_inc(d_prod, 1)

            for first in (0, 2 * ROUNDS):
                def o_round(r, first=first):
                    for j in range(2):
                        dense(first + 2 * r + j)
                rounds(pe, o_round)

            def turn_h(c, r, j):
                hold(pe, gathered["H"][j], GATHER * (r + 1))
                hold(pe, fx_set["H"], c)
                turn("H", slot[:, j], D)
            turn_h(0, 0, 0)

            def h_round(r):
                for j in range(RING):
                    c = RING * r + j
                    if not last(c + 1):
                        turn_h(c + 1, r + (j + 1) // RING, (j + 1) % RING)
                    hold(pe, fx_set["H"], c + 1)
                    products("H", c, j, bs[:, :, :].rearrange("p f n -> p (f n)"), D * SH, xb_set_h, xb_used_h)
            rounds(pe, h_round)


def coupling():
    import math
    import numpy as np
    combos = [(0, 0, 0), (0, 1, 1), (1, 0, 1), (1, 1, 0), (1, 1, 1), (2, 1, 1)]

    def coefficient(j1, m1, j2, m2, j3, m3):
        f = math.factorial
        lo, hi = max(0, j2 - j3 - m1, j1 + m2 - j3), min(j1 + j2 - j3, j1 - m1, j2 + m2)
        pref = (2 * j3 + 1) * f(j3 + j1 - j2) * f(j3 - j1 + j2) * f(j1 + j2 - j3) / f(j1 + j2 + j3 + 1)
        pref *= f(j3 + m3) * f(j3 - m3) * f(j1 - m1) * f(j1 + m1) * f(j2 - m2) * f(j2 + m2)
        return math.sqrt(pref) * sum((-1) ** v / (f(v) * f(j1 + j2 - j3 - v) * f(j1 - m1 - v) * f(j2 + m2 - v) * f(j3 - j2 + m1 + v)
                                                  * f(j3 - j1 - m2 + v)) for v in range(lo, hi + 1))

    def basis(l):
        q = np.zeros((2 * l + 1, 2 * l + 1), complex)
        for m in range(-l, 0):
            q[l + m, l - m], q[l + m, l + m] = 2 ** -0.5, -1j * 2 ** -0.5
        q[l, l] = 1
        for m in range(1, l + 1):
            q[l + m, l + m], q[l + m, l - m] = (-1) ** m * 2 ** -0.5, 1j * (-1) ** m * 2 ** -0.5
        return (-1j) ** l * q

    table = np.zeros((6, D, D, SH), np.float32)
    for n, (l1, l2, l3) in enumerate(combos):
        c = np.zeros((2 * l1 + 1, 2 * l2 + 1, 2 * l3 + 1), complex)
        for m1 in range(-l1, l1 + 1):
            for m2 in range(-l2, l2 + 1):
                if abs(m1 + m2) <= l3:
                    c[m1 + l1, m2 + l2, m1 + m2 + l3] = coefficient(l1, m1, l2, m2, l3, m1 + m2)
        c = np.einsum("ij,kl,mn,ikn->jlm", basis(l1), basis(l2), np.conj(basis(l3)).T, c).real
        c /= np.linalg.norm(c)
        for m in range(8):
            for j in range(2 * l2 + 1):
                for o in range(8):
                    for k in range(2 * l3 + 1):
                        table[n, m if l2 == 0 else 8 + 3 * m + j, o if l3 == 0 else 8 + 3 * o + k, l1 * l1:(l1 + 1) ** 2] = c[:, j, k]
    return table


def kernel(**inputs):
    import numpy as np
    import concourse.bacc as bacc
    from concourse.bass_utils import run_bass_kernel_spmd as run

    a = {k: np.asarray(v) for k, v in inputs.items()}
    w = a["L0_gnn_W"]
    w2, w4 = np.zeros((65, 64), np.float32), np.zeros((128, 128), np.float32)
    for k in range(4):
        w4[32 * k:32 * k + 32, 32 * k:32 * k + 32] = w
    w2[0:64] = w4[0:64, 0:64]
    wq = np.zeros((65, QW), np.float32)
    wq[0:32, CUR:CUR + D] = a["L1_gnn_self_loop_weight"]
    wq[0:32, Q1:Q1 + D] = a["L1_gnn_A1_w"].T
    wq[64, Q1:Q1 + D] = a["L1_gnn_A1_b"]
    wq[32:64, Q2:Q2 + D] = a["L1_gnn_A2_w"].T
    wq[64, Q2:Q2 + D] = a["L1_gnn_A2_b"]
    relc = np.concatenate([a["L1_gnn_rel_emb"], a["L1_gnn_w_comp"]], axis=1)
    wcat = a["L1_gnn_weight"].transpose(1, 2, 0).reshape(D, D * BASES)
    channel = np.array([i if i < 8 else (i - 8) // 3 for i in range(D)])
    wt = a["L3_gnn_W"][:, channel][:, :, channel].transpose(1, 0, 2)
    cg = coupling().transpose(1, 0, 2, 3)
    p, t, c = np.meshgrid(np.arange(128), np.arange(TILES), np.arange(32), indexing="ij")
    own = (CHUNK * c + TILES * p + t).astype(np.float32)
    k, t, lane = (v.reshape(-1) for v in np.meshgrid(np.arange(ROWS), np.arange(TILES), np.arange(32), indexing="ij"))
    own_blocks = (CHUNK * (k // BLOCKS) + TILES * (32 * (k % BLOCKS) + lane) + t).astype(np.float32).reshape(ROWS, BLOCK)
    ins = {
        "x": a["x"], "src": a["src"], "dst": a["dst"], "attr3": a["edge_attr_3"].reshape(-1), "attr5": a["edge_attr_5"].reshape(-1),
        "etype": a["edge_type_86"], "ew": a["edge_weight"], "ew1": a["edge_weight1"].reshape(-1),
        "bgb_in": np.stack([a["L0_gnn_b"], a["L0_gnn_gamma"], a["L0_gnn_beta"]]), "w_gcn": w, "w2": w2, "w4": w4, "wq": wq,
        "relc": relc, "wcat": wcat, "cg": cg, "wt": wt, "ident": np.eye(128, dtype=np.float32), "own_in": own, "own_blocks": own_blocks,
        "relno_in": np.arange(RELS, dtype=np.float32)[:, None],
    }
    nc = bacc.Bacc("TRN2", target_bir_lowering=False, num_devices=1)
    aps = {}
    for name, v in ins.items():
        ins[name] = v = np.ascontiguousarray(v)
        aps[name] = nc.dram_tensor(name, v.shape, mybir.dt.from_np(v.dtype), kind="ExternalInput").ap()
    for name, shape, dt in (("aug", (N, AUG), mybir.dt.float32), ("plane", (PLANES, ROWS * BLOCK), mybir.dt.float32),
                            ("mask", (2, ROWS * BLOCK), mybir.dt.bfloat16),
                            *((f"tab_{k}", (ROWS * BLOCK, D), mybir.dt.float32) for k in ("b", "r", "o1", "o2", "o3"))):
        aps[name] = nc.dram_tensor(name, shape, dt, kind="Internal").ap()
    aps["out"] = nc.dram_tensor("out", (N, D), mybir.dt.float32, kind="ExternalOutput").ap()
    build(nc, **aps)
    return run(nc, [ins], core_ids=[0]).results[0]["out"]
```

```python
from contextlib import ExitStack

import concourse.bass as bass
from concourse import mybir

N, E, D = 100000, 25000, 32
BLOCKS, TILES = 4, 7
BLOCK = TILES * 32
CHUNK = BLOCKS * BLOCK
CHUNKS = -(-E // CHUNK)
PAIRS = CHUNKS // 2
PT = 2 * TILES
PAIR = 2 * CHUNK
RING = 2
ROUNDS = PAIRS // RING
ROWS = CHUNKS * BLOCKS
FULL = E // BLOCK
TAIL = E - FULL * BLOCK
FAR = 2 * N
NOWHERE = 1 << 22
AUG = 36
BASES, RELS = 16, 86
SH = 9
PLANES = 6 + SH
STATK = 25
STATS = N // (128 * STATK)
LEFT = (N - STATS * 128 * STATK) // STATK
DK = 32
DSTEPS = 2 * PAIRS
DSTRIDE = (N - 128 * DK) // (DSTEPS - 1)
assert (N - 128 * DK) % (DSTEPS - 1) == 0 and CHUNKS == 2 * RING * ROUNDS and LEFT * STATK == N - STATS * 128 * STATK
EPS = 1e-5
ALPHA = 0.9
TINY = 1.2e-38
GATHER = 16 * PT
CUR, Q1, Q2, CO, QW = 0, 32, 64, 96, 112


def at(n):
    return slice(n, n + 1) if isinstance(n, int) else bass.ds(n, 1)


def whole(t):
    return t[tuple([slice(None)] * len(t.shape))]


def build(nc, x, src, dst, attr3, attr5, etype, ew, ew1, bgb_in, w_gcn, w2, w4, wq, relc, wcat, cg, wt,
          ident, own_in, own_blocks, relno_in, aug, plane, mask, tab_b, tab_r, tab_o1, tab_o2, tab_o3, out):
    fp32, bf16, i32 = mybir.dt.float32, mybir.dt.bfloat16, mybir.dt.int32
    ALU, ACT, AX = mybir.AluOpType, mybir.ActivationFunctionType, mybir.AxisListType
    ctx = ExitStack()
    with ctx:
        def sb(name, shape, dt=fp32):
            return ctx.enter_context(nc.sbuf_tensor(name, shape, dt))

        def sem(name):
            return ctx.enter_context(nc.semaphore(name))

        Z = sb("Z", [128, PAIRS, PT, 2 * D])
        P = sb("P", [128, PAIRS, PT, D])
        slot = sb("slot", [128, RING, PT, 2 * D])
        idx = sb("idx", [128, RING, PT], i32)
        oslot = sb("oslot", [128, RING, PT, D])
        oidx = sb("oidx", [128, RING, PT], i32)
        cont = sb("cont", [128, CHUNKS, BLOCK], bf16)
        pref = sb("pref", [128, CHUNKS, BLOCK], bf16)
        through = sb("through", [32, ROWS], bf16)
        scal = sb("scal", [128, PLANES, PAIRS, PT])
        srcs, dsts, degree, ends, weight, home = (scal[:, k] for k in range(6))
        dinv = sb("dinv", [128, PAIRS, PT])
        dis = sb("dis", [128, PAIRS, PT])
        endinv = sb("endinv", [128, PAIRS, PT])
        minus = sb("minus", [128, PAIRS, PT])
        norm2 = sb("norm2", [128, PAIRS, PT])
        i_src = sb("i_src", [128, PAIRS, PT], i32)
        i_dst = sb("i_dst", [128, PAIRS, PT], i32)
        i_aug = sb("i_aug", [128, PAIRS, PT], i32)
        i_out = sb("i_out", [128, PAIRS, PT], i32)
        i_ptr = sb("i_ptr", [128, PAIRS, PT], i32)
        i_home = sb("i_home", [128, PAIRS, PT], i32)
        idx2 = sb("idx2", [128, RING, PT], i32)
        trow = sb("trow", [128, PAIRS, PT, 4])
        tslot = sb("tslot", [128, RING, PT, 4])
        planes = Z[:, :, :, :].rearrange("p c t f -> p (c t f)")
        natural = planes[:, 0:PLANES * BLOCK].rearrange("p (k e) -> p k e", e=BLOCK)
        bp = planes[0:ROWS, PLANES * BLOCK:2 * PLANES * BLOCK].rearrange("p (k e) -> p k e", e=BLOCK)
        raw = planes[:, 2 * PLANES * BLOCK:3 * PLANES * BLOCK]
        left = planes[:, 3 * PLANES * BLOCK:3 * PLANES * BLOCK + 7 * PAIRS * PT].rearrange("p (k c t) -> p k c t", k=7, t=PT)
        ta, tb, tm, own = left[:, 0:2], left[:, 2:4], left[:, 4:6], left[:, 6]
        wide = sb("wide", [128, 6 * DK * D])
        dx, dy, dc, dq, do_, dxt = (wide[:, k * DK * D:(k + 1) * DK * D] for k in range(6))
        cgs = wide[0:D, 0:6 * D * SH].rearrange("p (k f n) -> p k f n", k=6, f=D)
        bs2 = wide[0:D, 6 * D * SH:7 * D * SH].rearrange("p (f n) -> p f n", n=SH)
        by_rows = wide[0:ROWS, 7 * D * SH:]
        raw3, raw5 = by_rows[:, 0:3 * BLOCK], by_rows[:, 3 * BLOCK:8 * BLOCK]
        bcont, bpref, bsum, bzero = (by_rows[:, k * BLOCK:(k + 1) * BLOCK] for k in range(8, 12))
        bdst, bprev, bnext, bsrc = (by_rows[:, k * BLOCK:(k + 1) * BLOCK].bitcast(i32) for k in range(12, 16))
        bmask = by_rows[:, 16 * BLOCK:17 * BLOCK].bitcast(bf16).rearrange("p (k e) -> p k e", k=2)
        bown = by_rows[:, 17 * BLOCK:18 * BLOCK]
        bgo, bback, blast = (raw3[:, k * BLOCK:(k + 1) * BLOCK] for k in range(3))
        gl = wide[:, 0:2 * PT * D].rearrange("p (q t f) -> p q t f", q=2, t=PT)
        gr = wide[:, 2 * PT * D:2 * PT * (2 * D + 1)].rearrange("p (q t f) -> p q t f", q=2, t=PT)
        oh = wide[:, 0:PAIR].rearrange("p (h e) -> p h e", h=2)
        types = wide[:, PAIR:2 * PAIR].bitcast(i32)
        prod = wide[:, 2 * PAIR:2 * PAIR + 4 * D * BASES].rearrange("p (q k n) -> p q k n", q=2, k=2)
        wide2 = sb("wide2", [128, PAIR + PT * (QW + D)])
        stx = wide2[:, 0:2 * STATK * D].rearrange("p (q k f) -> p q k f", q=2, f=D)
        sta = wide2[:, 2 * STATK * D:2 * STATK * (D + AUG)].rearrange("p (q k f) -> p q k f", q=2, f=AUG)
        fx = wide2[:, 0:PAIR].rearrange("p (q e) -> p q e", q=2)
        pz = wide2[:, PAIR:PAIR + PT * 2 * D].rearrange("p (t f) -> p t f", f=2 * D)
        cur = wide2[:, PAIR:PAIR + 2 * PT * D].rearrange("p (q t f) -> p q t f", q=2, f=D)
        qs = wide2[:, PAIR + 2 * PT * D:PAIR + PT * (QW + D)].rearrange("p (t f) -> p t f", f=QW - D)
        brow = sb("brow", [1, 6, ROWS + 1])
        bcarry = sb("bcarry", [ROWS, 2])
        msg, msg2 = (sb(n, [128, PT, D]) for n in ("msg", "msg2"))
        agg = msg
        turned_ = sb("turned_", [128, 2, 2 * BLOCK])
        fm, fs = turned_[:, 0], turned_[:, 1]
        fo = fm
        yq = turned_[:, :, :].rearrange("p q (t f) -> p (q t) f", f=D)
        blk = sb("blk", [32, 2 * BLOCKS])
        run = sb("run", [32, 2 * BLOCKS + 1])
        carry = sb("carry", [128, 2])
        y, yc = (sb(n, [128, 2 * PT, D]) for n in ("y", "yc"))
        ysum, yvar, ystd, yr = (sb(n, [128, 2 * PT]) for n in ("ysum", "yvar", "ystd", "yr"))
        sw = sb("sw", [128, PT])
        ob = sb("ob", [128, PT, D])
        ca = sb("ca", [128, PT, BASES])
        att = sb("att", [128, 3, PT])
        eps = sb("eps", [128, 2])
        dsum, dvar, dstd, dr = (sb(n, [128, DK]) for n in ("dsum", "dvar", "dstd", "dr"))
        idn = sb("idn", [128, 128])
        zer = sb("zer", [128, D + 1])
        ones = sb("ones", [128, 128])
        gram = sb("gram", [32, D + 1])
        wg, vv = sb("wg", [32, D]), sb("vv", [32, D])
        srep = sb("srep", [32, 128])
        bgb = sb("bgb", [128, 3, D])
        st = sb("st", [128, 8, D])
        w2s = sb("w2s", [128, 2 * D])
        w4s = sb("w4s", [128, 128])
        t16 = sb("t16", [1, 16, D])
        wqs = sb("wqs", [128, QW])
        relcs = sb("relcs", [128, D + BASES])
        wcs = sb("wcs", [128, D * BASES])
        relno = sb("relno", [128, 1])
        wts = sb("wts", [32, 6, D])
        bs = sb("bs", [128, D, SH])
        bank = [ctx.enter_context(nc.psum_tensor(f"bank{i}", [128, 512], fp32)) for i in range(8)]
        G = bank[7][0:32, 0:D + 1]

        (cleared, blocks_in, consts_in, planes_set, planes_out, planes_in, masks_in, ends_scanned, ends_turned,
         ends_summed, carry_out, roots_in, roots_out, indices_set, own_used, stx_free, sta_set, sta_free) = (sem(n) for n in (
             "cleared blocks_in consts_in planes_set planes_out planes_in masks_in ends_scanned ends_turned "
             "ends_summed carry_out roots_in roots_out indices_set own_used stx_free sta_set sta_free").split())
        stx_in = [sem(f"stx_in{q}") for q in range(2)]
        aug_out = [sem(f"aug_out{q}") for q in range(2)]
        (gram_done, gram_read, mean_done, vv_set, square_done, spread_in, spread_out, bn_set, table3_set) = (sem(n) for n in (
            "gram_done gram_read mean_done vv_set square_done spread_in spread_out bn_set table3_set").split())
        def each(what, passes):
            return {n: sem(f"{what}_{n}") for n in passes.split()}

        staged = each("staged", "D T A R O1 O2 O3 H")
        used = each("used", "A O1 O2 O3")
        stored = each("stored", "B R O1 O2 O3")
        turned = each("turned", "B R H")
        fx_set = each("fx_set", "B R H")
        var_set = each("var_set", "B R O3 H")
        std_set = each("std_set", "B R O3 H")
        gathered = {n: [sem(f"gathered_{n}{j}") for j in range(RING)] for n in "D T A R O1 O2 O3 H".split()}
        scattered = [sem(f"scattered{j}") for j in range(RING)]
        tabled = {n: [sem(f"tabled_{n}{j}") for j in range(RING)] for n in "B R O1 O2 O3".split()}
        (copied_a, gram_set, gram_used, pz_set, bn_out, bn_used, types_in, types_read, q_set, q_out, q_used, dot_set, tanh_set,
         xb_set_r, xb_used_r, xb_set_h, xb_used_h, rows_set) = (sem(n) for n in (
             "copied_a gram_set gram_used pz_set bn_out bn_used types_in types_read q_set q_out q_used dot_set tanh_set "
             "xb_set_r xb_used_r xb_set_h xb_used_h rows_set").split())
        pool_passed, pe_passed = sem("pool_passed"), sem("pe_passed")
        (d_in, d_turned, d_xt, d_prod, d_y, d_c1, d_q1, d_v1, d_s1, d_x2, d_relu, d_c2, d_q2, d_v2, d_s2, d_set, d_out) = (
            sem(f"dense_{n}") for n in "in turned xt prod y c1 q1 v1 s1 x2 relu c2 q2 v2 s2 set out".split())
        block = ctx.enter_context(nc.Block())

        def rounds(eng, body):
            body(0)
            with eng.Fori(1, ROUNDS - 1) as r:
                body(r)
            body(ROUNDS - 1)

        def hold(eng, semaphore, value, passed=None):
            if isinstance(value, int):
                if value > 0:
                    eng.wait_ge(semaphore, value)
            else:
                eng.wait_ge(semaphore, value)
                if passed is not None:
                    eng.sem_inc(passed, 1)

        def last(c):
            return isinstance(c, int) and c >= PAIRS

        def col(t, c):
            return t[:, at(c)].rearrange("p c t -> p (c t)")

        def chunk(t, c, a=0, z=None):
            return t[:, at(c), :, a:z].rearrange("p c t f -> p (c t) f")

        turns = ((bank[0], bank[1]), (bank[6], bank[7]))

        def over(v, n=D):
            return v.unsqueeze(2).broadcast_to([v.shape[0], v.shape[1], n])

        @block.sync
        def _(sp):
            for t, a in ((idn, ident), (own, own_in), (bown, own_blocks), (relno, relno_in), (wg, w_gcn), (w2s, w2), (w4s, w4), (wqs, wq),
                         (relcs, relc), (wcs, wcat), (cgs, cg), (wts, wt), (bgb, bgb_in.unsqueeze(0).broadcast_to([128, 3, D]))):
                sp.dma_start(whole(t), a).then_inc(consts_in, 16)
            sp.wait_ge(cleared, 1)
            sp.dma_start(bprev[0:1, 1:BLOCK], dst[0:BLOCK - 1].unsqueeze(0)).then_inc(blocks_in, 16)
            for t, a, lo, off, w in ((bdst, dst, 0, 0, 1), (bprev, dst, 1, -1, 1), (bnext, dst, 0, 1, 1), (bsrc, src, 0, 0, 1),
                                     (bp[:, 4], ew, 0, 0, 1), (bp[:, 6], ew1, 0, 0, 1), (raw3, attr3, 0, 0, 3), (raw5, attr5, 0, 0, 5)):
                k = BLOCK * w
                sp.dma_start(t[lo:FULL, :], a[lo * k + off:FULL * k + off].rearrange("(p k) -> p k", k=k)).then_inc(blocks_in, 16)
                sp.dma_start(t[FULL:FULL + 1, 0:TAIL * w - off], a[FULL * k + off:E * w].unsqueeze(0)).then_inc(blocks_in, 16)
            sp.wait_ge(planes_set, 1)
            sp.dma_start(plane.rearrange("k (p e) -> p k e", e=BLOCK), bp).then_inc(planes_out, 16)
            sp.dma_start(mask.rearrange("k (p e) -> p k e", e=BLOCK), bmask[:, :, :]).then_inc(planes_out, 16)
            sp.wait_ge(planes_out, 32)
            by_block = plane.rearrange("k (c b e) -> b c k e", b=BLOCKS, e=BLOCK)
            masks = mask.rearrange("k (c b e) -> k b c e", b=BLOCKS, e=BLOCK)
            for q in range(BLOCKS):
                sp.dma_start(natural[32 * q:32 * q + CHUNKS], by_block[q]).then_inc(planes_in, 16)
            for k, t in enumerate((cont, pref)):
                for q in range(BLOCKS):
                    sp.dma_start(t[32 * q:32 * q + 32], masks[k, q].unsqueeze(0).broadcast_to([32, CHUNKS, BLOCK])).then_inc(masks_in, 16)
            ends_row = mask.rearrange("k (p e) -> k e p", e=BLOCK)[1, BLOCK - 1]
            with nc.allow_non_contiguous_dma("one column of the blocks"):
                sp.dma_start(through[:, :], ends_row.unsqueeze(0).broadcast_to([32, ROWS])).then_inc(masks_in, 16)

            def load_stat(q, n0, parts):
                rows = x[n0:n0 + parts * STATK] if isinstance(n0, int) else x[bass.ds(n0, parts * STATK)]
                sp.dma_start(stx[0:parts, q], rows.rearrange("(p k) f -> p k f", k=STATK)).then_inc(stx_in[q], 16)

            def store_stat(q, n0, parts):
                rows = aug[n0:n0 + parts * STATK] if isinstance(n0, int) else aug[bass.ds(n0, parts * STATK)]
                sp.dma_start(rows.rearrange("(p k) f -> p k f", k=STATK), sta[0:parts, q]).then_inc(aug_out[q], 16)

            step = 128 * STATK
            load_stat(0, 0, 128)
            load_stat(1, step, 128)
            with sp.Fori(0, (STATS - 3) // 2) as r:
                for q in range(2):
                    k = 2 * r + q
                    hold(sp, sta_set, k + 1)
                    store_stat(q, k * step, 128)
                    load_stat(q, (k + 2) * step, 128)
            for k in range(STATS - 3, STATS + 1):
                sp.wait_ge(sta_set, k + 1)
                store_stat(k % 2, k * step, 128 if k < STATS else LEFT)
                if k + 2 <= STATS:
                    load_stat(k % 2, (k + 2) * step, 128 if k + 2 < STATS else LEFT)

            def store_table(name, table, c, j, rows):
                hold(sp, stored[name], c + 1)
                view = table.rearrange("(c p t) f -> c p t f", p=128, t=PT)[at(c)]
                sp.dma_start(view.rearrange("c p t f -> (c p) t f"), rows).then_inc(tabled[name][j], 16)

            def dense_rows(t, k):
                n = 128 * DK
                v = t[k * DSTRIDE:k * DSTRIDE + n] if isinstance(k, int) else t[bass.ds(k * DSTRIDE, n)]
                return v.rearrange("(p k) f -> p (k f)", k=DK)

            def dense_store(k):
                hold(sp, d_set, k + 1)
                sp.dma_start(dense_rows(out, k), do_).then_inc(d_out, 16)

            def dense_load(k):
                hold(sp, d_y, k)
                sp.dma_start(dx, dense_rows(x, k)).then_inc(d_in, 16)

            def b_round(r):
                for j in range(RING):
                    c = RING * r + j
                    store_table("B", tab_b, c, j, chunk(Z, c, D))
            rounds(sp, b_round)

            def load_types(c):
                n = min(PAIR, E - c * PAIR) if isinstance(c, int) else PAIR
                row = etype[c * PAIR:c * PAIR + n] if isinstance(c, int) else etype[bass.ds(c * PAIR, n)]
                hold(sp, types_read, c)
                sp.dma_start(types[:, 0:n], row.unsqueeze(0).broadcast_to([128, n])).then_inc(types_in, 16)

            def r_round(r):
                for j in range(RING):
                    c = RING * r + j
                    if not last(c + 1):
                        load_types(c + 1)
                    store_table("R", tab_r, c, j, chunk(Z, c, D))
            load_types(0)
            rounds(sp, r_round)

            dense_load(0)
            for name, table, first in (("O1", tab_o1, 0), ("O2", tab_o2, PAIRS)):
                def o_round(r, name=name, table=table, first=first):
                    for j in range(RING):
                        k = first + RING * r + j
                        if not (isinstance(k, int) and k == DSTEPS - 1):
                            dense_load(k + 1)
                        store_table(name, table, RING * r + j, j, ob[:, :, :])
                        dense_store(k)
                rounds(sp, o_round)

            def o3_round(r):
                for j in range(RING):
                    c = RING * r + j
                    store_table("O3", tab_o3, c, j, chunk(Z, c, D))
            rounds(sp, o3_round)
            sp.wait_ge(d_out, 16 * DSTEPS)

        @block.gpsimd
        def _(pool):
            def gather(name, table, rows, c, j, width=D):
                hold(pool, staged[name], c + 1, pool_passed)
                for t in range(PT):
                    nc.gpsimd.indirect_dma_start(
                        slot[:, j, t, 0:width], None, table, bass.IndirectOffsetOnAxis(ap=idx[:, j, t:t + 1], axis=0),
                        bounds_check=rows - 1, oob_is_err=False).then_inc(gathered[name][j], 16)
                if name == "R":
                    for t in range(PT):
                        nc.gpsimd.indirect_dma_start(
                            slot[:, j, t, D:2 * D], None, table, bass.IndirectOffsetOnAxis(ap=idx2[:, j, t:t + 1], axis=0),
                            bounds_check=rows - 1, oob_is_err=False).then_inc(gathered[name][j], 16)

            def gathers(name, table, rows, width=D):
                def body(r):
                    for j in range(RING):
                        gather(name, table, rows, RING * r + j, j, width)
                rounds(pool, body)

            gathers("D", x, N)
            for q in range(2):
                pool.wait_ge(aug_out[q], 16 * ((STATS + 2 - q) // 2))
            quads = aug.rearrange("n (a f) -> (n a) f", f=4)

            def t_round(r):
                for j in range(RING):
                    hold(pool, staged["T"], RING * r + j + 1, pool_passed)
                    for t in range(PT):
                        nc.gpsimd.indirect_dma_start(
                            quads, bass.IndirectOffsetOnAxis(ap=idx[:, j, t:t + 1], axis=0), tslot[:, j, t, :], None,
                            bounds_check=N * AUG // 4 - 1, oob_is_err=False).then_inc(gathered["T"][j], 16)
            rounds(pool, t_round)
            for j in range(RING):
                pool.wait_ge(gathered["T"][j], GATHER * ROUNDS)
            gathers("A", aug, N, AUG)
            for name, prev, table in (("R", "B", tab_b), ("O1", "R", tab_r), ("O2", "O1", tab_o1), ("O3", "O2", tab_o2)):
                for q in range(2):
                    pool.wait_ge(tabled[prev][q], 16 * PAIRS // 2)
                gathers(name, table, ROWS * BLOCK)
            for q in range(2):
                pool.wait_ge(tabled["O3"][q], 16 * PAIRS // 2)
            pool.wait_ge(d_out, 16 * DSTEPS)

            def scatter(c, j):
                hold(pool, rows_set, c + 1, pool_passed)
                for t in range(PT):
                    nc.gpsimd.indirect_dma_start(
                        out, bass.IndirectOffsetOnAxis(ap=oidx[:, j, t:t + 1], axis=0), oslot[:, j, t, :], None,
                        bounds_check=N - 1, oob_is_err=False).then_inc(scattered[j], 16)

            def h_round(r):
                for j in range(RING):
                    c = RING * r + j
                    gather("H", tab_o3, ROWS * BLOCK, c, j)
                    if not (isinstance(c, int) and c == 0):
                        scatter(c - 1, (j - 1) % RING)
            rounds(pool, h_round)
            scatter(PAIRS - 1, (PAIRS - 1) % RING)
            for j in range(RING):
                pool.wait_ge(scattered[j], GATHER * ROUNDS)

        @block.scalar
        def _(act):
            def copy(o, i):
                return nc.scalar.activation(o, i, ACT.Copy)

            act.wait_ge(cleared, 1)
            act.wait_ge(roots_in, 1)
            nc.scalar.activation(tb, ta, ACT.Sqrt).then_inc(roots_out, 1)

            def stat(k, r, q, parts):
                hold(act, stx_in[q], 16 * (r + 1))
                hold(act, sta_free, k - 1)
                hold(act, aug_out[q], 16 * r)
                copy(sta[0:parts, q, :, 0:D], stx[0:parts, q]).then_inc(sta_set, 1)
            for k in range(2):
                stat(k, 0, k, 128)
            with act.Fori(1, STATS // 2) as r:
                for q in range(2):
                    stat(2 * r + q, r, q, 128)
            for k in range(STATS - 1, STATS + 1):
                stat(k, k // 2, k % 2, 128 if k < STATS else LEFT)

            def stage(name, c, j, rows, index):
                if rows is not None:
                    copy(slot[:, j, :, 0:D], chunk(rows, c, 0, D))
                copy(idx[:, j, :], col(index, c)).then_inc(staged[name], 1)

            for j in range(RING):
                act.wait_ge(gathered["T"][j], GATHER * ROUNDS)
            for c in range(RING):
                stage("A", c, c, None, i_src)

            def a_round(r):
                for j in range(RING):
                    c = RING * r + j
                    hold(act, gathered["A"][j], GATHER * (r + 1))
                    copy(chunk(Z, c, 0, D), slot[:, j, :, 0:D]).then_inc(copied_a, 1)
                    if not last(c + RING):
                        hold(act, used["A"], c + 1)
                        stage("A", c + RING, j, None, i_src)
            rounds(act, a_round)

            act.wait_ge(spread_in, 1)
            nc.scalar.activation(st[:, 4], st[:, 3], ACT.Sqrt, bias=eps[:, 0:1]).then_inc(spread_out, 1)

            def root(name, c, n=2 * PT):
                hold(act, var_set[name], c + 1)
                nc.scalar.activation(ystd[:, 0:n], yvar[:, 0:n], ACT.Sqrt, bias=eps[:, 0:1], scale=1.0 / D).then_inc(std_set[name], 1)

            def evacuate(name, c, h, k):
                a, b = turns[h]
                hold(act, turned[name], c + 1)
                copy(fx[0:k, h, 0:512], a[0:k, :])
                copy(fx[0:k, h, 512:CHUNK], b[0:k, 0:CHUNK - 512]).then_inc(fx_set[name], 1)

            act.wait_ge(bn_set, 1)

            def fetch_b(c):
                hold(act, turned["B"], 2 * c)
                copy(pz[:, :, 0:D], chunk(Z, c, 0, D))
                copy(pz[:, :, D:], chunk(P, c, 0, D)).then_inc(pz_set, 1)
                for h in range(2):
                    hold(act, bn_out, 2 * c + h - 1)
                    evacuate("B", 2 * c + h, h, 2 * D)
            fetch_b(0)

            def b_round(r):
                for j in range(RING):
                    c = RING * r + j
                    if not last(c + 1):
                        fetch_b(c + 1)
                    root("B", c)
            rounds(act, b_round)

            act.wait_ge(stored["B"], PAIRS)

            def stage_r(c, j):
                copy(idx2[:, j, :], col(i_home, c))
                stage("R", c, j, Z, i_ptr)
            for c in range(RING):
                stage_r(c, c)

            def fetch_r(c, j):
                for h in range(2):
                    hold(act, xb_set_r, TILES * (2 * c + h - 1))
                    evacuate("R", 2 * c + h, h, 2 * D)
                    if h == 0:
                        hold(act, q_used, c)
                    hold(act, q_set, 2 * c + h + 1)
                    for b, lo, hi in ((bank[2], 0, 4), (bank[3], 4, TILES)):
                        q = b[:, 0:(hi - lo) * QW].rearrange("p (t w) -> p t w", w=QW)
                        copy(cur[:, j, TILES * h + lo:TILES * h + hi], q[:, :, 0:D])
                        op = copy(qs[:, TILES * h + lo:TILES * h + hi], q[:, :, D:])
                    op.then_inc(q_out, 1)
                hold(act, dot_set, c + 1)
                nc.scalar.activation(att[:, 1], att[:, 0], ACT.Tanh).then_inc(tanh_set, 1)
            fetch_r(0, 0)

            def r_round(r):
                for j in range(RING):
                    c = RING * r + j
                    if not last(c + RING):
                        hold(act, turned["R"], 2 * c + 2)
                        stage_r(c + RING, j)
                    if not last(c + 1):
                        hold(act, stored["R"], c)
                        fetch_r(c + 1, (j + 1) % RING)
                    root("R", c)
            rounds(act, r_round)

            def dense_turned(k):
                hold(act, d_turned, k + 1)
                hold(act, d_prod, k)
                copy(dxt[:, 0:512], bank[0][:, :])
                copy(dxt[:, 512:1024], bank[1][:, :]).then_inc(d_xt, 1)

            def dense_square1(k):
                hold(act, d_c1, k + 1)
                nc.scalar.activation(dq, dc, ACT.Square).then_inc(d_q1, 1)

            def dense(k, more):
                hold(act, d_v1, k + 1)
                nc.scalar.activation(dstd[:, :], dvar[:, :], ACT.Sqrt, bias=eps[:, 1:2], scale=(1.0 + EPS) / D).then_inc(d_s1, 1)
                hold(act, d_x2, k + 1)
                nc.scalar.activation(dq, dy, ACT.Relu, scale=1.0 - ALPHA).then_inc(d_relu, 1)
                if more:
                    dense_turned(k + 1)
                hold(act, d_c2, k + 1)
                nc.scalar.activation(dy, dq, ACT.Square).then_inc(d_q2, 1)
                hold(act, d_v2, k + 1)
                nc.scalar.activation(dstd[:, :], dvar[:, :], ACT.Sqrt, bias=eps[:, 1:2], scale=(1.0 + EPS) / D).then_inc(d_s2, 1)
            dense_turned(0)

            for name, prev, rows in (("O1", "R", Z), ("O2", "O1", P), ("O3", "O2", P)):
                act.wait_ge(stored[prev], PAIRS)
                for c in range(RING):
                    stage(name, c, c, rows, i_ptr)

                def o_round(r, name=name, rows=rows):
                    for j in range(RING):
                        c = RING * r + j
                        k = (0 if name == "O1" else PAIRS) + c
                        if name != "O3":
                            dense_square1(k)
                        if not last(c + RING):
                            hold(act, used[name], c + 1)
                            stage(name, c + RING, j, rows, i_ptr)
                        if name == "O3":
                            root(name, c)
                        else:
                            dense(k, not (isinstance(k, int) and k == DSTEPS - 1))
                rounds(act, o_round)

            act.wait_ge(stored["O3"], PAIRS)
            for c in range(RING):
                stage("H", c, c, Z, i_ptr)

            def fetch_h(c):
                for h in range(2):
                    hold(act, xb_set_h, TILES * (2 * c + h - 1))
                    evacuate("H", 2 * c + h, h, D)
            fetch_h(0)

            def h_round(r):
                for j in range(RING):
                    c = RING * r + j
                    if not last(c + RING):
                        hold(act, turned["H"], 2 * c + 2)
                        stage("H", c + RING, j, Z, i_ptr)
                    root("H", c, PT)
                    if not last(c + 1):
                        fetch_h(c + 1)
            rounds(act, h_round)

        @block.vector
        def _(dve):
            v = nc.vector

            def settle():
                v.drain()

            v.memset(whole(bs), 0.0)
            for t, value in ((bdst, FAR), (bprev, FAR), (bnext, FAR), (bsrc, 0)):
                v.memset(t[:, :], value)
            for t, value in ((planes[:, 0:2 * PLANES * BLOCK], 0.0), (by_rows[:, 0:12 * BLOCK], 0.0), (brow, 0.0), (zer, 0.0), (ones, 1.0), (eps[:, 0:1], EPS),
                             (eps[:, 1:2], EPS * EPS), (slot, 0.0), (trow, 0.0), (sta, 0.0)):
                v.memset(whole(t), value)
            settle()
            v.memset(bprev[0:1, 0:1], -1)
            v.memset(sta[:, :, :, D:D + 1], 1.0)
            v.memset(sta[:, :, :, D + 2:D + 3], float(NOWHERE))
            settle()
            v.memset(run[:, 0:1], 0.0).then_inc(cleared, 1)

            dve.wait_ge(blocks_in, 16 * 17)
            v.tensor_tensor(bcont, bdst[:, :], bprev[:, :], ALU.is_equal)
            v.tensor_tensor(bp[:, 3], bdst[:, :], bnext[:, :], ALU.not_equal)
            v.tensor_copy(bp[:, 0], bsrc[:, :])
            v.tensor_copy(bp[:, 1], bdst[:, :])
            v.tensor_copy(bp[:, 7:10], raw3.rearrange("p (e k) -> p k e", k=3))
            v.tensor_copy(bp[:, 10:15], raw5.rearrange("p (e k) -> p k e", k=5))
            settle()
            v.tensor_tensor_scan(bsum, bcont, bp[:, 4], 0.0, ALU.mult, ALU.add)
            v.tensor_tensor_scan(bpref, bcont, bzero, 1.0, ALU.mult, ALU.add)
            settle()
            dve.wait_ge(consts_in, 16 * 13)
            v.tensor_tensor(bback, bp[:, 3], bown, ALU.mult)
            v.tensor_scalar(bgo, bp[:, 3], -1.0, 1.0, ALU.mult, ALU.add)
            settle()
            v.tensor_tensor_scan(bp[:, 5, ::-1], bgo[:, ::-1], bback[:, ::-1], 0.0, ALU.mult, ALU.add)
            v.tensor_tensor_scan(blast[:, ::-1], bgo[:, ::-1], bzero, 1.0, ALU.mult, ALU.add)
            settle()
            v.tensor_copy(bmask[:, 0], bcont)
            settle()
            v.memset(bmask[:, 0, 0:1], 0.0)
            v.tensor_copy(bmask[:, 1], bpref).then_inc(ends_scanned, 1)
            dve.wait_ge(ends_turned, 1)
            v.tensor_copy(brow[0:1, 0, 0:ROWS], bank[6][0:1, 0:ROWS])
            v.tensor_copy(brow[0:1, 1, 0:ROWS], bank[6][0:1, 128:128 + ROWS])
            v.tensor_copy(brow[0:1, 3, 0:ROWS], bank[6][0:1, 256:256 + ROWS])
            v.tensor_copy(brow[0:1, 4, 0:ROWS], bank[6][0:1, 384:384 + ROWS])
            settle()
            v.tensor_tensor_scan(brow[0:1, 5, 0:ROWS][:, ::-1], brow[0:1, 4, 0:ROWS][:, ::-1], brow[0:1, 3, 0:ROWS][:, ::-1], 0.0,
                                 ALU.mult, ALU.add)
            v.tensor_tensor_scan(brow[0:1, 2, 1:ROWS + 1], brow[0:1, 1, 0:ROWS], brow[0:1, 0, 0:ROWS], 0.0,
                                 ALU.mult, ALU.add).then_inc(ends_summed, 1)
            dve.wait_ge(carry_out, 1)
            v.tensor_copy(bcarry[:, :], bank[6][0:ROWS, 256:258])
            settle()
            v.scalar_tensor_tensor(bp[:, 5], blast, bcarry[:, 1:2], bp[:, 5], ALU.mult, ALU.add)
            v.scalar_tensor_tensor(bp[:, 2], bpref, bcarry[:, 0:1], bsum, ALU.mult, ALU.add).then_inc(planes_set, 1)

            dve.wait_ge(planes_in, 16 * BLOCKS)
            v.transpose(raw, planes[:, 0:PLANES * BLOCK])
            settle()
            for h in range(2):
                v.tensor_copy(scal[:, :, :, TILES * h:TILES * (h + 1)].rearrange("p k c t -> p k t c"),
                              raw.rearrange("p (k t c) -> p k t c", k=PLANES, t=TILES)[:, :, :, h:CHUNKS:2])
            settle()
            v.tensor_scalar(tm[:, 0], degree, 1.0, None, ALU.add)
            v.tensor_scalar(tm[:, 1], degree, 0.0, None, ALU.is_gt)
            v.tensor_scalar(ta[:, 1], degree, TINY, None, ALU.max)
            v.tensor_copy(i_home[:, :, :], home)
            v.tensor_copy(trow[:, :, :, 2], own)
            v.tensor_copy(i_src[:, :, :], srcs)
            v.tensor_copy(i_dst[:, :, :], dsts)
            v.tensor_scalar(minus[:, :, :], ends, -1.0, None, ALU.mult)
            v.tensor_scalar(tb[:, 0], dsts, float(-NOWHERE), None, ALU.add)
            v.tensor_scalar(tb[:, 1], dsts, float(AUG // 4), float(D // 4 - NOWHERE), ALU.mult, ALU.add)
            settle()
            v.tensor_scalar(ta[:, 0], tm[:, 0], TINY, None, ALU.max)
            v.tensor_tensor(tb[:, 0], tb[:, 0], ends, ALU.mult)
            v.tensor_tensor(tb[:, 1], tb[:, 1], ends, ALU.mult)
            settle()
            v.tensor_scalar(tm[:, 0], tm[:, 0], 0.0, None, ALU.is_gt)
            v.tensor_scalar(i_out[:, :, :], tb[:, 0], float(NOWHERE), None, ALU.add)
            v.tensor_scalar(i_aug[:, :, :], tb[:, 1], float(NOWHERE), None, ALU.add).then_inc(roots_in, 1)
            dve.wait_ge(roots_out, 1)
            v.reciprocal(tb, tb)
            settle()
            v.tensor_tensor(dinv[:, :, :], tb[:, 0], tm[:, 0], ALU.mult)
            v.tensor_tensor(dis[:, :, :], tb[:, 1], tm[:, 1], ALU.mult)
            settle()
            v.tensor_tensor(endinv[:, :, :], dinv[:, :, :], ends, ALU.mult)
            v.tensor_copy(trow[:, :, :, 0], dinv[:, :, :])
            v.tensor_copy(trow[:, :, :, 1], dis[:, :, :])
            settle()

            def stage_d(c, j):
                v.tensor_copy(idx[:, j, :], col(i_dst, c)).then_inc(staged["D"], 1)
            for c in range(RING):
                stage_d(c, c)

            def d_round(r):
                for j in range(RING):
                    c = RING * r + j
                    hold(dve, gathered["D"][j], GATHER * (r + 1))
                    v.tensor_copy(chunk(Z, c, D), slot[:, j, :, 0:D])
                    settle()
                    if not last(c + RING):
                        stage_d(c + RING, j)
            rounds(dve, d_round)

            def t_round(r):
                for j in range(RING):
                    c = RING * r + j
                    hold(dve, gathered["T"][j], GATHER * r)
                    v.tensor_copy(tslot[:, j], trow[:, at(c)].rearrange("p c t f -> p (c t) f"))
                    v.tensor_copy(idx[:, j, :], col(i_aug, c)).then_inc(staged["T"], 1)
            rounds(dve, t_round)

            for k in range(6):
                w_ = over(wts[:, k], SH)
                v.tensor_tensor(bs[0:D] if k == 0 else bs2, cgs[:, k], w_, ALU.mult)
                settle()
                if k:
                    v.tensor_tensor(bs[0:D], bs[0:D], bs2, ALU.add)
                    settle()

            def flat(t):
                return t[:, :, :].rearrange("p t f -> p (t f)")

            def sum_in_blocks(c):
                v.transpose(fm, flat(msg))
                settle()
                v.tensor_tensor_scan(fs, two(cont, c), fm, 0.0, ALU.mult, ALU.add)
                settle()

            def sum_over_blocks(c):
                for q in range(BLOCKS):
                    v.tensor_copy(blk[:, q::BLOCKS], fs[32 * q:32 * q + 32, BLOCK - 1::BLOCK])
                settle()
                n = 2 * BLOCKS
                ends_ = through[:, c * n:(c + 1) * n] if isinstance(c, int) else through[:, bass.ds(c * n, n)]
                v.tensor_tensor_scan(run[:, 1:n + 1], ends_, blk[:, :], run[:, 0:1], ALU.mult, ALU.add)
                settle()
                for q in range(BLOCKS):
                    v.tensor_copy(carry[32 * q:32 * q + 32, :], run[:, q:n:BLOCKS])
                settle()
                v.tensor_copy(run[:, 0:1], run[:, n:n + 1])

            def sum_out(c):
                for h in range(2):
                    e = slice(h * BLOCK, (h + 1) * BLOCK)
                    v.scalar_tensor_tensor(fo[:, e], two(pref, c)[:, e], carry[:, h:h + 1], fs[:, e], ALU.mult, ALU.add)
                settle()
                v.transpose(flat(agg), fo)
                settle()

            def sum_runs(c):
                sum_in_blocks(c)
                sum_over_blocks(c)
                sum_out(c)

            def two(t, c):
                e = t[:, 2 * c:2 * c + 2] if isinstance(c, int) else t[:, bass.ds(2 * c, 2)]
                return e.rearrange("p c e -> p (c e)")

            v.memset(gr, 1.0)
            settle()
            dve.wait_ge(masks_in, 16 * (2 * BLOCKS + 1))

            def a_round(r):
                for j in range(RING):
                    c = RING * r + j
                    hold(dve, gathered["A"][j], GATHER * (r + 1))
                    s = slot[:, j]
                    v.tensor_tensor(sw[:, :], col(weight, c), s[:, :, D], ALU.mult)
                    v.tensor_tensor(col(norm2, c), col(weight, c), s[:, :, D + 1], ALU.mult)
                    v.tensor_copy(col(i_ptr, c), s[:, :, D + 2])
                    v.tensor_tensor(msg2[:, :, :], chunk(Z, c, D), over(col(endinv, c)), ALU.mult)
                    settle()
                    v.tensor_tensor(msg[:, :, :], s[:, :, 0:D], over(sw[:, :]), ALU.mult)
                    settle()
                    v.tensor_tensor(msg[:, :, :], msg[:, :, :], msg2[:, :, :], ALU.add).then_inc(used["A"], 1)
                    settle()
                    sum_runs(c)
                    v.tensor_tensor(msg2[:, :, :], agg[:, :, :], over(col(dinv, c)), ALU.mult)
                    settle()
                    v.tensor_copy(chunk(P, c), msg2[:, :, :])
                    hold(dve, gram_used, c)
                    v.tensor_copy(gr[:, 0, :, 0:D], msg2[:, :, :])
                    v.tensor_copy(gr[:, 1, :, 0:D], chunk(Z, c, D))
                    v.tensor_tensor(gl[:, 0], msg2[:, :, :], over(col(ends, c)), ALU.mult)
                    v.tensor_tensor(gl[:, 1], chunk(Z, c, D), over(col(minus, c)), ALU.mult).then_inc(gram_set, 1)
                    settle()
            rounds(dve, a_round)

            dve.wait_ge(gram_done, 1)
            v.tensor_copy(gram[:, :], G)
            v.tensor_copy(srep[:, :], G[:, D:D + 1].broadcast_to([32, 128])).then_inc(gram_read, 1)
            dve.wait_ge(mean_done, 1)
            v.tensor_scalar(st[:, 0], bank[6][:, 0:D], 1.0 / N, None, ALU.mult)
            v.tensor_tensor(vv[:, :], bank[6][0:32, 64:64 + D], wg[:, :], ALU.mult).then_inc(vv_set, 1)
            dve.wait_ge(square_done, 1)
            v.tensor_scalar(st[:, 1], bank[6][:, 128:128 + D], 1.0 / N, None, ALU.mult)
            settle()
            v.tensor_tensor(st[:, 2], st[:, 0], st[:, 0], ALU.mult)
            v.tensor_tensor(st[:, 6], st[:, 0], bgb[:, 0], ALU.add)
            settle()
            v.tensor_tensor(st[:, 3], st[:, 1], st[:, 2], ALU.subtract)
            v.tensor_tensor(st[:, 6], bgb[:, 0], st[:, 6], ALU.subtract)
            settle()
            v.tensor_scalar(st[:, 3], st[:, 3], 0.0, None, ALU.max)
            settle()
            v.drain().then_inc(spread_in, 1)
            dve.wait_ge(spread_out, 1)
            v.reciprocal(st[:, 5], st[:, 4])
            settle()
            v.tensor_tensor(st[:, 5], st[:, 5], bgb[:, 1], ALU.mult)
            settle()
            v.tensor_tensor(st[:, 6], st[:, 6], st[:, 5], ALU.mult)
            settle()
            v.tensor_tensor(st[:, 7], st[:, 6], bgb[:, 2], ALU.add)

            def tiled(row, n):
                return row.unsqueeze(1).broadcast_to([row.shape[0], n, D])
            settle()
            v.tensor_tensor(w2s[0:64, :].rearrange("p (n f) -> p n f", f=D), w2s[0:64, :].rearrange("p (n f) -> p n f", f=D), tiled(st[0:64, 5], 2), ALU.mult)
            v.tensor_copy(w2s[64:65, :].rearrange("p (n f) -> p n f", f=D), tiled(st[64:65, 7], 2))
            v.tensor_tensor(w4s[:, :].rearrange("p (n f) -> p n f", f=D), w4s[:, :].rearrange("p (n f) -> p n f", f=D), tiled(st[:, 5], 4), ALU.mult)
            v.tensor_copy(t16[0:1], tiled(st[0:1, 7], 16))
            v.memset(fx[64:128], 0.0)
            settle()
            v.memset(fx[64:65], 1.0)
            settle()
            v.memset(run[:, 0:1], 0.0).then_inc(bn_set, 1)

            def layer_norm(name, c, o, n=2 * PT):
                yn = y[:, 0:n]
                v.tensor_reduce(ysum[:, 0:n], yn, AX.X, ALU.add)
                settle()
                v.scalar_tensor_tensor(yc[:, 0:n], over(ysum[:, 0:n]), 1.0 / D, yn, ALU.mult, ALU.subtract)
                settle()
                v.tensor_tensor(yq[:, 0:n], yc[:, 0:n], yc[:, 0:n], ALU.mult)
                settle()
                v.tensor_reduce(yvar[:, 0:n], yq[:, 0:n], AX.X, ALU.add).then_inc(var_set[name], 1)
                hold(dve, std_set[name], c + 1)
                v.reciprocal(yr[:, 0:n], ystd[:, 0:n])
                settle()
                return v.scalar_tensor_tensor(o, yc[:, 0:n], -1.0, over(yr[:, 0:n]), ALU.mult, ALU.mult)

            def pairs(c):
                return Z[:, at(c)].rearrange("p c t (h f) -> p (c t h) f", f=D)

            yh = y[:, :, :].rearrange("p (t h) f -> p t h f", h=2)

            def b_round(r):
                for j in range(RING):
                    c = RING * r + j
                    for h in range(2):
                        hold(dve, bn_out, 2 * c + h + 1)
                        e = slice(h * PT, (h + 1) * PT)
                        v.scalar_tensor_tensor(y[:, e], bank[2 + h][:, 0:PT * D].rearrange("p (n f) -> p n f", f=D), 0.0, pairs(c)[:, e],
                                               ALU.max, ALU.add).then_inc(bn_used, 1)
                    settle()
                    layer_norm("B", c, pairs(c)).then_inc(stored["B"], 1)
                    settle()
            rounds(dve, b_round)

            def basis(name, c, j, n, xb_set, xb_used):
                def view(t):
                    return prod[:, t // 2 % 2, :, 0:D * n].rearrange("p k (f n) -> p k f n", n=n)

                def times(t):
                    for t in (t, t + 1):
                        hold(dve, xb_set, PT * c + t + 1)
                        v.tensor_tensor(view(t)[:, t % 2], bank[4 + t % 2][:, 0:D * n].rearrange("p (f n) -> p f n", n=n),
                                        ca[:, t, 0:n].unsqueeze(1).broadcast_to([128, D, n]), ALU.mult).then_inc(xb_used, 1)
                times(0)
                for t in range(0, PT, 2):
                    settle()
                    if t + 2 < PT:
                        times(t + 2)
                    v.tensor_reduce(msg[:, t:t + 2, :], view(t), AX.X, ALU.add)
                settle()

            def one_hot(c):
                hold(dve, types_in, 16 * (c + 1))
                hold(dve, q_set, 2 * c)
                for h in range(2):
                    op = v.tensor_scalar(oh[:, h].rearrange("k (t b r) -> k b t r", b=BLOCKS, r=32),
                                         types[:, h * CHUNK:(h + 1) * CHUNK].rearrange("k (b t r) -> k b t r", b=BLOCKS, r=32),
                                         relno[:, 0:1], None, ALU.is_equal)
                op.then_inc(types_read, 1)

            def dots(c):
                hold(dve, q_out, 2 * c + 2)
                v.tensor_tensor(yq[:, 0:PT], qs[:, :, Q1 - D:Q2 - D], qs[:, :, Q2 - D:CO - D], ALU.mult)
                settle()
                v.tensor_reduce(att[:, 2], yq[:, 0:PT], AX.X, ALU.add)
                settle()
                v.tensor_scalar(att[:, 0], att[:, 2], float(D ** -0.5), 0.0, ALU.mult, ALU.max).then_inc(dot_set, 1)

            one_hot(0)
            dots(0)
            v.memset(run[:, 0:1], 0.0)
            settle()

            def r_round(r):
                for j in range(RING):
                    c = RING * r + j
                    hold(dve, tanh_set, c + 1)
                    v.tensor_tensor(ca[:, :, :], qs[:, :, CO - D:], over(att[:, 1], BASES), ALU.mult).then_inc(q_used, 1)
                    settle()
                    if not last(c + 1):
                        one_hot(c + 1)
                    basis("R", c, j, BASES, xb_set_r, xb_used_r)
                    sum_runs(c)
                    v.tensor_tensor(agg[:, :, :], agg[:, :, :], cur[:, j], ALU.add)
                    v.tensor_copy(yh[:, :, 0], chunk(Z, c, 0, D))
                    settle()
                    v.scalar_tensor_tensor(yh[:, :, 1], agg[:, :, :], 0.0, chunk(Z, c, D), ALU.max, ALU.add)
                    settle()
                    if not last(c + 1):
                        dots(c + 1)
                    layer_norm("R", c, pairs(c)).then_inc(stored["R"], 1)
                    settle()
            rounds(dve, r_round)

            def groups(t):
                return t.rearrange("p (k f) -> p k f", f=D)

            def dense_first(k):
                hold(dve, d_prod, k + 1)
                v.scalar_tensor_tensor(dy[:, 0:512], bank[2][:, :], 0.0, dx[:, 0:512], ALU.max, ALU.add)
                v.scalar_tensor_tensor(dy[:, 512:1024], bank[3][:, :], 0.0, dx[:, 512:1024], ALU.max, ALU.add).then_inc(d_y, 1)
                settle()
                v.tensor_reduce(dsum[:, :], groups(dy), AX.X, ALU.add)
                settle()
                v.scalar_tensor_tensor(groups(dc), over(dsum[:, :]), 1.0 / D, groups(dy), ALU.mult, ALU.subtract).then_inc(d_c1, 1)

            def dense_spread1(k):
                hold(dve, d_q1, k + 1)
                v.tensor_reduce(dvar[:, :], groups(dq), AX.X, ALU.add).then_inc(d_v1, 1)

            def dense_norm1(k):
                hold(dve, d_s1, k + 1)
                v.reciprocal(dr[:, :], dstd[:, :])
                settle()
                v.scalar_tensor_tensor(groups(dy), groups(dc), -1.0, over(dr[:, :]), ALU.mult, ALU.mult).then_inc(d_x2, 1)

            def dense_second(k):
                hold(dve, d_relu, k + 1)
                v.scalar_tensor_tensor(dc, dq, 1.0, dy, ALU.min, ALU.add)
                settle()
                v.tensor_reduce(dsum[:, :], groups(dc), AX.X, ALU.add)
                settle()
                v.scalar_tensor_tensor(groups(dq), over(dsum[:, :]), 1.0 / D, groups(dc), ALU.mult, ALU.subtract).then_inc(d_c2, 1)

            def dense_spread2(k):
                hold(dve, d_q2, k + 1)
                v.tensor_reduce(dvar[:, :], groups(dy), AX.X, ALU.add).then_inc(d_v2, 1)

            def dense_norm2(k):
                hold(dve, d_s2, k + 1)
                v.reciprocal(dr[:, :], dstd[:, :])
                settle()
                hold(dve, d_out, 16 * k)
                v.scalar_tensor_tensor(groups(do_), groups(dq), -1.0, over(dr[:, :]), ALU.mult, ALU.mult).then_inc(d_set, 1)

            for name in ("O1", "O2", "O3"):
                v.memset(run[:, 0:1], 0.0)
                settle()

                def o_round(r, name=name):
                    for j in range(RING):
                        c = RING * r + j
                        k = (0 if name == "O1" else PAIRS) + c
                        dense = name != "O3"
                        if dense:
                            dense_first(k)
                        hold(dve, gathered[name][j], GATHER * (r + 1))
                        v.tensor_tensor(msg[:, :, :], slot[:, j, :, 0:D], over(col(norm2, c)), ALU.mult).then_inc(used[name], 1)
                        v.tensor_scalar(msg2[:, :, :], chunk(Z, c, D), 1.0 - ALPHA, None, ALU.mult)
                        if name == "O1":
                            v.tensor_scalar(yq[:, 0:PT], chunk(Z, c, 0, D), 1.0 - ALPHA, 0.0, ALU.mult, ALU.max)
                            settle()
                            v.tensor_scalar(chunk(P, c), yq[:, 0:PT], 1.0, None, ALU.min)
                        settle()
                        if dense:
                            dense_spread1(k)
                        sum_in_blocks(c)
                        if dense:
                            dense_norm1(k)
                        sum_over_blocks(c)
                        if dense:
                            dense_second(k)
                        sum_out(c)
                        v.tensor_tensor(agg[:, :, :], agg[:, :, :], over(col(dis, c)), ALU.mult)
                        if dense:
                            dense_spread2(k)
                        settle()
                        v.scalar_tensor_tensor(msg[:, :, :], agg[:, :, :], ALPHA, msg2[:, :, :], ALU.mult, ALU.add)
                        settle()
                        if name == "O3":
                            v.tensor_scalar(msg[:, :, :], msg[:, :, :], 0.0, 1.0, ALU.max, ALU.min)
                            v.tensor_tensor(yh[:, :, 0], chunk(Z, c, 0, D), chunk(P, c), ALU.add)
                            settle()
                            v.tensor_tensor(yh[:, :, 1], chunk(Z, c, D), msg[:, :, :], ALU.add)
                            settle()
                            layer_norm(name, c, pairs(c)).then_inc(stored[name], 1)
                        else:
                            if not (isinstance(c, int) and c == 0):
                                hold(dve, tabled[name][(j - 1) % RING], 16 * (r + j))
                            v.tensor_scalar(ob[:, :, :], msg[:, :, :], 0.0, 1.0, ALU.max, ALU.min).then_inc(stored[name], 1)
                            dense_norm2(k)
                        settle()
                rounds(dve, o_round)

            v.memset(run[:, 0:1], 0.0)

            def h_round(r):
                for j in range(RING):
                    c = RING * r + j
                    v.tensor_copy(ca[:, :, 0:SH], scal[:, 6:PLANES, at(c)].rearrange("p k c t -> p (c t) k"))
                    settle()
                    basis("H", c, j, SH, xb_set_h, xb_used_h)
                    sum_runs(c)
                    v.tensor_tensor(y[:, 0:PT], agg[:, :, :], chunk(Z, c, D), ALU.add)
                    if not (isinstance(c, int) and c < RING):
                        hold(dve, scattered[j], GATHER * r)
                    v.tensor_copy(oidx[:, j, :], col(i_out, c))
                    settle()
                    layer_norm("H", c, oslot[:, j], PT).then_inc(rows_set, 1)
                    settle()
            rounds(dve, h_round)

        @block.tensor
        def _(pe):
            t_ = nc.tensor
            pe.wait_ge(consts_in, 16 * 13)
            pe.wait_ge(cleared, 1)
            t_.matmul(G, zer[:, 0:32], zer[:, 0:D + 1], start=True, stop=False)
            pe.wait_ge(ends_scanned, 1)
            t_.transpose(bank[6][0:1, 0:ROWS], bsum[:, BLOCK - 1:BLOCK], idn[0:ROWS, 0:ROWS])
            t_.transpose(bank[6][0:1, 128:128 + ROWS], bpref[:, BLOCK - 1:BLOCK], idn[0:ROWS, 0:ROWS])
            t_.transpose(bank[6][0:1, 256:256 + ROWS], bp[:, 5, 0:1], idn[0:ROWS, 0:ROWS])
            t_.transpose(bank[6][0:1, 384:384 + ROWS], blast[:, 0:1], idn[0:ROWS, 0:ROWS]).then_inc(ends_turned, 1)
            pe.wait_ge(ends_summed, 1)
            t_.matmul(bank[6][0:ROWS, 256:257], brow[0:1, 2, 0:ROWS], ones[0:1, 0:1], start=True, stop=True)
            t_.matmul(bank[6][0:ROWS, 257:258], brow[0:1, 5, 1:ROWS + 1], ones[0:1, 0:1], start=True, stop=True).then_inc(carry_out, 1)

            def stat(k, q, parts):
                hold(pe, sta_set, k + 1)
                for i in range(STATK):
                    op = t_.matmul(G, sta[0:parts, q, i, 0:D], sta[0:parts, q, i, 0:D + 1], start=False, stop=False)
                op.then_inc(sta_free, 1)
            with pe.Fori(0, (STATS - 1) // 2) as r:
                for q in range(2):
                    stat(2 * r + q, q, 128)
            for k in range(STATS - 1, STATS + 1):
                stat(k, k % 2, 128 if k < STATS else LEFT)

            def a_round(r):
                for j in range(RING):
                    c = RING * r + j
                    hold(pe, gram_set, c + 1)
                    for q in range(2):
                        for t in range(PT):
                            end = isinstance(c, int) and c == PAIRS - 1 and q == 1 and t == PT - 1
                            op = t_.matmul(G, gl[:, q, t, :], gr[:, q, t, :], start=False, stop=end)
                    op.then_inc(gram_used, 1)
            rounds(pe, a_round)
            t_.drain().then_inc(gram_done, 1)
            pe.wait_ge(gram_read, 1)
            t_.matmul(bank[6][:, 0:D], srep[:, :], wg[:, :], start=True, stop=True)
            t_.matmul(bank[6][0:32, 64:64 + D], gram[:, 0:D], wg[:, :], start=True, stop=True).then_inc(mean_done, 1)
            pe.wait_ge(vv_set, 1)
            t_.matmul(bank[6][:, 128:128 + D], ones[0:32, :], vv[:, :], start=True, stop=True).then_inc(square_done, 1)

            def turn(name, rows, h, k):
                for t in range(TILES):
                    b = turns[h][t // 4]
                    op = t_.transpose(b[0:k, 128 * (t % 4):128 * (t % 4) + 128], rows[:, TILES * h + t, 0:k], idn[:, :])
                op.then_inc(turned[name], 1)

            pe.wait_ge(bn_set, 1)

            def b_round(r):
                for j in range(RING):
                    c = RING * r + j
                    hold(pe, pz_set, c + 1)
                    for h in range(2):
                        hold(pe, fx_set["B"], 2 * c + h - 1, pe_passed)
                        turn("B", pz, h, 2 * D)
                    for h in range(2):
                        hold(pe, fx_set["B"], 2 * c + h + 1)
                        hold(pe, bn_used, 2 * c + h - 1)
                        for t in range(TILES):
                            op = t_.matmul(bank[2 + h][:, 2 * D * t:2 * D * (t + 1)], fx[:, h, 128 * t:128 * (t + 1)], w2s[:, :],
                                           start=True, stop=True)
                        op.then_inc(bn_out, 1)
            rounds(pe, b_round)

            def product(c, t, rhs, n, xb_set, xb_used):
                hold(pe, xb_used, PT * c + t - 1)
                t_.matmul(bank[4 + t % 2][:, 0:n], fx[:, t // TILES, 128 * (t % TILES):128 * (t % TILES + 1)], rhs,
                          start=True, stop=True).then_inc(xb_set, 1)

            def turn_r(c, r, j, h):
                hold(pe, gathered["R"][j], 2 * GATHER * (r + 1), pe_passed)
                hold(pe, fx_set["R"], 2 * c + h - 1, pe_passed)
                turn("R", slot[:, j], h, 2 * D)

            def attend(c, h, t):
                if t == 0:
                    hold(pe, fx_set["R"], 2 * c + h + 1)
                    hold(pe, q_out, 2 * c + h)
                    hold(pe, types_read, c + 1)
                b = bank[2] if t < 4 else bank[3]
                o = QW * (t % 4)
                t_.matmul(b[:, o:o + QW], fx[:, h, 128 * t:128 * (t + 1)], wqs[:, :], start=True, stop=False)
                op = t_.matmul(b[:, o + Q2:o + QW], oh[:, h, 128 * t:128 * (t + 1)], relcs[:, :], start=False, stop=True)
                if t == TILES - 1:
                    op.then_inc(q_set, 1)
            for h in range(2):
                turn_r(0, 0, 0, h)
            for h in range(2):
                for t in range(TILES):
                    attend(0, h, t)

            def r_round(r):
                for j in range(RING):
                    c = RING * r + j
                    for t in range(TILES):
                        product(c, t, wcs[:, :], D * BASES, xb_set_r, xb_used_r)
                    if not last(c + 1):
                        for h in range(2):
                            turn_r(c + 1, r + (j + 1) // RING, (j + 1) % RING, h)
                    for t in range(TILES):
                        product(c, TILES + t, wcs[:, :], D * BASES, xb_set_r, xb_used_r)
                        if not last(c + 1):
                            attend(c + 1, 0, t)
                    if not last(c + 1):
                        for t in range(TILES):
                            attend(c + 1, 1, t)
            rounds(pe, r_round)

            def dense(k):
                hold(pe, d_in, 16 * (k + 1))
                hold(pe, d_xt, k)
                for g in range(8):
                    op = t_.transpose(bank[g // 4][:, 128 * (g % 4):128 * (g % 4 + 1)], dx[:, 128 * g:128 * (g + 1)], idn[:, :])
                op.then_inc(d_turned, 1)
                hold(pe, d_xt, k + 1)
                hold(pe, d_y, k)
                for h in range(2):
                    t_.matmul(bank[2 + h][:, :], ones[0:1, :], t16[0:1].rearrange("p n f -> p (n f)"), start=True, stop=False)
                for g in range(8):
                    op = t_.matmul(bank[2 + g // 4][:, 128 * (g % 4):128 * (g % 4 + 1)], dxt[:, 128 * g:128 * (g + 1)], w4s[:, :],
                                   start=False, stop=g % 4 == 3)
                op.then_inc(d_prod, 1)

            for first in (0, PAIRS):
                def o_round(r, first=first):
                    for j in range(RING):
                        dense(first + RING * r + j)
                rounds(pe, o_round)

            def turn_h(c, r, j, h):
                hold(pe, gathered["H"][j], GATHER * (r + 1))
                hold(pe, fx_set["H"], 2 * c + h - 1)
                turn("H", slot[:, j], h, D)
            for h in range(2):
                turn_h(0, 0, 0, h)

            def h_round(r):
                for j in range(RING):
                    c = RING * r + j
                    for h in range(2):
                        hold(pe, fx_set["H"], 2 * c + h + 1)
                        for t in range(TILES * h, TILES * (h + 1)):
                            product(c, t, bs[:, :, :].rearrange("p f n -> p (f n)"), D * SH, xb_set_h, xb_used_h)
                    if not last(c + 1):
                        for h in range(2):
                            turn_h(c + 1, r + (j + 1) // RING, (j + 1) % RING, h)
            rounds(pe, h_round)


def coupling():
    import math
    import numpy as np
    combos = [(0, 0, 0), (0, 1, 1), (1, 0, 1), (1, 1, 0), (1, 1, 1), (2, 1, 1)]

    def coefficient(j1, m1, j2, m2, j3, m3):
        f = math.factorial
        lo, hi = max(0, j2 - j3 - m1, j1 + m2 - j3), min(j1 + j2 - j3, j1 - m1, j2 + m2)
        pref = (2 * j3 + 1) * f(j3 + j1 - j2) * f(j3 - j1 + j2) * f(j1 + j2 - j3) / f(j1 + j2 + j3 + 1)
        pref *= f(j3 + m3) * f(j3 - m3) * f(j1 - m1) * f(j1 + m1) * f(j2 - m2) * f(j2 + m2)
        return math.sqrt(pref) * sum((-1) ** v / (f(v) * f(j1 + j2 - j3 - v) * f(j1 - m1 - v) * f(j2 + m2 - v) * f(j3 - j2 + m1 + v)
                                                  * f(j3 - j1 - m2 + v)) for v in range(lo, hi + 1))

    def basis(l):
        q = np.zeros((2 * l + 1, 2 * l + 1), complex)
        for m in range(-l, 0):
            q[l + m, l - m], q[l + m, l + m] = 2 ** -0.5, -1j * 2 ** -0.5
        q[l, l] = 1
        for m in range(1, l + 1):
            q[l + m, l + m], q[l + m, l - m] = (-1) ** m * 2 ** -0.5, 1j * (-1) ** m * 2 ** -0.5
        return (-1j) ** l * q

    table = np.zeros((6, D, D, SH), np.float32)
    for n, (l1, l2, l3) in enumerate(combos):
        c = np.zeros((2 * l1 + 1, 2 * l2 + 1, 2 * l3 + 1), complex)
        for m1 in range(-l1, l1 + 1):
            for m2 in range(-l2, l2 + 1):
                if abs(m1 + m2) <= l3:
                    c[m1 + l1, m2 + l2, m1 + m2 + l3] = coefficient(l1, m1, l2, m2, l3, m1 + m2)
        c = np.einsum("ij,kl,mn,ikn->jlm", basis(l1), basis(l2), np.conj(basis(l3)).T, c).real
        c /= np.linalg.norm(c)
        for m in range(8):
            for j in range(2 * l2 + 1):
                for o in range(8):
                    for k in range(2 * l3 + 1):
                        table[n, m if l2 == 0 else 8 + 3 * m + j, o if l3 == 0 else 8 + 3 * o + k, l1 * l1:(l1 + 1) ** 2] = c[:, j, k]
    return table


def kernel(**inputs):
    import numpy as np
    import concourse.bacc as bacc
    from concourse.bass_utils import run_bass_kernel_spmd as run

    a = {k: np.asarray(v) for k, v in inputs.items()}
    w = a["L0_gnn_W"]
    w2, w4 = np.zeros((128, 64), np.float32), np.zeros((128, 128), np.float32)
    for k in range(4):
        w4[32 * k:32 * k + 32, 32 * k:32 * k + 32] = w
    w2[0:64] = w4[0:64, 0:64]
    wq = np.zeros((128, QW), np.float32)
    wq[0:32, CUR:CUR + D] = a["L1_gnn_self_loop_weight"]
    wq[0:32, Q1:Q1 + D] = a["L1_gnn_A1_w"].T
    wq[64, Q1:Q1 + D] = a["L1_gnn_A1_b"]
    wq[32:64, Q2:Q2 + D] = a["L1_gnn_A2_w"].T
    wq[64, Q2:Q2 + D] = a["L1_gnn_A2_b"]
    relc, wcat = np.zeros((128, D + BASES), np.float32), np.zeros((128, D * BASES), np.float32)
    relc[0:RELS, 0:D], relc[0:RELS, D:] = a["L1_gnn_rel_emb"], a["L1_gnn_w_comp"]
    wcat[0:D] = a["L1_gnn_weight"].transpose(1, 2, 0).reshape(D, D * BASES)
    channel = np.array([i if i < 8 else (i - 8) // 3 for i in range(D)])
    wt = a["L3_gnn_W"][:, channel][:, :, channel].transpose(1, 0, 2)
    cg = coupling().transpose(1, 0, 2, 3)
    p, c, t = np.meshgrid(np.arange(128), np.arange(PAIRS), np.arange(PT), indexing="ij")
    own = (PAIR * c + PT * p + t).astype(np.float32)
    k, t, lane = (v.reshape(-1) for v in np.meshgrid(np.arange(ROWS), np.arange(TILES), np.arange(32), indexing="ij"))
    c, partition = k // BLOCKS, 32 * (k % BLOCKS) + lane
    own_blocks = (PAIR * (c // 2) + PT * partition + TILES * (c % 2) + t).astype(np.float32).reshape(ROWS, BLOCK)
    ins = {
        "x": a["x"], "src": a["src"], "dst": a["dst"], "attr3": a["edge_attr_3"].reshape(-1), "attr5": a["edge_attr_5"].reshape(-1),
        "etype": a["edge_type_86"], "ew": a["edge_weight"], "ew1": a["edge_weight1"].reshape(-1),
        "bgb_in": np.stack([a["L0_gnn_b"], a["L0_gnn_gamma"], a["L0_gnn_beta"]]), "w_gcn": w, "w2": w2, "w4": w4, "wq": wq,
        "relc": relc, "wcat": wcat, "cg": cg, "wt": wt, "ident": np.eye(128, dtype=np.float32), "own_in": own, "own_blocks": own_blocks,
        "relno_in": np.arange(128, dtype=np.float32)[:, None],
    }
    nc = bacc.Bacc("TRN2", target_bir_lowering=False, num_devices=1)
    aps = {}
    for name, v in ins.items():
        ins[name] = v = np.ascontiguousarray(v)
        aps[name] = nc.dram_tensor(name, v.shape, mybir.dt.from_np(v.dtype), kind="ExternalInput").ap()
    for name, shape, dt in (("aug", (N, AUG), mybir.dt.float32), ("plane", (PLANES, ROWS * BLOCK), mybir.dt.float32),
                            ("mask", (2, ROWS * BLOCK), mybir.dt.bfloat16),
                            *((f"tab_{k}", (ROWS * BLOCK, D), mybir.dt.float32) for k in ("b", "r", "o1", "o2", "o3"))):
        aps[name] = nc.dram_tensor(name, shape, dt, kind="Internal").ap()
    aps["out"] = nc.dram_tensor("out", (N, D), mybir.dt.float32, kind="ExternalOutput").ap()
    build(nc, **aps)
    return run(nc, [ins], core_ids=[0]).results[0]["out"]
```

```python
from contextlib import ExitStack

import concourse.bass as bass
from concourse import mybir

N, E, D = 100000, 25000, 32
BLOCKS, TILES = 4, 7
BLOCK = TILES * 32
CHUNK = BLOCKS * BLOCK
CHUNKS = -(-E // CHUNK)
PAIRS = CHUNKS // 2
PT = 2 * TILES
PAIR = 2 * CHUNK
RING = 2
ROUNDS = PAIRS // RING
ROWS = CHUNKS * BLOCKS
FULL = E // BLOCK
TAIL = E - FULL * BLOCK
FAR = 2 * N
NOWHERE = 1 << 22
AUG = 36
BASES, RELS = 16, 86
SH = 9
PLANES = 6 + SH
STATK = 25
STATS = N // (128 * STATK)
LEFT = (N - STATS * 128 * STATK) // STATK
DK = 20
DW = DK * D
DALONE = {"O1": 2, "O2": 2, "O3": 1}
DFIRST = {"O1": 0, "O2": DALONE["O1"] + PAIRS, "O3": DALONE["O1"] + DALONE["O2"] + 2 * PAIRS}
DSTEPS = DFIRST["O3"] + DALONE["O3"] + ROUNDS
DSTRIDE = (N - 128 * DK) // (DSTEPS - 1)
DSHIFT = N - 128 * DK - (DSTEPS - 1) * DSTRIDE
WIDE = 7 * D * SH + 18 * BLOCK
assert DSTRIDE + DSHIFT <= 128 * DK and 5 * DW <= WIDE and DW <= RING * PT * D and DW > 512 and CHUNKS == 2 * RING * ROUNDS and LEFT * STATK == N - STATS * 128 * STATK
EPS = 1e-5
ALPHA = 0.9
TINY = 1.2e-38
GATHER = 16 * PT
CUR, Q1, Q2, CO, QW = 0, 32, 64, 96, 112


def at(n):
    return slice(n, n + 1) if isinstance(n, int) else bass.ds(n, 1)


def whole(t):
    return t[tuple([slice(None)] * len(t.shape))]


def build(nc, x, src, dst, attr3, attr5, etype, ew, ew1, bgb_in, w_gcn, w2, w4, wq, relc, wcat, cg, wt,
          ident, own_in, own_blocks, relno_in, aug, plane, mask, tab_b, tab_r, tab_o1, tab_o2, tab_o3, out):
    fp32, bf16, i32 = mybir.dt.float32, mybir.dt.bfloat16, mybir.dt.int32
    ALU, ACT, AX = mybir.AluOpType, mybir.ActivationFunctionType, mybir.AxisListType
    ctx = ExitStack()
    with ctx:
        def sb(name, shape, dt=fp32):
            return ctx.enter_context(nc.sbuf_tensor(name, shape, dt))

        def sem(name):
            return ctx.enter_context(nc.semaphore(name))

        Z = sb("Z", [128, PAIRS, PT, 2 * D])
        P = sb("P", [128, PAIRS, PT, D])
        slot = sb("slot", [128, RING, PT, 2 * D])
        idx = sb("idx", [128, RING, PT], i32)
        oslot = sb("oslot", [128, RING, PT, D])
        oidx = sb("oidx", [128, RING, PT], i32)
        cont = sb("cont", [128, CHUNKS, BLOCK], bf16)
        pref = sb("pref", [128, CHUNKS, BLOCK], bf16)
        through = sb("through", [32, ROWS], bf16)
        scal = sb("scal", [128, PLANES, PAIRS, PT])
        srcs, dsts, degree, ends, weight, home = (scal[:, k] for k in range(6))
        dinv = sb("dinv", [128, PAIRS, PT])
        dis = sb("dis", [128, PAIRS, PT])
        endinv = sb("endinv", [128, PAIRS, PT])
        minus = sb("minus", [128, PAIRS, PT])
        norm2 = sb("norm2", [128, PAIRS, PT])
        i_src = sb("i_src", [128, PAIRS, PT], i32)
        i_dst = sb("i_dst", [128, PAIRS, PT], i32)
        i_aug = sb("i_aug", [128, PAIRS, PT], i32)
        i_out = sb("i_out", [128, PAIRS, PT], i32)
        i_ptr = sb("i_ptr", [128, PAIRS, PT], i32)
        i_home = sb("i_home", [128, PAIRS, PT], i32)
        idx2 = sb("idx2", [128, RING, PT], i32)
        trow = sb("trow", [128, PAIRS, PT, 4])
        tslot = sb("tslot", [128, RING, PT, 4])
        planes = Z[:, :, :, :].rearrange("p c t f -> p (c t f)")
        natural = planes[:, 0:PLANES * BLOCK].rearrange("p (k e) -> p k e", e=BLOCK)
        bp = planes[0:ROWS, PLANES * BLOCK:2 * PLANES * BLOCK].rearrange("p (k e) -> p k e", e=BLOCK)
        raw = planes[:, 2 * PLANES * BLOCK:3 * PLANES * BLOCK]
        left = planes[:, 3 * PLANES * BLOCK:3 * PLANES * BLOCK + 7 * PAIRS * PT].rearrange("p (k c t) -> p k c t", k=7, t=PT)
        ta, tb, tm, own = left[:, 0:2], left[:, 2:4], left[:, 4:6], left[:, 6]
        wide = sb("wide", [128, WIDE])
        dxt, dy, dc, dq, do_ = (wide[:, k * DW:(k + 1) * DW] for k in range(5))
        dx = oslot[:, :, :, :].rearrange("p j t f -> p (j t f)")[:, 0:DW]
        cgs = wide[0:D, 0:6 * D * SH].rearrange("p (k f n) -> p k f n", k=6, f=D)
        bs2 = wide[0:D, 6 * D * SH:7 * D * SH].rearrange("p (f n) -> p f n", n=SH)
        by_rows = wide[0:ROWS, 7 * D * SH:]
        raw3, raw5 = by_rows[:, 0:3 * BLOCK], by_rows[:, 3 * BLOCK:8 * BLOCK]
        bcont, bpref, bsum, bzero = (by_rows[:, k * BLOCK:(k + 1) * BLOCK] for k in range(8, 12))
        bdst, bprev, bnext, bsrc = (by_rows[:, k * BLOCK:(k + 1) * BLOCK].bitcast(i32) for k in range(12, 16))
        bmask = by_rows[:, 16 * BLOCK:17 * BLOCK].bitcast(bf16).rearrange("p (k e) -> p k e", k=2)
        bown = by_rows[:, 17 * BLOCK:18 * BLOCK]
        bgo, bback, blast = (raw3[:, k * BLOCK:(k + 1) * BLOCK] for k in range(3))
        gl = wide[:, 0:2 * PT * D].rearrange("p (q t f) -> p q t f", q=2, t=PT)
        gr = wide[:, 2 * PT * D:2 * PT * (2 * D + 1)].rearrange("p (q t f) -> p q t f", q=2, t=PT)
        oh = wide[:, 0:PAIR].rearrange("p (h e) -> p h e", h=2)
        types = wide[:, PAIR:2 * PAIR].bitcast(i32)
        prod = wide[:, 2 * PAIR:2 * PAIR + 4 * D * BASES].rearrange("p (q k n) -> p q k n", q=2, k=2)
        wide2 = sb("wide2", [128, PAIR + PT * (QW + D)])
        stx = wide2[:, 0:2 * STATK * D].rearrange("p (q k f) -> p q k f", q=2, f=D)
        sta = wide2[:, 2 * STATK * D:2 * STATK * (D + AUG)].rearrange("p (q k f) -> p q k f", q=2, f=AUG)
        fx = wide2[:, 0:PAIR].rearrange("p (q e) -> p q e", q=2)
        pz = wide2[:, PAIR:PAIR + PT * 2 * D].rearrange("p (t f) -> p t f", f=2 * D)
        cur = wide2[:, PAIR:PAIR + 2 * PT * D].rearrange("p (q t f) -> p q t f", q=2, f=D)
        qs = wide2[:, PAIR + 2 * PT * D:PAIR + PT * (QW + D)].rearrange("p (t f) -> p t f", f=QW - D)
        brow = sb("brow", [1, 6, ROWS + 1])
        bcarry = sb("bcarry", [ROWS, 2])
        msg, msg2 = (sb(n, [128, PT, D]) for n in ("msg", "msg2"))
        agg = msg
        turned_ = sb("turned_", [128, 2, 2 * BLOCK])
        fm, fs = turned_[:, 0], turned_[:, 1]
        fo = fm
        yq = turned_[:, :, :].rearrange("p q (t f) -> p (q t) f", f=D)
        blk = sb("blk", [32, 2 * BLOCKS])
        run = sb("run", [32, 2 * BLOCKS + 1])
        carry = sb("carry", [128, 2])
        y, yc = (sb(n, [128, 2 * PT, D]) for n in ("y", "yc"))
        yh = y[:, :, :].rearrange("p (t h) f -> p t h f", h=2)
        ysum, yvar, ystd, yr = (sb(n, [128, 2 * PT]) for n in ("ysum", "yvar", "ystd", "yr"))
        sw = sb("sw", [128, PT])
        ob = sb("ob", [128, PT, D])
        ca = sb("ca", [128, PT, BASES])
        att = sb("att", [128, 3, PT])
        eps = sb("eps", [128, 2])
        dsum, dvar, dstd, dr = (sb(n, [128, DK]) for n in ("dsum", "dvar", "dstd", "dr"))
        idn = sb("idn", [128, 128])
        zer = sb("zer", [128, D + 1])
        ones = sb("ones", [128, 128])
        gram = sb("gram", [32, D + 1])
        wg, vv = sb("wg", [32, D]), sb("vv", [32, D])
        srep = sb("srep", [32, 128])
        bgb = sb("bgb", [128, 3, D])
        st = sb("st", [128, 8, D])
        w2s = sb("w2s", [128, 2 * D])
        w4s = sb("w4s", [128, 128])
        t16 = sb("t16", [1, 16, D])
        wqs = sb("wqs", [128, QW])
        relcs = sb("relcs", [128, D + BASES])
        wcs = sb("wcs", [128, D * BASES])
        relno = sb("relno", [128, 1])
        wts = sb("wts", [32, 6, D])
        bs = sb("bs", [128, D, SH])
        bank = [ctx.enter_context(nc.psum_tensor(f"bank{i}", [128, 512], fp32)) for i in range(8)]
        G = bank[7][0:32, 0:D + 1]

        (padded, first_in, cleared, blocks_in, consts_in, planes_set, planes_out, planes_in, masks_in, ends_scanned, ends_turned,
         ends_summed, carry_out, roots_in, roots_out, sta_set, sta_free) = (sem(n) for n in (
             "padded first_in cleared blocks_in consts_in planes_set planes_out planes_in masks_in ends_scanned ends_turned "
             "ends_summed carry_out roots_in roots_out sta_set sta_free").split())
        stx_in = [sem(f"stx_in{q}") for q in range(2)]
        aug_out = [sem(f"aug_out{q}") for q in range(2)]
        (gram_done, gram_read, mean_done, vv_set, square_done, spread_in, spread_out, bn_set) = (sem(n) for n in (
            "gram_done gram_read mean_done vv_set square_done spread_in spread_out bn_set").split())
        def each(what, passes):
            return {n: sem(f"{what}_{n}") for n in passes.split()}

        staged = each("staged", "D T A R O1 O2 O3 H")
        used = each("used", "A O1 O2 O3")
        stored = each("stored", "B R O1 O2 O3")
        turned = each("turned", "B R H")
        fx_set = each("fx_set", "B R H")
        centered = each("centered", "B R O3 H")
        squared = each("squared", "B R O3 H")
        var_set = each("var_set", "B R O3 H")
        std_set = each("std_set", "B R O3 H")
        gathered = {n: [sem(f"gathered_{n}{j}") for j in range(RING)] for n in "D T A R O1 O2 O3 H".split()}
        scattered = [sem(f"scattered{j}") for j in range(RING)]
        tabled = {n: [sem(f"tabled_{n}{j}") for j in range(RING)] for n in "B R O1 O2 O3".split()}
        (copied_a, gram_set, gram_used, pz_set, bn_out, bn_used, types_in, types_read, types_set, q_set, q_out, q_used, source_set, chain_set, dot_set, tanh_set,
         xb_set_r, xb_used_r, xb_set_h, xb_used_h, rows_set) = (sem(n) for n in (
             "copied_a gram_set gram_used pz_set bn_out bn_used types_in types_read types_set q_set q_out q_used source_set chain_set dot_set tanh_set "
             "xb_set_r xb_used_r xb_set_h xb_used_h rows_set").split())
        pool_passed, pe_passed = sem("pool_passed"), sem("pe_passed")
        (d_in, d_turned, d_xt, d_prod, d_y, d_c1, d_q1, d_v1, d_s1, d_x2, d_relu, d_c2, d_q2, d_v2, d_s2, d_set, d_out) = (
            sem(f"dense_{n}") for n in "in turned xt prod y c1 q1 v1 s1 x2 relu c2 q2 v2 s2 set out".split())
        block = ctx.enter_context(nc.Block())

        def rounds(eng, body):
            body(0)
            with eng.Fori(1, ROUNDS - 1) as r:
                body(r)
            body(ROUNDS - 1)

        def hold(eng, semaphore, value, passed=None):
            if isinstance(value, int):
                if value > 0:
                    eng.wait_ge(semaphore, value)
            else:
                eng.wait_ge(semaphore, value)
                if passed is not None:
                    eng.sem_inc(passed, 1)

        def dense_steps(name, c, r, j):
            if name == "O3":
                return (DFIRST[name] + DALONE[name] + r,) if j == 0 else ()
            return (DFIRST[name] + DALONE[name] + c,)

        def dense_alone(name):
            return range(DFIRST[name], DFIRST[name] + DALONE[name])

        def final(k):
            return isinstance(k, int) and k == DSTEPS - 1

        def last(c):
            return isinstance(c, int) and c >= PAIRS

        def col(t, c):
            return t[:, at(c)].rearrange("p c t -> p (c t)")

        def chunk(t, c, a=0, z=None):
            return t[:, at(c), :, a:z].rearrange("p c t f -> p (c t) f")

        def xb(t):
            return bank[(0, 1, 6, 7, 2, 3)[t] if t < 6 else 4 + t % 2]

        turns = ((bank[0], bank[1]), (bank[6], bank[7]))

        def over(v, n=D):
            return v.unsqueeze(2).broadcast_to([v.shape[0], v.shape[1], n])

        @block.sync
        def _(sp):
            with nc.allow_non_contiguous_dma("the first pairs' targets, an element each"):
                for k in range(2 * RING):
                    for q in range(BLOCKS):
                        n0 = k * CHUNK + q * BLOCK
                        by_lane = dst[n0:n0 + BLOCK].rearrange("(t r) -> r t", r=32)
                        sp.dma_start(idx[32 * q:32 * q + 32, k // 2, TILES * (k % 2):TILES * (k % 2 + 1)], by_lane).then_inc(first_in, 16)
            sp.wait_ge(padded, 1)
            sp.dma_start(bprev[0:1, 1:BLOCK], dst[0:BLOCK - 1].unsqueeze(0)).then_inc(blocks_in, 16)
            for t, a, lo, off, w in ((bdst, dst, 0, 0, 1), (bprev, dst, 1, -1, 1), (bnext, dst, 0, 1, 1), (bsrc, src, 0, 0, 1),
                                     (bp[:, 4], ew, 0, 0, 1), (bp[:, 6], ew1, 0, 0, 1), (raw3, attr3, 0, 0, 3), (raw5, attr5, 0, 0, 5)):
                k = BLOCK * w
                sp.dma_start(t[lo:FULL, :], a[lo * k + off:FULL * k + off].rearrange("(p k) -> p k", k=k)).then_inc(blocks_in, 16)
                sp.dma_start(t[FULL:FULL + 1, 0:TAIL * w - off], a[FULL * k + off:E * w].unsqueeze(0)).then_inc(blocks_in, 16)
            for t, a in ((idn, ident), (own, own_in), (bown, own_blocks), (relno, relno_in), (wg, w_gcn), (w2s, w2), (w4s, w4), (wqs, wq),
                         (relcs, relc), (wcs, wcat), (cgs, cg), (wts, wt), (bgb, bgb_in.unsqueeze(0).broadcast_to([128, 3, D]))):
                sp.dma_start(whole(t), a).then_inc(consts_in, 16)
            sp.wait_ge(planes_set, 1)
            sp.dma_start(plane.rearrange("k (p e) -> p k e", e=BLOCK), bp).then_inc(planes_out, 16)
            sp.dma_start(mask.rearrange("k (p e) -> p k e", e=BLOCK), bmask[:, :, :]).then_inc(planes_out, 16)
            sp.wait_ge(planes_out, 32)
            by_block = plane.rearrange("k (c b e) -> b c k e", b=BLOCKS, e=BLOCK)
            masks = mask.rearrange("k (c b e) -> k b c e", b=BLOCKS, e=BLOCK)
            for q in range(BLOCKS):
                sp.dma_start(natural[32 * q:32 * q + CHUNKS], by_block[q]).then_inc(planes_in, 16)
            for k, t in enumerate((cont, pref)):
                for q in range(BLOCKS):
                    sp.dma_start(t[32 * q:32 * q + 32], masks[k, q].unsqueeze(0).broadcast_to([32, CHUNKS, BLOCK])).then_inc(masks_in, 16)
            ends_row = mask.rearrange("k (p e) -> k e p", e=BLOCK)[1, BLOCK - 1]
            with nc.allow_non_contiguous_dma("one column of the blocks"):
                sp.dma_start(through[:, :], ends_row.unsqueeze(0).broadcast_to([32, ROWS])).then_inc(masks_in, 16)

            def load_stat(q, n0, parts):
                rows = x[n0:n0 + parts * STATK] if isinstance(n0, int) else x[bass.ds(n0, parts * STATK)]
                sp.dma_start(stx[0:parts, q], rows.rearrange("(p k) f -> p k f", k=STATK)).then_inc(stx_in[q], 16)

            def store_stat(q, n0, parts):
                rows = aug[n0:n0 + parts * STATK] if isinstance(n0, int) else aug[bass.ds(n0, parts * STATK)]
                sp.dma_start(rows.rearrange("(p k) f -> p k f", k=STATK), sta[0:parts, q]).then_inc(aug_out[q], 16)

            step = 128 * STATK
            load_stat(0, 0, 128)
            load_stat(1, step, 128)
            with sp.Fori(0, (STATS - 3) // 2) as r:
                for q in range(2):
                    k = 2 * r + q
                    hold(sp, sta_set, k + 1)
                    store_stat(q, k * step, 128)
                    load_stat(q, (k + 2) * step, 128)
            for k in range(STATS - 3, STATS + 1):
                sp.wait_ge(sta_set, k + 1)
                store_stat(k % 2, k * step, 128 if k < STATS else LEFT)
                if k + 2 <= STATS:
                    load_stat(k % 2, (k + 2) * step, 128 if k + 2 < STATS else LEFT)

            def store_table(name, table, c, j, rows):
                hold(sp, stored[name], c + 1)
                view = table.rearrange("(c p t) f -> c p t f", p=128, t=PT)[at(c)]
                sp.dma_start(view.rearrange("c p t f -> (c p) t f"), rows).then_inc(tabled[name][j], 16)

            def dense_rows(t, k):
                n = 128 * DK
                n0 = 0 if isinstance(k, int) and k == 0 else k * DSTRIDE + DSHIFT
                v = t[n0:n0 + n] if isinstance(k, int) else t[bass.ds(n0, n)]
                return v.rearrange("(p k) f -> p (k f)", k=DK)

            def dense_store(k):
                hold(sp, d_set, k + 1)
                sp.dma_start(dense_rows(out, k), do_).then_inc(d_out, 16)

            def dense_load(k):
                hold(sp, d_y, k)
                sp.dma_start(dx, dense_rows(x, k)).then_inc(d_in, 16)

            def b_round(r):
                for j in range(RING):
                    c = RING * r + j
                    store_table("B", tab_b, c, j, chunk(Z, c, D))
            rounds(sp, b_round)

            def load_types(c):
                n = min(PAIR, E - c * PAIR) if isinstance(c, int) else PAIR
                row = etype[c * PAIR:c * PAIR + n] if isinstance(c, int) else etype[bass.ds(c * PAIR, n)]
                hold(sp, types_read, c)
                sp.dma_start(types[:, 0:n], row.unsqueeze(0).broadcast_to([128, n])).then_inc(types_in, 16)

            def r_round(r):
                for j in range(RING):
                    c = RING * r + j
                    if not last(c + 1):
                        load_types(c + 1)
                    if not (isinstance(c, int) and c == 0):
                        store_table("R", tab_r, c - 1, (j - 1) % RING, chunk(Z, c - 1, D))
            load_types(0)
            dense_load(0)
            rounds(sp, r_round)
            store_table("R", tab_r, PAIRS - 1, (PAIRS - 1) % RING, chunk(Z, PAIRS - 1, D))
            for name, table in (("O1", tab_o1), ("O2", tab_o2), ("O3", tab_o3)):
                for k in dense_alone(name):
                    dense_load(k + 1)
                    dense_store(k)

                def o_round(r, name=name, table=table):
                    for j in range(RING):
                        c = RING * r + j
                        for k in dense_steps(name, c, r, j):
                            if not final(k):
                                dense_load(k + 1)
                        store_table(name, table, c, j, ob[:, :, :] if name != "O3" else chunk(Z, c, D))
                        for k in dense_steps(name, c, r, j):
                            dense_store(k)
                rounds(sp, o_round)
            sp.wait_ge(d_out, 16 * DSTEPS)

        @block.gpsimd
        def _(pool):
            def gather(name, table, rows, c, j, width=D):
                if name == "D":
                    if isinstance(c, int) and c < RING:
                        pool.wait_ge(first_in, 16 * 2 * RING * BLOCKS)
                        pool.wait_ge(padded, 1)
                    hold(pool, staged[name], c + 1 - RING, pool_passed)
                else:
                    hold(pool, staged[name], c + 1, pool_passed)
                for t in range(PT):
                    nc.gpsimd.indirect_dma_start(
                        slot[:, j, t, 0:width], None, table, bass.IndirectOffsetOnAxis(ap=idx[:, j, t:t + 1], axis=0),
                        bounds_check=rows - 1, oob_is_err=False).then_inc(gathered[name][j], 16)
                if name == "R":
                    for t in range(PT):
                        nc.gpsimd.indirect_dma_start(
                            slot[:, j, t, D:2 * D], None, table, bass.IndirectOffsetOnAxis(ap=idx2[:, j, t:t + 1], axis=0),
                            bounds_check=rows - 1, oob_is_err=False).then_inc(gathered[name][j], 16)

            def gathers(name, table, rows, width=D):
                def body(r):
                    for j in range(RING):
                        gather(name, table, rows, RING * r + j, j, width)
                rounds(pool, body)

            gathers("D", x, N)
            for q in range(2):
                pool.wait_ge(aug_out[q], 16 * ((STATS + 2 - q) // 2))
            quads = aug.rearrange("n (a f) -> (n a) f", f=4)

            def t_round(r):
                for j in range(RING):
                    hold(pool, staged["T"], RING * r + j + 1, pool_passed)
                    for t in range(PT):
                        nc.gpsimd.indirect_dma_start(
                            quads, bass.IndirectOffsetOnAxis(ap=idx[:, j, t:t + 1], axis=0), tslot[:, j, t, :], None,
                            bounds_check=N * AUG // 4 - 1, oob_is_err=False).then_inc(gathered["T"][j], 16)
            rounds(pool, t_round)
            for j in range(RING):
                pool.wait_ge(gathered["T"][j], GATHER * ROUNDS)
            gathers("A", aug, N, AUG)
            for name, prev, table in (("R", "B", tab_b), ("O1", "R", tab_r), ("O2", "O1", tab_o1), ("O3", "O2", tab_o2)):
                for q in range(2):
                    pool.wait_ge(tabled[prev][q], 16 * PAIRS // 2)
                gathers(name, table, ROWS * BLOCK)
            for q in range(2):
                pool.wait_ge(tabled["O3"][q], 16 * PAIRS // 2)
            pool.wait_ge(d_out, 16 * DSTEPS)

            def scatter(c, j):
                hold(pool, rows_set, c + 1, pool_passed)
                for t in range(PT):
                    nc.gpsimd.indirect_dma_start(
                        out, bass.IndirectOffsetOnAxis(ap=oidx[:, j, t:t + 1], axis=0), oslot[:, j, t, :], None,
                        bounds_check=N - 1, oob_is_err=False).then_inc(scattered[j], 16)

            def h_round(r):
                for j in range(RING):
                    c = RING * r + j
                    gather("H", tab_o3, ROWS * BLOCK, c, j)
                    if not (isinstance(c, int) and c == 0):
                        scatter(c - 1, (j - 1) % RING)
            rounds(pool, h_round)
            scatter(PAIRS - 1, (PAIRS - 1) % RING)
            for j in range(RING):
                pool.wait_ge(scattered[j], GATHER * ROUNDS)

        @block.scalar
        def _(act):
            def copy(o, i):
                return nc.scalar.activation(o, i, ACT.Copy)

            act.wait_ge(cleared, 1)
            act.wait_ge(roots_in, 1)
            nc.scalar.activation(tb, ta, ACT.Sqrt).then_inc(roots_out, 1)

            def stat(k, r, q, parts):
                hold(act, stx_in[q], 16 * (r + 1))
                hold(act, sta_free, k - 1)
                hold(act, aug_out[q], 16 * r)
                copy(sta[0:parts, q, :, 0:D], stx[0:parts, q]).then_inc(sta_set, 1)
            for k in range(2):
                stat(k, 0, k, 128)
            with act.Fori(1, STATS // 2) as r:
                for q in range(2):
                    stat(2 * r + q, r, q, 128)
            for k in range(STATS - 1, STATS + 1):
                stat(k, k // 2, k % 2, 128 if k < STATS else LEFT)

            def stage(name, c, j, rows, index):
                if rows is not None:
                    copy(slot[:, j, :, 0:D], chunk(rows, c, 0, D))
                copy(idx[:, j, :], col(index, c)).then_inc(staged[name], 1)

            for j in range(RING):
                act.wait_ge(gathered["T"][j], GATHER * ROUNDS)
            for c in range(RING):
                stage("A", c, c, None, i_src)

            def a_round(r):
                for j in range(RING):
                    c = RING * r + j
                    hold(act, gathered["A"][j], GATHER * (r + 1))
                    copy(chunk(Z, c, 0, D), slot[:, j, :, 0:D]).then_inc(copied_a, 1)
                    if not last(c + RING):
                        hold(act, used["A"], c + 1)
                        stage("A", c + RING, j, None, i_src)
            rounds(act, a_round)

            act.wait_ge(spread_in, 1)
            nc.scalar.activation(st[:, 4], st[:, 3], ACT.Sqrt, bias=eps[:, 0:1]).then_inc(spread_out, 1)

            def root(name, c, n=2 * PT):
                for h in range(2):
                    hold(act, centered[name], 2 * c + h + 1)
                    e = slice(h * n // 2, (h + 1) * n // 2)
                    nc.scalar.activation(yq[:, e], yc[:, e], ACT.Square).then_inc(squared[name], 1)
                hold(act, var_set[name], c + 1)
                nc.scalar.activation(ystd[:, 0:n], yvar[:, 0:n], ACT.Sqrt, bias=eps[:, 0:1], scale=1.0 / D).then_inc(std_set[name], 1)

            def evacuate(name, c, h, k):
                a, b = turns[h]
                hold(act, turned[name], c + 1)
                copy(fx[0:k, h, 0:512], a[0:k, :])
                copy(fx[0:k, h, 512:CHUNK], b[0:k, 0:CHUNK - 512]).then_inc(fx_set[name], 1)

            act.wait_ge(bn_set, 1)

            def fetch_b(c):
                hold(act, turned["B"], 2 * c)
                copy(pz[:, :, 0:D], chunk(Z, c, 0, D))
                copy(pz[:, :, D:], chunk(P, c, 0, D)).then_inc(pz_set, 1)

            def leave_b(c):
                for h in range(2):
                    hold(act, bn_out, 2 * c + h - 1)
                    evacuate("B", 2 * c + h, h, 2 * D)
            fetch_b(0)
            leave_b(0)
            fetch_b(1)

            def b_round(r):
                for j in range(RING):
                    c = RING * r + j
                    if not last(c + 1):
                        leave_b(c + 1)
                    if not last(c + 2):
                        fetch_b(c + 2)
                    root("B", c)
            rounds(act, b_round)

            act.wait_ge(stored["B"], PAIRS)

            def stage_r(c, j):
                copy(idx2[:, j, :], col(i_home, c))
                stage("R", c, j, Z, i_ptr)
            for c in range(RING):
                stage_r(c, c)

            def fetch_r(c, j):
                for h in range(2):
                    hold(act, xb_set_r, TILES * (2 * c + h - 1))
                    evacuate("R", 2 * c + h, h, 2 * D)
                    if h == 0:
                        hold(act, q_used, c)
                    hold(act, q_set, 2 * c + h + 1)
                    for b, lo, hi in ((bank[2], 0, 4), (bank[3], 4, TILES)):
                        q = b[:, 0:(hi - lo) * QW].rearrange("p (t w) -> p t w", w=QW)
                        copy(cur[:, j, TILES * h + lo:TILES * h + hi], q[:, :, 0:D])
                        op = copy(qs[:, TILES * h + lo:TILES * h + hi], q[:, :, D:])
                    op.then_inc(q_out, 1)

            def squash(c):
                hold(act, dot_set, c + 1)
                nc.scalar.activation(att[:, 1], att[:, 0], ACT.Tanh).then_inc(tanh_set, 1)

            def one_hot(c):
                hold(act, types_in, 16 * (c + 1))
                hold(act, q_set, 2 * c)
                for h in range(2):
                    op = nc.scalar.activation(oh[:, h].rearrange("k (t b r) -> k b t r", b=BLOCKS, r=32),
                                              types[:, h * CHUNK:(h + 1) * CHUNK].rearrange("k (b t r) -> k b t r", b=BLOCKS, r=32),
                                              ACT.Abs, bias=relno[:, 0:1])
                op.then_inc(types_read, 1)
                act.drain()
                for h in range(2):
                    op = nc.scalar.activation(oh[:, h], oh[:, h], ACT.Relu, scale=-1.0, bias=ones[:, 0:1])
                op.then_inc(types_set, 1)
            one_hot(0)
            fetch_r(0, 0)
            squash(0)

            def r_round(r):
                for j in range(RING):
                    c = RING * r + j
                    if not last(c + RING):
                        hold(act, turned["R"], 2 * c + 2)
                        stage_r(c + RING, j)
                    if not last(c + 1):
                        one_hot(c + 1)
                    hold(act, centered["R"], 2 * c)
                    copy(yh[:, :, 0], chunk(Z, c, 0, D)).then_inc(source_set, 1)
                    if not last(c + 1):
                        hold(act, stored["R"], c)
                        fetch_r(c + 1, (j + 1) % RING)
                    root("R", c)
                    if not last(c + 1):
                        squash(c + 1)
            rounds(act, r_round)

            def dense_turned(k):
                hold(act, d_turned, k + 1)
                hold(act, d_prod, k)
                copy(dxt[:, 0:512], bank[0][:, :])
                copy(dxt[:, 512:], bank[1][:, 0:DW - 512]).then_inc(d_xt, 1)

            def dense_square1(k):
                hold(act, d_c1, k + 1)
                nc.scalar.activation(dq, dc, ACT.Square).then_inc(d_q1, 1)

            def dense(k):
                hold(act, d_v1, k + 1)
                nc.scalar.activation(dstd[:, :], dvar[:, :], ACT.Sqrt, bias=eps[:, 1:2], scale=(1.0 + EPS) / D).then_inc(d_s1, 1)
                hold(act, d_x2, k + 1)
                nc.scalar.activation(dq, dy, ACT.Relu, scale=1.0 - ALPHA).then_inc(d_relu, 1)
                if not final(k):
                    dense_turned(k + 1)
                hold(act, d_c2, k + 1)
                nc.scalar.activation(dy, dq, ACT.Square).then_inc(d_q2, 1)
                hold(act, d_v2, k + 1)
                nc.scalar.activation(dstd[:, :], dvar[:, :], ACT.Sqrt, bias=eps[:, 1:2], scale=(1.0 + EPS) / D).then_inc(d_s2, 1)
            dense_turned(0)

            def chain(c):
                nc.scalar.activation(chunk(P, c), chunk(Z, c, 0, D), ACT.Relu, scale=1.0 - ALPHA).then_inc(chain_set, 1)

            for name, prev, rows in (("O1", "R", Z), ("O2", "O1", P), ("O3", "O2", P)):
                act.wait_ge(stored[prev], PAIRS)
                for c in range(RING):
                    stage(name, c, c, rows, i_ptr)

                if name == "O1":
                    chain(0)
                for k in dense_alone(name):
                    dense_square1(k)
                    dense(k)

                def o_round(r, name=name, rows=rows):
                    for j in range(RING):
                        c = RING * r + j
                        for k in dense_steps(name, c, r, j):
                            dense_square1(k)
                        if not last(c + RING):
                            hold(act, used[name], c + 1)
                            stage(name, c + RING, j, rows, i_ptr)
                        if name == "O1" and not last(c + 1):
                            chain(c + 1)
                        for k in dense_steps(name, c, r, j):
                            dense(k)
                        if name == "O3":
                            root(name, c)
                rounds(act, o_round)

            act.wait_ge(stored["O3"], PAIRS)
            for c in range(RING):
                stage("H", c, c, Z, i_ptr)

            def fetch_h(c):
                for h in range(2):
                    hold(act, xb_set_h, TILES * (2 * c + h - 1))
                    evacuate("H", 2 * c + h, h, D)
            fetch_h(0)

            def h_round(r):
                for j in range(RING):
                    c = RING * r + j
                    if not last(c + RING):
                        hold(act, turned["H"], 2 * c + 2)
                        stage("H", c + RING, j, Z, i_ptr)
                    root("H", c, PT)
                    if not last(c + 1):
                        fetch_h(c + 1)
            rounds(act, h_round)

        @block.vector
        def _(dve):
            v = nc.vector

            def settle():
                v.drain()

            for t, value in ((bdst, FAR), (bprev, FAR), (bnext, FAR), (bsrc, 0), (bp[:, 4], 0.0), (bp[:, 6], 0.0), (by_rows[:, 0:8 * BLOCK], 0.0), (slot, 0.0)):
                v.memset(whole(t), value)
            settle()
            v.memset(bprev[0:1, 0:1], -1).then_inc(padded, 1)
            v.memset(whole(bs), 0.0)
            for t, value in ((planes[:, 0:PLANES * BLOCK], 0.0), (bzero, 0.0), (brow, 0.0), (zer, 0.0), (ones, 1.0), (eps[:, 0:1], EPS),
                             (eps[:, 1:2], EPS * EPS), (trow, 0.0), (sta, 0.0)):
                v.memset(whole(t), value)
            settle()
            v.memset(sta[:, :, :, D:D + 1], 1.0)
            v.memset(sta[:, :, :, D + 2:D + 3], float(NOWHERE))
            settle()
            v.memset(run[:, 0:1], 0.0).then_inc(cleared, 1)

            dve.wait_ge(blocks_in, 16 * 17)
            v.tensor_tensor(bcont, bdst[:, :], bprev[:, :], ALU.is_equal)
            v.tensor_tensor(bp[:, 3], bdst[:, :], bnext[:, :], ALU.not_equal)
            v.tensor_copy(bp[:, 0], bsrc[:, :])
            v.tensor_copy(bp[:, 1], bdst[:, :])
            v.tensor_copy(bp[:, 7:10], raw3.rearrange("p (e k) -> p k e", k=3))
            v.tensor_copy(bp[:, 10:15], raw5.rearrange("p (e k) -> p k e", k=5))
            settle()
            v.tensor_tensor_scan(bsum, bcont, bp[:, 4], 0.0, ALU.mult, ALU.add)
            v.tensor_tensor_scan(bpref, bcont, bzero, 1.0, ALU.mult, ALU.add)
            settle()
            dve.wait_ge(consts_in, 16 * 13)
            v.tensor_tensor(bback, bp[:, 3], bown, ALU.mult)
            v.tensor_scalar(bgo, bp[:, 3], -1.0, 1.0, ALU.mult, ALU.add)
            settle()
            v.tensor_tensor_scan(bp[:, 5, ::-1], bgo[:, ::-1], bback[:, ::-1], 0.0, ALU.mult, ALU.add)
            v.tensor_tensor_scan(blast[:, ::-1], bgo[:, ::-1], bzero, 1.0, ALU.mult, ALU.add)
            settle()
            v.tensor_copy(bmask[:, 0], bcont)
            settle()
            v.memset(bmask[:, 0, 0:1], 0.0)
            v.tensor_copy(bmask[:, 1], bpref).then_inc(ends_scanned, 1)
            dve.wait_ge(ends_turned, 1)
            v.tensor_copy(brow[0:1, 0, 0:ROWS], bank[6][0:1, 0:ROWS])
            v.tensor_copy(brow[0:1, 1, 0:ROWS], bank[6][0:1, 128:128 + ROWS])
            v.tensor_copy(brow[0:1, 3, 0:ROWS], bank[6][0:1, 256:256 + ROWS])
            v.tensor_copy(brow[0:1, 4, 0:ROWS], bank[6][0:1, 384:384 + ROWS])
            settle()
            v.tensor_tensor_scan(brow[0:1, 5, 0:ROWS][:, ::-1], brow[0:1, 4, 0:ROWS][:, ::-1], brow[0:1, 3, 0:ROWS][:, ::-1], 0.0,
                                 ALU.mult, ALU.add)
            v.tensor_tensor_scan(brow[0:1, 2, 1:ROWS + 1], brow[0:1, 1, 0:ROWS], brow[0:1, 0, 0:ROWS], 0.0,
                                 ALU.mult, ALU.add).then_inc(ends_summed, 1)
            dve.wait_ge(carry_out, 1)
            v.tensor_copy(bcarry[:, :], bank[6][0:ROWS, 256:258])
            settle()
            v.scalar_tensor_tensor(bp[:, 5], blast, bcarry[:, 1:2], bp[:, 5], ALU.mult, ALU.add)
            v.scalar_tensor_tensor(bp[:, 2], bpref, bcarry[:, 0:1], bsum, ALU.mult, ALU.add).then_inc(planes_set, 1)

            dve.wait_ge(planes_in, 16 * BLOCKS)
            v.transpose(raw, planes[:, 0:PLANES * BLOCK])
            settle()
            for h in range(2):
                v.tensor_copy(i_dst[:, :, TILES * h:TILES * (h + 1)].rearrange("p c t -> p t c"),
                              raw.rearrange("p (k t c) -> p k t c", k=PLANES, t=TILES)[:, 1, :, h:CHUNKS:2])
            settle()

            def stage_d(c, j):
                v.tensor_copy(idx[:, j, :], col(i_dst, c)).then_inc(staged["D"], 1)

            def d_round(r):
                for j in range(RING):
                    c = RING * r + j
                    hold(dve, gathered["D"][j], GATHER * (r + 1))
                    v.tensor_copy(chunk(Z, c, D), slot[:, j, :, 0:D])
                    settle()
                    if not last(c + RING):
                        stage_d(c + RING, j)
            d_round(0)
            for h in range(2):
                v.tensor_copy(scal[:, :, :, TILES * h:TILES * (h + 1)].rearrange("p k c t -> p k t c"),
                              raw.rearrange("p (k t c) -> p k t c", k=PLANES, t=TILES)[:, :, :, h:CHUNKS:2])
            settle()
            v.tensor_scalar(tm[:, 0], degree, 1.0, None, ALU.add)
            v.tensor_scalar(tm[:, 1], degree, 0.0, None, ALU.is_gt)
            v.tensor_scalar(ta[:, 1], degree, TINY, None, ALU.max)
            v.tensor_copy(i_home[:, :, :], home)
            v.tensor_copy(trow[:, :, :, 2], own)
            v.tensor_copy(i_src[:, :, :], srcs)
            v.tensor_scalar(minus[:, :, :], ends, -1.0, None, ALU.mult)
            v.tensor_scalar(tb[:, 0], dsts, float(-NOWHERE), None, ALU.add)
            v.tensor_scalar(tb[:, 1], dsts, float(AUG // 4), float(D // 4 - NOWHERE), ALU.mult, ALU.add)
            settle()
            v.tensor_scalar(ta[:, 0], tm[:, 0], TINY, None, ALU.max)
            v.tensor_tensor(tb[:, 0], tb[:, 0], ends, ALU.mult)
            v.tensor_tensor(tb[:, 1], tb[:, 1], ends, ALU.mult)
            settle()
            v.tensor_scalar(tm[:, 0], tm[:, 0], 0.0, None, ALU.is_gt)
            v.tensor_scalar(i_out[:, :, :], tb[:, 0], float(NOWHERE), None, ALU.add)
            v.tensor_scalar(i_aug[:, :, :], tb[:, 1], float(NOWHERE), None, ALU.add).then_inc(roots_in, 1)
            dve.wait_ge(roots_out, 1)
            v.reciprocal(tb, tb)
            settle()
            v.tensor_tensor(dinv[:, :, :], tb[:, 0], tm[:, 0], ALU.mult)
            v.tensor_tensor(dis[:, :, :], tb[:, 1], tm[:, 1], ALU.mult)
            settle()
            v.tensor_tensor(endinv[:, :, :], dinv[:, :, :], ends, ALU.mult)
            v.tensor_copy(trow[:, :, :, 0], dinv[:, :, :])
            v.tensor_copy(trow[:, :, :, 1], dis[:, :, :])
            settle()

            with dve.Fori(1, ROUNDS - 1) as r:
                d_round(r)
            d_round(ROUNDS - 1)

            def t_round(r):
                for j in range(RING):
                    c = RING * r + j
                    hold(dve, gathered["T"][j], GATHER * r)
                    v.tensor_copy(tslot[:, j], trow[:, at(c)].rearrange("p c t f -> p (c t) f"))
                    v.tensor_copy(idx[:, j, :], col(i_aug, c)).then_inc(staged["T"], 1)
            rounds(dve, t_round)
            v.tensor_scalar(dis[:, :, :], dis[:, :, :], ALPHA, None, ALU.mult)

            for k in range(6):
                w_ = over(wts[:, k], SH)
                v.tensor_tensor(bs[0:D] if k == 0 else bs2, cgs[:, k], w_, ALU.mult)
                settle()
                if k:
                    v.tensor_tensor(bs[0:D], bs[0:D], bs2, ALU.add)
                    settle()

            def flat(t):
                return t[:, :, :].rearrange("p t f -> p (t f)")

            def sum_in_blocks(c):
                v.transpose(fm, flat(msg))
                settle()
                v.tensor_tensor_scan(fs, two(cont, c), fm, 0.0, ALU.mult, ALU.add)
                settle()

            def sum_over_blocks(c):
                for q in range(BLOCKS):
                    v.tensor_copy(blk[:, q::BLOCKS], fs[32 * q:32 * q + 32, BLOCK - 1::BLOCK])
                settle()
                n = 2 * BLOCKS
                ends_ = through[:, c * n:(c + 1) * n] if isinstance(c, int) else through[:, bass.ds(c * n, n)]
                v.tensor_tensor_scan(run[:, 1:n + 1], ends_, blk[:, :], run[:, 0:1], ALU.mult, ALU.add)
                settle()
                for q in range(BLOCKS):
                    v.tensor_copy(carry[32 * q:32 * q + 32, :], run[:, q:n:BLOCKS])
                settle()
                v.tensor_copy(run[:, 0:1], run[:, n:n + 1])

            def sum_out(c):
                for h in range(2):
                    e = slice(h * BLOCK, (h + 1) * BLOCK)
                    v.scalar_tensor_tensor(fo[:, e], two(pref, c)[:, e], carry[:, h:h + 1], fs[:, e], ALU.mult, ALU.add)
                settle()
                v.transpose(flat(agg), fo)
                settle()

            def sum_runs(c):
                sum_in_blocks(c)
                sum_over_blocks(c)
                sum_out(c)

            def two(t, c):
                e = t[:, 2 * c:2 * c + 2] if isinstance(c, int) else t[:, bass.ds(2 * c, 2)]
                return e.rearrange("p c e -> p (c e)")

            v.memset(gr, 1.0)
            dve.wait_ge(sta_free, STATS + 1)
            for q in range(2):
                dve.wait_ge(aug_out[q], 16 * ((STATS + 2 - q) // 2))
            v.memset(fx[64:128], 0.0)
            settle()
            v.memset(fx[64:65], 1.0)
            settle()
            dve.wait_ge(masks_in, 16 * (2 * BLOCKS + 1))

            def a_round(r):
                for j in range(RING):
                    c = RING * r + j
                    hold(dve, gathered["A"][j], GATHER * (r + 1))
                    s = slot[:, j]
                    v.tensor_tensor(sw[:, :], col(weight, c), s[:, :, D], ALU.mult)
                    v.tensor_tensor(col(norm2, c), col(weight, c), s[:, :, D + 1], ALU.mult)
                    v.tensor_copy(col(i_ptr, c), s[:, :, D + 2])
                    v.tensor_tensor(msg2[:, :, :], chunk(Z, c, D), over(col(endinv, c)), ALU.mult)
                    settle()
                    v.tensor_tensor(msg[:, :, :], s[:, :, 0:D], over(sw[:, :]), ALU.mult)
                    settle()
                    v.tensor_tensor(msg[:, :, :], msg[:, :, :], msg2[:, :, :], ALU.add).then_inc(used["A"], 1)
                    settle()
                    sum_runs(c)
                    v.tensor_tensor(msg2[:, :, :], agg[:, :, :], over(col(dinv, c)), ALU.mult)
                    settle()
                    v.tensor_copy(chunk(P, c), msg2[:, :, :])
                    hold(dve, gram_used, c)
                    v.tensor_copy(gr[:, 0, :, 0:D], msg2[:, :, :])
                    v.tensor_copy(gr[:, 1, :, 0:D], chunk(Z, c, D))
                    v.tensor_tensor(gl[:, 0], msg2[:, :, :], over(col(ends, c)), ALU.mult)
                    v.tensor_tensor(gl[:, 1], chunk(Z, c, D), over(col(minus, c)), ALU.mult).then_inc(gram_set, 1)
                    settle()
            rounds(dve, a_round)

            dve.wait_ge(gram_done, 1)
            v.tensor_copy(gram[:, :], G)
            v.tensor_copy(srep[:, :], G[:, D:D + 1].broadcast_to([32, 128])).then_inc(gram_read, 1)
            dve.wait_ge(mean_done, 1)
            v.tensor_scalar(st[:, 0], bank[6][:, 0:D], 1.0 / N, None, ALU.mult)
            v.tensor_tensor(vv[:, :], bank[6][0:32, 64:64 + D], wg[:, :], ALU.mult).then_inc(vv_set, 1)
            dve.wait_ge(square_done, 1)
            v.tensor_scalar(st[:, 1], bank[6][:, 128:128 + D], 1.0 / N, None, ALU.mult)
            settle()
            v.tensor_tensor(st[:, 2], st[:, 0], st[:, 0], ALU.mult)
            v.tensor_tensor(st[:, 6], st[:, 0], bgb[:, 0], ALU.add)
            settle()
            v.tensor_tensor(st[:, 3], st[:, 1], st[:, 2], ALU.subtract)
            v.tensor_tensor(st[:, 6], bgb[:, 0], st[:, 6], ALU.subtract)
            settle()
            v.tensor_scalar(st[:, 3], st[:, 3], 0.0, None, ALU.max)
            settle()
            v.drain().then_inc(spread_in, 1)
            dve.wait_ge(spread_out, 1)
            v.reciprocal(st[:, 5], st[:, 4])
            settle()
            v.tensor_tensor(st[:, 5], st[:, 5], bgb[:, 1], ALU.mult)
            settle()
            v.tensor_tensor(st[:, 6], st[:, 6], st[:, 5], ALU.mult)
            settle()
            v.tensor_tensor(st[:, 7], st[:, 6], bgb[:, 2], ALU.add)

            def tiled(row, n):
                return row.unsqueeze(1).broadcast_to([row.shape[0], n, D])
            settle()
            v.tensor_tensor(w2s[0:64, :].rearrange("p (n f) -> p n f", f=D), w2s[0:64, :].rearrange("p (n f) -> p n f", f=D), tiled(st[0:64, 5], 2), ALU.mult)
            v.tensor_copy(w2s[64:65, :].rearrange("p (n f) -> p n f", f=D), tiled(st[64:65, 7], 2))
            v.tensor_tensor(w4s[:, :].rearrange("p (n f) -> p n f", f=D), w4s[:, :].rearrange("p (n f) -> p n f", f=D), tiled(st[:, 5], 4), ALU.mult)
            v.tensor_copy(t16[0:1], tiled(st[0:1, 7], 16))
            settle()
            v.memset(run[:, 0:1], 0.0).then_inc(bn_set, 1)

            def layer_norm(name, c, o, n=2 * PT):
                halves_ = (slice(0, n // 2), slice(n // 2, n))
                v.tensor_reduce(ysum[:, 0:n], y[:, 0:n], AX.X, ALU.add)
                settle()
                for e in halves_:
                    v.scalar_tensor_tensor(yc[:, e], over(ysum[:, e]), 1.0 / D, y[:, e], ALU.mult, ALU.subtract).then_inc(centered[name], 1)
                for h, e in enumerate(halves_):
                    hold(dve, squared[name], 2 * c + h + 1)
                    op = v.tensor_reduce(yvar[:, e], yq[:, e], AX.X, ALU.add)
                op.then_inc(var_set[name], 1)
                if name == "R" and not last(c + 1):
                    dots(c + 1)
                if name == "B" and not last(c + 1):
                    normalise(c + 1)
                hold(dve, std_set[name], c + 1)
                v.reciprocal(yr[:, 0:n], ystd[:, 0:n])
                settle()
                return v.scalar_tensor_tensor(o, yc[:, 0:n], -1.0, over(yr[:, 0:n]), ALU.mult, ALU.mult)

            def pairs(c):
                return Z[:, at(c)].rearrange("p c t (h f) -> p (c t h) f", f=D)

            def normalise(c):
                for h in range(2):
                    hold(dve, bn_out, 2 * c + h + 1)
                    e = slice(h * PT, (h + 1) * PT)
                    v.scalar_tensor_tensor(y[:, e], bank[2 + h][:, 0:PT * D].rearrange("p (n f) -> p n f", f=D), 0.0, pairs(c)[:, e],
                                           ALU.max, ALU.add).then_inc(bn_used, 1)

            def b_round(r):
                for j in range(RING):
                    c = RING * r + j
                    layer_norm("B", c, pairs(c)).then_inc(stored["B"], 1)
                    settle()
            normalise(0)
            settle()
            rounds(dve, b_round)

            def basis(name, c, j, n, xb_set, xb_used):
                def view(t):
                    return prod[:, t // 2 % 2, :, 0:D * n].rearrange("p k (f n) -> p k f n", n=n)

                def times(t):
                    for t in (t, t + 1):
                        hold(dve, xb_set, PT * c + t + 1)
                        v.tensor_tensor(view(t)[:, t % 2], xb(t)[:, 0:D * n].rearrange("p (f n) -> p f n", n=n),
                                        ca[:, t, 0:n].unsqueeze(1).broadcast_to([128, D, n]), ALU.mult).then_inc(xb_used, 1)
                times(0)
                for t in range(0, PT, 2):
                    settle()
                    if t + 2 < PT:
                        times(t + 2)
                    v.tensor_reduce(msg[:, t:t + 2, :], view(t), AX.X, ALU.add)
                settle()

            def dots(c):
                hold(dve, q_out, 2 * c + 2)
                v.tensor_tensor(msg2[:, :], qs[:, :, Q1 - D:Q2 - D], qs[:, :, Q2 - D:CO - D], ALU.mult)
                settle()
                v.tensor_reduce(att[:, 2], msg2[:, :], AX.X, ALU.add)
                settle()
                v.tensor_scalar(att[:, 0], att[:, 2], float(D ** -0.5), 0.0, ALU.mult, ALU.max).then_inc(dot_set, 1)

            dots(0)
            v.memset(run[:, 0:1], 0.0)
            settle()

            def r_round(r):
                for j in range(RING):
                    c = RING * r + j
                    hold(dve, tanh_set, c + 1)
                    v.tensor_tensor(ca[:, :, :], qs[:, :, CO - D:], over(att[:, 1], BASES), ALU.mult).then_inc(q_used, 1)
                    settle()
                    basis("R", c, j, BASES, xb_set_r, xb_used_r)
                    sum_runs(c)
                    v.tensor_tensor(agg[:, :, :], agg[:, :, :], cur[:, j], ALU.add)
                    settle()
                    v.scalar_tensor_tensor(yh[:, :, 1], agg[:, :, :], 0.0, chunk(Z, c, D), ALU.max, ALU.add)
                    settle()
                    hold(dve, source_set, c + 1)
                    layer_norm("R", c, pairs(c)).then_inc(stored["R"], 1)
                    settle()
            rounds(dve, r_round)

            def groups(t):
                return t.rearrange("p (k f) -> p k f", f=D)

            def dense_first(k):
                hold(dve, d_prod, k + 1)
                v.scalar_tensor_tensor(dy[:, 0:512], bank[2][:, :], 0.0, dx[:, 0:512], ALU.max, ALU.add)
                v.scalar_tensor_tensor(dy[:, 512:], bank[3][:, 0:DW - 512], 0.0, dx[:, 512:], ALU.max, ALU.add).then_inc(d_y, 1)
                settle()
                v.tensor_reduce(dsum[:, :], groups(dy), AX.X, ALU.add)
                settle()
                v.scalar_tensor_tensor(groups(dc), over(dsum[:, :]), 1.0 / D, groups(dy), ALU.mult, ALU.subtract).then_inc(d_c1, 1)

            def dense_spread1(k):
                hold(dve, d_q1, k + 1)
                v.tensor_reduce(dvar[:, :], groups(dq), AX.X, ALU.add).then_inc(d_v1, 1)

            def dense_norm1(k):
                hold(dve, d_s1, k + 1)
                v.reciprocal(dr[:, :], dstd[:, :])
                settle()
                v.scalar_tensor_tensor(groups(dy), groups(dc), -1.0, over(dr[:, :]), ALU.mult, ALU.mult).then_inc(d_x2, 1)

            def dense_second(k):
                hold(dve, d_relu, k + 1)
                v.scalar_tensor_tensor(dc, dq, 1.0, dy, ALU.min, ALU.add)
                settle()
                v.tensor_reduce(dsum[:, :], groups(dc), AX.X, ALU.add)
                settle()
                v.scalar_tensor_tensor(groups(dq), over(dsum[:, :]), 1.0 / D, groups(dc), ALU.mult, ALU.subtract).then_inc(d_c2, 1)

            def dense_spread2(k):
                hold(dve, d_q2, k + 1)
                v.tensor_reduce(dvar[:, :], groups(dy), AX.X, ALU.add).then_inc(d_v2, 1)

            def dense_norm2(k):
                hold(dve, d_s2, k + 1)
                v.reciprocal(dr[:, :], dstd[:, :])
                settle()
                hold(dve, d_out, 16 * k)
                v.scalar_tensor_tensor(groups(do_), groups(dq), -1.0, over(dr[:, :]), ALU.mult, ALU.mult).then_inc(d_set, 1)

            for name in ("O1", "O2", "O3"):
                v.memset(run[:, 0:1], 0.0)
                settle()
                for k in dense_alone(name):
                    for part in (dense_first, dense_spread1, dense_norm1, dense_second, dense_spread2, dense_norm2):
                        part(k)
                    settle()

                def o_round(r, name=name):
                    for j in range(RING):
                        c = RING * r + j
                        dense = dense_steps(name, c, r, j)
                        for k in dense:
                            dense_first(k)
                        hold(dve, gathered[name][j], GATHER * (r + 1))
                        v.tensor_tensor(msg[:, :, :], slot[:, j, :, 0:D], over(col(norm2, c)), ALU.mult).then_inc(used[name], 1)
                        if name == "O1":
                            hold(dve, chain_set, c + 1)
                            v.tensor_scalar(chunk(P, c), chunk(P, c), 1.0, None, ALU.min)
                        settle()
                        for k in dense:
                            dense_spread1(k)
                        sum_in_blocks(c)
                        for k in dense:
                            dense_norm1(k)
                        sum_over_blocks(c)
                        for k in dense:
                            dense_second(k)
                        sum_out(c)
                        v.tensor_tensor(agg[:, :, :], agg[:, :, :], over(col(dis, c)), ALU.mult)
                        for k in dense:
                            dense_spread2(k)
                        settle()
                        v.scalar_tensor_tensor(msg[:, :, :], chunk(Z, c, D), 1.0 - ALPHA, agg[:, :, :], ALU.mult, ALU.add)
                        settle()
                        if name == "O3":
                            for k in dense:
                                dense_norm2(k)
                            v.tensor_scalar(msg[:, :, :], msg[:, :, :], 0.0, 1.0, ALU.max, ALU.min)
                            v.tensor_tensor(yh[:, :, 0], chunk(Z, c, 0, D), chunk(P, c), ALU.add)
                            settle()
                            v.tensor_tensor(yh[:, :, 1], chunk(Z, c, D), msg[:, :, :], ALU.add)
                            settle()
                            layer_norm(name, c, pairs(c)).then_inc(stored[name], 1)
                        else:
                            if not (isinstance(c, int) and c == 0):
                                hold(dve, tabled[name][(j - 1) % RING], 16 * (r + j))
                            v.tensor_scalar(ob[:, :, :], msg[:, :, :], 0.0, 1.0, ALU.max, ALU.min).then_inc(stored[name], 1)
                            for k in dense:
                                dense_norm2(k)
                        settle()
                rounds(dve, o_round)

            v.memset(run[:, 0:1], 0.0)

            def h_round(r):
                for j in range(RING):
                    c = RING * r + j
                    v.tensor_copy(ca[:, :, 0:SH], scal[:, 6:PLANES, at(c)].rearrange("p k c t -> p (c t) k"))
                    settle()
                    basis("H", c, j, SH, xb_set_h, xb_used_h)
                    sum_runs(c)
                    v.tensor_tensor(y[:, 0:PT], agg[:, :, :], chunk(Z, c, D), ALU.add)
                    if not (isinstance(c, int) and c < RING):
                        hold(dve, scattered[j], GATHER * r)
                    v.tensor_copy(oidx[:, j, :], col(i_out, c))
                    settle()
                    layer_norm("H", c, oslot[:, j], PT).then_inc(rows_set, 1)
                    settle()
            rounds(dve, h_round)

        @block.tensor
        def _(pe):
            t_ = nc.tensor
            pe.wait_ge(consts_in, 16 * 13)
            pe.wait_ge(cleared, 1)
            t_.matmul(G, zer[:, 0:32], zer[:, 0:D + 1], start=True, stop=False)
            pe.wait_ge(ends_scanned, 1)
            t_.transpose(bank[6][0:1, 0:ROWS], bsum[:, BLOCK - 1:BLOCK], idn[0:ROWS, 0:ROWS])
            t_.transpose(bank[6][0:1, 128:128 + ROWS], bpref[:, BLOCK - 1:BLOCK], idn[0:ROWS, 0:ROWS])
            t_.transpose(bank[6][0:1, 256:256 + ROWS], bp[:, 5, 0:1], idn[0:ROWS, 0:ROWS])
            t_.transpose(bank[6][0:1, 384:384 + ROWS], blast[:, 0:1], idn[0:ROWS, 0:ROWS]).then_inc(ends_turned, 1)
            pe.wait_ge(ends_summed, 1)
            t_.matmul(bank[6][0:ROWS, 256:257], brow[0:1, 2, 0:ROWS], ones[0:1, 0:1], start=True, stop=True)
            t_.matmul(bank[6][0:ROWS, 257:258], brow[0:1, 5, 1:ROWS + 1], ones[0:1, 0:1], start=True, stop=True).then_inc(carry_out, 1)

            def stat(k, q, parts):
                hold(pe, sta_set, k + 1)
                for i in range(STATK):
                    op = t_.matmul(G, sta[0:parts, q, i, 0:D], sta[0:parts, q, i, 0:D + 1], start=False, stop=False)
                op.then_inc(sta_free, 1)
            with pe.Fori(0, (STATS - 1) // 2) as r:
                for q in range(2):
                    stat(2 * r + q, q, 128)
            for k in range(STATS - 1, STATS + 1):
                stat(k, k % 2, 128 if k < STATS else LEFT)

            def a_round(r):
                for j in range(RING):
                    c = RING * r + j
                    hold(pe, gram_set, c + 1)
                    for q in range(2):
                        for t in range(PT):
                            end = isinstance(c, int) and c == PAIRS - 1 and q == 1 and t == PT - 1
                            op = t_.matmul(G, gl[:, q, t, :], gr[:, q, t, :], start=False, stop=end)
                    op.then_inc(gram_used, 1)
            rounds(pe, a_round)
            t_.drain().then_inc(gram_done, 1)
            pe.wait_ge(gram_read, 1)
            t_.matmul(bank[6][:, 0:D], srep[:, :], wg[:, :], start=True, stop=True)
            t_.matmul(bank[6][0:32, 64:64 + D], gram[:, 0:D], wg[:, :], start=True, stop=True).then_inc(mean_done, 1)
            pe.wait_ge(vv_set, 1)
            t_.matmul(bank[6][:, 128:128 + D], ones[0:32, :], vv[:, :], start=True, stop=True).then_inc(square_done, 1)

            def turn(name, rows, h, k):
                for t in range(TILES):
                    b = turns[h][t // 4]
                    op = t_.transpose(b[0:k, 128 * (t % 4):128 * (t % 4) + 128], rows[:, TILES * h + t, 0:k], idn[:, :])
                op.then_inc(turned[name], 1)

            pe.wait_ge(bn_set, 1)

            def b_round(r):
                for j in range(RING):
                    c = RING * r + j
                    hold(pe, pz_set, c + 1)
                    for h in range(2):
                        hold(pe, fx_set["B"], 2 * c + h - 1, pe_passed)
                        turn("B", pz, h, 2 * D)
                    for h in range(2):
                        hold(pe, fx_set["B"], 2 * c + h + 1)
                        hold(pe, bn_used, 2 * c + h - 1)
                        for t in range(TILES):
                            op = t_.matmul(bank[2 + h][:, 2 * D * t:2 * D * (t + 1)], fx[:, h, 128 * t:128 * (t + 1)], w2s[:, :],
                                           start=True, stop=True)
                        op.then_inc(bn_out, 1)
            rounds(pe, b_round)

            def product(c, t, rhs, n, xb_set, xb_used):
                if t >= 6:
                    hold(pe, xb_used, PT * c + t - (1 if t > 7 else 7))
                t_.matmul(xb(t)[:, 0:n], fx[:, t // TILES, 128 * (t % TILES):128 * (t % TILES + 1)], rhs,
                          start=True, stop=True).then_inc(xb_set, 1)

            def turn_r(c, r, j, h):
                hold(pe, gathered["R"][j], 2 * GATHER * (r + 1), pe_passed)
                hold(pe, fx_set["R"], 2 * c + h - 1, pe_passed)
                turn("R", slot[:, j], h, 2 * D)

            def attend(c, h, t):
                if t == 0:
                    hold(pe, fx_set["R"], 2 * c + h + 1)
                    hold(pe, q_out, 2 * c + h)
                    hold(pe, types_set, c + 1)
                b = bank[2] if t < 4 else bank[3]
                o = QW * (t % 4)
                t_.matmul(b[:, o:o + QW], fx[:, h, 128 * t:128 * (t + 1)], wqs[:, :], start=True, stop=False)
                op = t_.matmul(b[:, o + Q2:o + QW], oh[:, h, 128 * t:128 * (t + 1)], relcs[:, :], start=False, stop=True)
                if t == TILES - 1:
                    op.then_inc(q_set, 1)
            for h in range(2):
                turn_r(0, 0, 0, h)
            for h in range(2):
                for t in range(TILES):
                    attend(0, h, t)

            def r_round(r):
                for j in range(RING):
                    c = RING * r + j
                    basis_r = (wcs[:, :], D * BASES, xb_set_r, xb_used_r)
                    early = 8
                    for t in range(early):
                        if t == 4:
                            hold(pe, q_out, 2 * c + 2)
                        product(c, t, *basis_r)
                    if not last(c + 1):
                        for h in range(2):
                            hold(pe, xb_used_r, PT * c + 2 * h + 2, pe_passed)
                            turn_r(c + 1, r + (j + 1) // RING, (j + 1) % RING, h)
                    for t in range(early, PT):
                        product(c, t, *basis_r)
                        if t > early and not last(c + 1):
                            attend(c + 1, 0, t - early - 1)
                    if not last(c + 1):
                        for t in range(PT - early - 1, TILES):
                            attend(c + 1, 0, t)
                        for t in range(TILES):
                            attend(c + 1, 1, t)
            rounds(pe, r_round)

            def dense(k):
                hold(pe, d_in, 16 * (k + 1))
                hold(pe, d_xt, k)
                for g in range(DW // 128):
                    op = t_.transpose(bank[g // 4][:, 128 * (g % 4):128 * (g % 4 + 1)], dx[:, 128 * g:128 * (g + 1)], idn[:, :])
                op.then_inc(d_turned, 1)
                hold(pe, d_xt, k + 1)
                hold(pe, d_y, k)
                for h, n in enumerate((512, DW - 512)):
                    t_.matmul(bank[2 + h][:, 0:n], ones[0:1, :], t16[0:1, 0:n // D].rearrange("p n f -> p (n f)"), start=True, stop=False)
                for g in range(DW // 128):
                    op = t_.matmul(bank[2 + g // 4][:, 128 * (g % 4):128 * (g % 4 + 1)], dxt[:, 128 * g:128 * (g + 1)], w4s[:, :],
                                   start=False, stop=g % 4 == 3 or g == DW // 128 - 1)
                op.then_inc(d_prod, 1)

            for name in ("O1", "O2", "O3"):
                for k in dense_alone(name):
                    dense(k)

                def o_round(r, name=name):
                    for j in range(RING):
                        for k in dense_steps(name, RING * r + j, r, j):
                            dense(k)
                rounds(pe, o_round)

            def turn_h(c, r, j, h):
                hold(pe, gathered["H"][j], GATHER * (r + 1))
                hold(pe, fx_set["H"], 2 * c + h - 1)
                turn("H", slot[:, j], h, D)
            for h in range(2):
                turn_h(0, 0, 0, h)

            def h_round(r):
                for j in range(RING):
                    c = RING * r + j
                    hold(pe, fx_set["H"], 2 * c + 2)
                    for h in range(2):
                        for t in range(TILES * h, TILES * (h + 1)):
                            product(c, t, bs[:, :, :].rearrange("p f n -> p (f n)"), D * SH, xb_set_h, xb_used_h)
                    if not last(c + 1):
                        for h in range(2):
                            turn_h(c + 1, r + (j + 1) // RING, (j + 1) % RING, h)
            rounds(pe, h_round)


def coupling():
    import math
    import numpy as np
    combos = [(0, 0, 0), (0, 1, 1), (1, 0, 1), (1, 1, 0), (1, 1, 1), (2, 1, 1)]

    def coefficient(j1, m1, j2, m2, j3, m3):
        f = math.factorial
        lo, hi = max(0, j2 - j3 - m1, j1 + m2 - j3), min(j1 + j2 - j3, j1 - m1, j2 + m2)
        pref = (2 * j3 + 1) * f(j3 + j1 - j2) * f(j3 - j1 + j2) * f(j1 + j2 - j3) / f(j1 + j2 + j3 + 1)
        pref *= f(j3 + m3) * f(j3 - m3) * f(j1 - m1) * f(j1 + m1) * f(j2 - m2) * f(j2 + m2)
        return math.sqrt(pref) * sum((-1) ** v / (f(v) * f(j1 + j2 - j3 - v) * f(j1 - m1 - v) * f(j2 + m2 - v) * f(j3 - j2 + m1 + v)
                                                  * f(j3 - j1 - m2 + v)) for v in range(lo, hi + 1))

    def basis(l):
        q = np.zeros((2 * l + 1, 2 * l + 1), complex)
        for m in range(-l, 0):
            q[l + m, l - m], q[l + m, l + m] = 2 ** -0.5, -1j * 2 ** -0.5
        q[l, l] = 1
        for m in range(1, l + 1):
            q[l + m, l + m], q[l + m, l - m] = (-1) ** m * 2 ** -0.5, 1j * (-1) ** m * 2 ** -0.5
        return (-1j) ** l * q

    table = np.zeros((6, D, D, SH), np.float32)
    for n, (l1, l2, l3) in enumerate(combos):
        c = np.zeros((2 * l1 + 1, 2 * l2 + 1, 2 * l3 + 1), complex)
        for m1 in range(-l1, l1 + 1):
            for m2 in range(-l2, l2 + 1):
                if abs(m1 + m2) <= l3:
                    c[m1 + l1, m2 + l2, m1 + m2 + l3] = coefficient(l1, m1, l2, m2, l3, m1 + m2)
        c = np.einsum("ij,kl,mn,ikn->jlm", basis(l1), basis(l2), np.conj(basis(l3)).T, c).real
        c /= np.linalg.norm(c)
        for m in range(8):
            for j in range(2 * l2 + 1):
                for o in range(8):
                    for k in range(2 * l3 + 1):
                        table[n, m if l2 == 0 else 8 + 3 * m + j, o if l3 == 0 else 8 + 3 * o + k, l1 * l1:(l1 + 1) ** 2] = c[:, j, k]
    return table


def kernel(**inputs):
    import numpy as np
    import concourse.bacc as bacc
    from concourse.bass_utils import run_bass_kernel_spmd as run

    a = {k: np.asarray(v) for k, v in inputs.items()}
    w = a["L0_gnn_W"]
    w2, w4 = np.zeros((128, 64), np.float32), np.zeros((128, 128), np.float32)
    for k in range(4):
        w4[32 * k:32 * k + 32, 32 * k:32 * k + 32] = w
    w2[0:64] = w4[0:64, 0:64]
    wq = np.zeros((128, QW), np.float32)
    wq[0:32, CUR:CUR + D] = a["L1_gnn_self_loop_weight"]
    wq[0:32, Q1:Q1 + D] = a["L1_gnn_A1_w"].T
    wq[64, Q1:Q1 + D] = a["L1_gnn_A1_b"]
    wq[32:64, Q2:Q2 + D] = a["L1_gnn_A2_w"].T
    wq[64, Q2:Q2 + D] = a["L1_gnn_A2_b"]
    relc, wcat = np.zeros((128, D + BASES), np.float32), np.zeros((128, D * BASES), np.float32)
    relc[0:RELS, 0:D], relc[0:RELS, D:] = a["L1_gnn_rel_emb"], a["L1_gnn_w_comp"]
    wcat[0:D] = a["L1_gnn_weight"].transpose(1, 2, 0).reshape(D, D * BASES)
    channel = np.array([i if i < 8 else (i - 8) // 3 for i in range(D)])
    wt = a["L3_gnn_W"][:, channel][:, :, channel].transpose(1, 0, 2)
    cg = coupling().transpose(1, 0, 2, 3)
    p, c, t = np.meshgrid(np.arange(128), np.arange(PAIRS), np.arange(PT), indexing="ij")
    own = (PAIR * c + PT * p + t).astype(np.float32)
    k, t, lane = (v.reshape(-1) for v in np.meshgrid(np.arange(ROWS), np.arange(TILES), np.arange(32), indexing="ij"))
    c, partition = k // BLOCKS, 32 * (k % BLOCKS) + lane
    own_blocks = (PAIR * (c // 2) + PT * partition + TILES * (c % 2) + t).astype(np.float32).reshape(ROWS, BLOCK)
    ins = {
        "x": a["x"], "src": a["src"], "dst": a["dst"], "attr3": a["edge_attr_3"].reshape(-1), "attr5": a["edge_attr_5"].reshape(-1),
        "etype": a["edge_type_86"], "ew": a["edge_weight"], "ew1": a["edge_weight1"].reshape(-1),
        "bgb_in": np.stack([a["L0_gnn_b"], a["L0_gnn_gamma"], a["L0_gnn_beta"]]), "w_gcn": w, "w2": w2, "w4": w4, "wq": wq,
        "relc": relc, "wcat": wcat, "cg": cg, "wt": wt, "ident": np.eye(128, dtype=np.float32), "own_in": own, "own_blocks": own_blocks,
        "relno_in": -np.arange(128, dtype=np.float32)[:, None],
    }
    nc = bacc.Bacc("TRN2", target_bir_lowering=False, num_devices=1)
    aps = {}
    for name, v in ins.items():
        ins[name] = v = np.ascontiguousarray(v)
        aps[name] = nc.dram_tensor(name, v.shape, mybir.dt.from_np(v.dtype), kind="ExternalInput").ap()
    for name, shape, dt in (("aug", (N, AUG), mybir.dt.float32), ("plane", (PLANES, ROWS * BLOCK), mybir.dt.float32),
                            ("mask", (2, ROWS * BLOCK), mybir.dt.bfloat16),
                            *((f"tab_{k}", (ROWS * BLOCK, D), mybir.dt.float32) for k in ("b", "r", "o1", "o2", "o3"))):
        aps[name] = nc.dram_tensor(name, shape, dt, kind="Internal").ap()
    aps["out"] = nc.dram_tensor("out", (N, D), mybir.dt.float32, kind="ExternalOutput").ap()
    build(nc, **aps)
    return run(nc, [ins], core_ids=[0]).results[0]["out"]
```
